# Optimizing a Trainium2 kernel written in Bass

```python
import numpy as np
import jax
import jax.numpy as jnp

def _softmax(x, axis=-1):
    return jax.nn.softmax(x, axis=axis)

def _gelu(x):
    return jax.nn.gelu(x, approximate=True)

def _silu(x):
    return jax.nn.silu(x)

def _sigmoid(x):
    return jax.nn.sigmoid(x)

def _layernorm(x, axis=-1, eps=1e-05):
    m = jnp.mean(x, axis=axis, keepdims=True)
    v = jnp.var(x, axis=axis, keepdims=True)
    return (x - m) / jnp.sqrt(v + eps)

def _scatter_add(tgt, idx, src, axis=0):
    return tgt.at[idx].add(src)

def _segment_sum(src, seg, n):
    return jax.ops.segment_sum(src, seg, n)
kernel_name = 'mk_flamingo_gated_d2_seqx_r2_7758e7'

def setup_inputs(seed: int=0):
    np.random.seed(seed)
    _w = jnp.asarray

    def _rec_inputs():
        import jax
        import jax.numpy as jnp
        _rk = jax.random.key(seed)
        x = -0.0002928 + 1 * jax.random.normal(jax.random.fold_in(_rk, 1), (2, 2048, 512), jnp.float32)
        _lenS = 2048 - jax.random.randint(jax.random.fold_in(_rk, 7), (2,), 0, max(1, 2048 // 4) + 1, jnp.int32)
        _lenS2 = 154 - jax.random.randint(jax.random.fold_in(_rk, 8), (2,), 0, max(1, 154 // 4) + 1, jnp.int32)
        _ctx_1024P = jax.random.normal(jax.random.fold_in(_rk, 11), (2, 16, 512), jnp.float32)
        _ctx_1024c = jax.random.dirichlet(jax.random.fold_in(_rk, 511), 0.3 * jnp.ones((16,), jnp.float32), (2, 154))
        _ctx_1024t = jnp.einsum('bsk,bkd->bsd', _ctx_1024c, _ctx_1024P)
        _ctx_1024t = _ctx_1024t * jax.lax.rsqrt(jnp.mean(jnp.square(_ctx_1024t)) + 1e-12) * 0.953939
        ctx_1024 = -1.39393e-06 + 0.999914 * (_ctx_1024t + 0.3 * jax.random.normal(jax.random.fold_in(_rk, 611), (2, 154, 512), jnp.float32))
        _validS = jnp.arange(2048)[None, :] < _lenS[:, None]
        _validS2 = jnp.arange(154)[None, :] < _lenS2[:, None]
        _causal = jnp.tril(jnp.ones((2048, 2048), dtype=bool))
        mask_BxS2_ik0 = jnp.where(jnp.broadcast_to(_validS2[:, :], (2, 154)), 0, 1).astype(jnp.int32)
        _g = jax.random.normal(jax.random.fold_in(_rk, 9001), (2, 2), jnp.float32)
        _g = jnp.sign(_g) * jnp.maximum(jnp.abs(_g), 1.0) + (_g == 0) * 1.0
        g_xattn = _g[0]
        g_ffn = _g[1]
        return (x, ctx_1024, mask_BxS2_ik0, g_xattn, g_ffn)
    x, ctx_1024, mask_BxS2_ik0, g_xattn, g_ffn = _rec_inputs()

    def _L0_xattn_setup():
        import jax, jax.numpy as jnp
        import numpy as np
        MAX_CLAMP_VALUE = 50000.0
        NEG_FILL = -9000000000000000.0
        EMBED_DIM = 512
        NUM_HEADS = 16
        HEAD_DIM = EMBED_DIM // NUM_HEADS
        MASTER_DIM = 512
        SLAVE_DIM = 512
        key = jax.random.key(seed)
        ks = jax.random.split(key, 12)
        B, T, S = (2, 1024, 1024)
        master = jax.random.normal(ks[0], (B, T, MASTER_DIM), dtype=jnp.float32)
        slave = jax.random.normal(ks[1], (B, S, SLAVE_DIM), dtype=jnp.float32)
        attention_mask = jax.random.randint(ks[2], (B, S), 0, 2, dtype=jnp.int32)

        def xavier(k, shape):
            fan_out, fan_in = shape
            lim = jnp.sqrt(6.0 / (fan_in + fan_out)).astype(jnp.float32)
            return jax.random.uniform(k, shape, jnp.float32, -lim, lim)
        Wq = xavier(ks[3], (EMBED_DIM, MASTER_DIM))
        bq = jnp.zeros((EMBED_DIM,), jnp.float32)
        Wk = xavier(ks[4], (EMBED_DIM, SLAVE_DIM))
        bk = jnp.zeros((EMBED_DIM,), jnp.float32)
        Wv = xavier(ks[5], (EMBED_DIM, SLAVE_DIM))
        bv = jnp.zeros((EMBED_DIM,), jnp.float32)
        Wo = xavier(ks[6], (MASTER_DIM, EMBED_DIM))
        bo = jnp.zeros((MASTER_DIM,), jnp.float32)
        return {'master': master, 'slave': slave, 'attention_mask': attention_mask, 'Wq': Wq, 'bq': bq, 'Wk': Wk, 'bk': bk, 'Wv': Wv, 'bv': bv, 'Wo': Wo, 'bo': bo}
    _L0_xattn_all = _L0_xattn_setup()
    _L0_xattn_in = {k: v for k, v in _L0_xattn_all.items() if k in ('Wq', 'bq', 'Wk', 'bk', 'Wv', 'bv', 'Wo', 'bo')}
    del _L0_xattn_all

    def _L0_ffn_setup():
        import jax, jax.numpy as jnp
        import numpy as np
        NUM_OPS, B, T, D = (8, 8, 256, 512)
        key = jax.random.key(seed)
        k1, k2, k3, k4 = jax.random.split(key, 4)
        x = jax.random.normal(k1, (B, T, D), dtype=jnp.float32)
        W = jax.random.normal(k2, (NUM_OPS, D, D), dtype=jnp.float32) * 0.02
        b = jnp.zeros((NUM_OPS, D), dtype=jnp.float32)
        logits = 0.001 * jax.random.normal(k3, (NUM_OPS,), dtype=jnp.float32)
        u = jax.random.uniform(k4, (NUM_OPS,), dtype=jnp.float32, minval=1e-06, maxval=1.0 - 1e-06)
        return {'x': x, 'W': W, 'b': b, 'logits': logits, 'u': u}
    _L0_ffn_all = _L0_ffn_setup()
    _L0_ffn_in = {k: v for k, v in _L0_ffn_all.items() if k in ('W', 'b', 'logits', 'u')}
    del _L0_ffn_all

    def _L1_xattn_setup():
        import jax, jax.numpy as jnp
        import numpy as np
        DIM = 512
        NUM_HEADS = 16
        HEAD_DIM = DIM // NUM_HEADS
        key = jax.random.key(seed)
        ks = jax.random.split(key, 11)
        B, N, C = (2, 1024, DIM)
        s = 1.0 / np.sqrt(C)
        inp = {'q': jax.random.normal(ks[0], (B, N, C), jnp.float32), 'k': jax.random.normal(ks[1], (B, N, C), jnp.float32), 'v': jax.random.normal(ks[2], (B, N, C), jnp.float32), 'Wq': jax.random.normal(ks[3], (C, C), jnp.float32) * s, 'bq': jnp.zeros((C,), jnp.float32), 'Wk': jax.random.normal(ks[4], (C, C), jnp.float32) * s, 'bk': jnp.zeros((C,), jnp.float32), 'Wv': jax.random.normal(ks[5], (C, C), jnp.float32) * s, 'bv': jnp.zeros((C,), jnp.float32), 'Wo': jax.random.normal(ks[6], (C, C), jnp.float32) * s, 'bo': jnp.zeros((C,), jnp.float32)}
        return inp
    _L1_xattn_all = _L1_xattn_setup()
    _L1_xattn_in = {k: v for k, v in _L1_xattn_all.items() if k in ('Wq', 'bq', 'Wk', 'bk', 'Wv', 'bv', 'Wo', 'bo')}
    del _L1_xattn_all

    def _L1_ffn_setup():
        import jax, jax.numpy as jnp
        import numpy as np
        EPS = 1e-08

        def _ste(x, q):
            return x + jax.lax.stop_gradient(q - x)

        def quant_act_uint8(x):
            s = jax.lax.stop_gradient(jnp.maximum(jnp.max(x), EPS)) / 255.0
            q = jnp.clip(jnp.round(x / s), 0.0, 255.0) * s
            return (_ste(x, q), s)

        def quant_weight_int8_perchannel(w):
            s = jax.lax.stop_gradient(jnp.maximum(jnp.max(jnp.abs(w), axis=1, keepdims=True), EPS)) / 127.0
            q = jnp.clip(jnp.round(w / s), -128.0, 127.0) * s
            return (_ste(w, q), s[:, 0])

        def quant_bias_int32(b, s_in, s_w):
            s = jax.lax.stop_gradient(s_in * s_w)
            q = jnp.round(b / s) * s
            return _ste(b, q)

        def quant_linear(x, w, b):
            xq, s_in = quant_act_uint8(x)
            wq, s_w = quant_weight_int8_perchannel(w)
            bq = quant_bias_int32(b, s_in, s_w)
            return jnp.einsum('btd,fd->btf', xq, wq) + bq
        key = jax.random.key(seed)
        k1, k2, k3, k4, k5 = jax.random.split(key, 5)
        B, S, D, F = (4, 1024, 512, 2048)
        return {'x': jax.random.normal(k1, (B, S, D), dtype=jnp.float32), 'w1': jax.random.normal(k2, (F, D), dtype=jnp.float32) * (1.0 / np.sqrt(D)), 'b1': jax.random.normal(k3, (F,), dtype=jnp.float32) * 0.01, 'w2': jax.random.normal(k4, (D, F), dtype=jnp.float32) * (1.0 / np.sqrt(F)), 'b2': jax.random.normal(k5, (D,), dtype=jnp.float32) * 0.01}
    _L1_ffn_all = _L1_ffn_setup()
    _L1_ffn_in = {k: v for k, v in _L1_ffn_all.items() if k in ('w1', 'b1', 'w2', 'b2')}
    del _L1_ffn_all
    return {'x': x, 'ctx_1024': ctx_1024, 'mask_BxS2_ik0': mask_BxS2_ik0, 'g_xattn': g_xattn, 'g_ffn': g_ffn, 'L0_xattn_Wq': _L0_xattn_in['Wq'], 'L0_xattn_bq': _L0_xattn_in['bq'], 'L0_xattn_Wk': _L0_xattn_in['Wk'], 'L0_xattn_bk': _L0_xattn_in['bk'], 'L0_xattn_Wv': _L0_xattn_in['Wv'], 'L0_xattn_bv': _L0_xattn_in['bv'], 'L0_xattn_Wo': _L0_xattn_in['Wo'], 'L0_xattn_bo': _L0_xattn_in['bo'], 'L0_ffn_W': _L0_ffn_in['W'], 'L0_ffn_b': _L0_ffn_in['b'], 'L0_ffn_logits': _L0_ffn_in['logits'], 'L0_ffn_u': _L0_ffn_in['u'], 'L1_xattn_Wq': _L1_xattn_in['Wq'], 'L1_xattn_bq': _L1_xattn_in['bq'], 'L1_xattn_Wk': _L1_xattn_in['Wk'], 'L1_xattn_bk': _L1_xattn_in['bk'], 'L1_xattn_Wv': _L1_xattn_in['Wv'], 'L1_xattn_bv': _L1_xattn_in['bv'], 'L1_xattn_Wo': _L1_xattn_in['Wo'], 'L1_xattn_bo': _L1_xattn_in['bo'], 'L1_ffn_w1': _L1_ffn_in['w1'], 'L1_ffn_b1': _L1_ffn_in['b1'], 'L1_ffn_w2': _L1_ffn_in['w2'], 'L1_ffn_b2': _L1_ffn_in['b2']}

def reference(x, ctx_1024, mask_BxS2_ik0, g_xattn, g_ffn, L0_xattn_Wq, L0_xattn_bq, L0_xattn_Wk, L0_xattn_bk, L0_xattn_Wv, L0_xattn_bv, L0_xattn_Wo, L0_xattn_bo, L0_ffn_W, L0_ffn_b, L0_ffn_logits, L0_ffn_u, L1_xattn_Wq, L1_xattn_bq, L1_xattn_Wk, L1_xattn_bk, L1_xattn_Wv, L1_xattn_bv, L1_xattn_Wo, L1_xattn_bo, L1_ffn_w1, L1_ffn_b1, L1_ffn_w2, L1_ffn_b2):
    import jax
    import jax.numpy as jnp

    def _L0_xattn_ref(master, slave, attention_mask, Wq, bq, Wk, bk, Wv, bv, Wo, bo):
        import jax, jax.numpy as jnp
        import numpy as np
        MAX_CLAMP_VALUE = 50000.0
        NEG_FILL = -9000000000000000.0
        EMBED_DIM = 512
        NUM_HEADS = 16
        HEAD_DIM = EMBED_DIM // NUM_HEADS
        MASTER_DIM = 512
        SLAVE_DIM = 512
        B, T, _ = master.shape
        S = slave.shape[1]
        scale = HEAD_DIM ** (-0.5)

        def split_heads(x):
            return x.reshape(x.shape[0], x.shape[1], NUM_HEADS, HEAD_DIM).transpose(0, 2, 1, 3)
        q = split_heads((master @ Wq.T + bq) * scale)
        k = split_heads(slave @ Wk.T + bk)
        v = split_heads(slave @ Wv.T + bv)
        attn = jnp.einsum('bhtd,bhsd->bhts', q, k)
        attn = jnp.clip(attn, -MAX_CLAMP_VALUE, MAX_CLAMP_VALUE)
        m = attention_mask.astype(jnp.float32)[:, None, None, :]
        m = jnp.where(m == 0, jnp.float32(NEG_FILL), m)
        attn = attn + m
        attn = jax.nn.softmax(attn, axis=-1)
        out = jnp.einsum('bhts,bhsd->bhtd', attn, v)
        out = out.transpose(0, 2, 1, 3).reshape(B, T, EMBED_DIM)
        return out @ Wo.T + bo

    def _L0_ffn_ref(x, W, b, logits, u):
        import jax, jax.numpy as jnp
        import numpy as np
        NUM_OPS, B, T, D = (8, 8, 256, 512)
        gumbel = -jnp.log(-jnp.log(u))
        idx = jnp.argmax(jax.nn.log_softmax(logits) + gumbel)
        out = jnp.einsum('btd,de->bte', x, W[idx]) + b[idx]
        return out

    def _L1_xattn_ref(q, k, v, Wq, bq, Wk, bk, Wv, bv, Wo, bo):
        import jax, jax.numpy as jnp
        import numpy as np
        DIM = 512
        NUM_HEADS = 16
        HEAD_DIM = DIM // NUM_HEADS
        B, Nq, C = q.shape
        Nkv = k.shape[1]
        H, D = (NUM_HEADS, HEAD_DIM)
        qh = (q @ Wq.T + bq).reshape(B, Nq, H, D).transpose(0, 2, 1, 3)
        kh = (k @ Wk.T + bk).reshape(B, Nkv, H, D).transpose(0, 2, 1, 3)
        vh = (v @ Wv.T + bv).reshape(B, Nkv, H, D).transpose(0, 2, 1, 3)
        scale = D ** (-0.5)
        attn = jax.nn.softmax(jnp.einsum('bhqd,bhkd->bhqk', qh, kh) * scale, axis=-1)
        out = jnp.einsum('bhqk,bhkd->bhqd', attn, vh)
        out = out.transpose(0, 2, 1, 3).reshape(B, Nq, C)
        return out @ Wo.T + bo

    def _L1_ffn_ref(x, w1, b1, w2, b2):
        import jax, jax.numpy as jnp
        import numpy as np
        EPS = 1e-08

        def _ste(x, q):
            return x + jax.lax.stop_gradient(q - x)

        def quant_act_uint8(x):
            s = jax.lax.stop_gradient(jnp.maximum(jnp.max(x), EPS)) / 255.0
            q = jnp.clip(jnp.round(x / s), 0.0, 255.0) * s
            return (_ste(x, q), s)

        def quant_weight_int8_perchannel(w):
            s = jax.lax.stop_gradient(jnp.maximum(jnp.max(jnp.abs(w), axis=1, keepdims=True), EPS)) / 127.0
            q = jnp.clip(jnp.round(w / s), -128.0, 127.0) * s
            return (_ste(w, q), s[:, 0])

        def quant_bias_int32(b, s_in, s_w):
            s = jax.lax.stop_gradient(s_in * s_w)
            q = jnp.round(b / s) * s
            return _ste(b, q)

        def quant_linear(x, w, b):
            xq, s_in = quant_act_uint8(x)
            wq, s_w = quant_weight_int8_perchannel(w)
            bq = quant_bias_int32(b, s_in, s_w)
            return jnp.einsum('btd,fd->btf', xq, wq) + bq
        h = jax.nn.relu(quant_linear(x, w1, b1))
        return quant_linear(h, w2, b2)
    x = x + jnp.tanh(g_xattn[0]) * _L0_xattn_ref(_layernorm(x, axis=-1), ctx_1024, mask_BxS2_ik0, L0_xattn_Wq, L0_xattn_bq, L0_xattn_Wk, L0_xattn_bk, L0_xattn_Wv, L0_xattn_bv, L0_xattn_Wo, L0_xattn_bo)
    x = x + jnp.tanh(g_ffn[0]) * _L0_ffn_ref(_layernorm(x, axis=-1), L0_ffn_W, L0_ffn_b, L0_ffn_logits, L0_ffn_u)
    x = x + jnp.tanh(g_xattn[1]) * _L1_xattn_ref(_layernorm(x, axis=-1), ctx_1024, ctx_1024, L1_xattn_Wq, L1_xattn_bq, L1_xattn_Wk, L1_xattn_bk, L1_xattn_Wv, L1_xattn_bv, L1_xattn_Wo, L1_xattn_bo)
    x = x + jnp.tanh(g_ffn[1]) * _L1_ffn_ref(_layernorm(x, axis=-1), L1_ffn_w1, L1_ffn_b1, L1_ffn_w2, L1_ffn_b2)
    return x

_drawn_inputs = setup_inputs


def setup_inputs(seed=0):
    import zlib

    import numpy as np

    out = dict(_drawn_inputs(seed))
    spreads = {'g_ffn': (-1.0, 0.546),
     'L0_xattn_bq': (0.0, 0.336),
     'L0_xattn_bk': (0.0, 0.8),
     'L0_xattn_bv': (0.0, 0.1),
     'L0_xattn_bo': (0.0, 0.1),
     'L0_ffn_b': (0.0, 0.1),
     'L1_xattn_bq': (0.0, 0.37),
     'L1_xattn_bk': (0.0, 0.8),
     'L1_xattn_bv': (0.0, 0.1),
     'L1_xattn_bo': (0.0, 0.1)}
    factors = {'L1_ffn_b1': 6.822, 'L1_ffn_b2': 8.0}
    for name, (base, spread) in spreads.items():
        noise = np.random.default_rng([zlib.crc32(name.encode()), seed]).standard_normal(out[name].shape)
        drawn = base * np.exp(spread * noise) if base else spread * noise
        out[name] = jnp.asarray(drawn.astype(out[name].dtype))
    for name, factor in factors.items():
        out[name] = (out[name] * factor).astype(out[name].dtype)
    return out
```

```python
from contextlib import ExitStack

import numpy as np
import concourse.bass as bass
from concourse import mybir

FP32 = mybir.dt.float32
FP32R = mybir.dt.float32r
BF16 = mybir.dt.bfloat16
I32 = mybir.dt.int32
U32 = mybir.dt.uint32
ALU = mybir.AluOpType
ACT = mybir.ActivationFunctionType
AX = mybir.AxisListType

P = 128
B, S, D = 2, 2048, 512
KEYS = 154
HEADS = 16
HD = D // HEADS
F = 2048
OPS = 8
LAYERS = 2
CH = D // P
HPG = P // HD
TOK = 512
SUB = TOK // P
TILES = B * S // P
STEPS_B = S // TOK
STEPS = B * STEPS_B
UNITS = CH * SUB
REM = KEYS - P
HALF = 2 * KEYS
FC = F // P
SCALE = float(HD) ** -0.5
CLAMP = 50000.0
NEG_FILL = -9.0e15
LN_EPS = 1e-5
Q_EPS = 1e-8
MAGIC = 12582912.0

KV_USES = CH + 2
XT, QP, PV, WO = 0, CH, 2 * CH, 3 * CH
ATT_USES = 4 * CH
FFN_USES = CH + SUB
CREDIT = 1
LAG_T = 2
LAG_O = 3


def flat(ap):
    return ap.rearrange("p a n -> p (a n)")


def attention_layers(nc, x, ctxT, mask, gates, cols, rows, weights, W0, logits, u, X, ident):
    ctx = ExitStack()
    with ctx:
        def sb(name, shape, dt):
            return ctx.enter_context(nc.sbuf_tensor(name, shape, dt))

        def sem(name):
            return ctx.enter_context(nc.semaphore(name))

        wa_hi = sb("wa_hi", [P, CH, D], FP32R)
        wa_lo = sb("wa_lo", [P, CH, D], FP32R)
        wo_hi = sb("wo_hi", [P, CH, D], FP32R)
        wo_lo = sb("wo_lo", [P, CH, D], FP32R)
        k_hi = sb("k_hi", [P, CH, HPG * KEYS], FP32R)
        k_lo = sb("k_lo", [P, CH, HPG * KEYS], FP32R)
        v_main = sb("v_main", [P, D], FP32)
        v_rem = sb("v_rem", [P, CH, P], FP32)
        xt_hi = sb("xt_hi", [P, CH, TOK], FP32R)
        xt_lo = sb("xt_lo", [P, CH, TOK], FP32R)
        q_hi = sb("q_hi", [P, CH, TOK], FP32R)
        q_lo = sb("q_lo", [P, CH, TOK], FP32R)
        xn = sb("xn", [P, SUB, D], FP32)
        sc = sb("sc", [P, 2, HPG, KEYS], FP32)
        pr = sb("pr", [P, 2, HPG, KEYS], FP32)
        pn = sb("pn", [P, 2, HPG * P + P], FP32)
        pT = sb("pT", [P, 2, HPG + 1, TOK], FP32)
        ctx_t = sb("ctx_t", [P, CH, B * KEYS], FP32)
        bias_cols = sb("bias_cols", [P, 2 * LAYERS, CH], FP32)
        bk_scaled = sb("bk_scaled", [P, LAYERS, CH], FP32)
        bv_row = sb("bv_row", [P, D], FP32)
        bo_row = sb("bo_row", [P, D], FP32)
        mask_add = sb("mask_add", [P, B, KEYS], FP32)
        gate_raw = sb("gate_raw", [P, 4], FP32)
        gate = sb("gate", [P, 4], FP32)
        stats = sb("stats", [P, SUB, 6], FP32)
        meanvar = sb("meanvar", [P, SUB, 2], FP32)
        vareps = sb("vareps", [P, SUB], FP32)
        rstd = sb("rstd", [P, SUB], FP32)
        neg_half = sb("neg_half", [P, SUB], FP32)
        smax = sb("smax", [P, 2, HPG], FP32)
        nmax = sb("nmax", [P, 2, HPG], FP32)
        rsum = sb("rsum", [P, 2, HPG], FP32)
        wait_pad = sb("wait_pad", [P, 1], FP32)
        rec = sb("rec", [P, 2, HPG], FP32)
        gum = sb("gum", [1, 8, OPS], FP32)
        gmax = sb("gmax", [1, OPS], FP32)
        gidx = sb("gidx", [1, OPS], U32)
        ps = ctx.enter_context(nc.psum_tensor("ps", [P, 8, 512], FP32))
        consts = sem("consts")
        zeroed = sem("zeroed")
        small_in = sem("small_in")
        x_in0 = sem("x_in0")
        x_in1 = sem("x_in1")
        raw_in = sem("raw_in")
        brow_in = sem("brow_in")
        prep = sem("prep")
        act_prep = sem("act_prep")
        bo_scaled = sem("bo_scaled")
        pick = sem("pick")
        split_hi = sem("split_hi")
        split_lo = sem("split_lo")
        stats_done = sem("stats_done")
        aggr_done = sem("aggr_done")
        eps_done = sem("eps_done")
        rstd_done = sem("rstd_done")
        xn_ready = sem("xn_ready")
        pre_added = sem("pre_added")
        a_full = sem("a_full")
        a_free = sem("a_free")
        hi_done = sem("hi_done")
        k_tmp_done = sem("k_tmp_done")
        s_full = sem("s_full")
        s_free = sem("s_free")
        masked = sem("masked")
        max_done = sem("max_done")
        exp_done = sem("exp_done")
        rec_done = sem("rec_done")
        pn_done = sem("pn_done")
        t_full = sem("t_full")
        ptm_out = sem("ptm_out")
        ptr_out = sem("ptr_out")
        block = ctx.enter_context(nc.Block())
        mask_i = xn[:, 0, 0:B * KEYS].bitcast(I32).rearrange("p (b k) -> p b k", b=B)
        mask_f = xn[:, 1, 0:B * KEYS].rearrange("p (b k) -> p b k", b=B)
        k_tmp = xn[:, 2:4, :].rearrange("p s d -> p (s d)")[:, 0:CH * KEYS].rearrange("p (c k) -> p c k", c=CH)
        raw = pT[:, :, :, :].rearrange("p b h n -> p (b h n)")
        raw_a = raw[:, 0:CH * D].rearrange("p (c n) -> p c n", c=CH)
        raw_b = raw[:, CH * D:2 * CH * D].rearrange("p (c n) -> p c n", c=CH)

        def work(a):
            return ps[:, a % 2, :]

        def score_bank(v):
            return ps[:, 2 + v % 4, 0:HALF]

        PTM, PTR = ps[:, 6, :], ps[:, 7, :]

        def tile_of(n):
            return flat(X[:, bass.ds(n, 1), :])

        kv_at, att_at, ffn_at = {}, {}, None
        uses = his = att = lns = 0
        for l in range(LAYERS):
            for b in range(B):
                kv_at[l, b] = (uses, his)
                uses, his = uses + KV_USES, his + CH
                att_at[l, b] = (uses, his, att, lns)
                uses += ATT_USES * STEPS_B
                his += 3 * CH * STEPS_B
                att, lns = att + STEPS_B, lns + STEPS_B
            if l == 0:
                ffn_at = (uses, his, lns)
                uses, his, lns = uses + FFN_USES * STEPS, his + CH * STEPS, lns + STEPS

        @block.sync
        def _(sp):
            for l in range(LAYERS):
                for k in range(2):
                    sp.dma_start(bias_cols[:, 2 * l + k, :], cols[l][k]).then_inc(small_in, 16)
            sp.dma_start(flat(mask_i[:, :, :]), mask.partition_broadcast(P)).then_inc(small_in, 16)
            sp.dma_start(gate_raw[:, :], gates.partition_broadcast(P)).then_inc(small_in, 16)
            sp.dma_start(gum[0:1, 0, :], u).then_inc(small_in, 16)
            sp.dma_start(gum[0:1, 1, :], logits).then_inc(small_in, 16)
            sp.dma_start(ctx_t[:, :, :], ctxT.rearrange("(c p) n -> p c n", p=P)).then_inc(small_in, 16)
            raws = 0

            def load_raw(dst, src):
                sp.dma_start(dst, src.rearrange("(c p) n -> p c n", p=P)).then_inc(raw_in, 16)

            sp.dma_start(bv_row[:, :], rows[0][0].partition_broadcast(P)).then_inc(brow_in, 16)
            sp.dma_start(bo_row[:, :], rows[0][1].partition_broadcast(P)).then_inc(brow_in, 16)
            load_raw(raw_a, weights[0][0])
            load_raw(raw_b, weights[0][3])
            xv = x.rearrange("(t p) n -> p t n", p=P)
            half = TILES // 2
            sp.dma_start(X[:, 0:half, :], xv[:, 0:half, :]).then_inc(x_in0, 16)
            sp.dma_start(X[:, half:TILES, :], xv[:, half:TILES, :]).then_inc(x_in1, 16)
            for l in range(LAYERS):
                if l:
                    sp.wait_ge(a_free, kv_at[l, 0][0])
                    sp.dma_start(bv_row[:, :], rows[l][0].partition_broadcast(P)).then_inc(brow_in, 16)
                    sp.dma_start(bo_row[:, :], rows[l][1].partition_broadcast(P)).then_inc(brow_in, 16)
                    load_raw(raw_a, weights[l][0])
                    load_raw(raw_b, weights[l][3])
                for b in range(B):
                    if b == 0:
                        sp.wait_ge(split_hi, 3 * l + 2)
                        sp.wait_ge(split_lo, 3 * l + 2)
                    else:
                        sp.wait_ge(a_free, kv_at[l, b][0])
                    load_raw(raw_a, weights[l][1])
                    load_raw(raw_b, weights[l][2])
                if l == 0:
                    sp.wait_ge(pick, 10)
                    sp.wait_ge(a_free, ffn_at[0])
                    idx = sp.value_load(gidx[0:1, 0:1], min_val=0, max_val=OPS - 1)
                    sp.dma_start(bo_row[:, :], rows[LAYERS][bass.ds(idx, 1), :].partition_broadcast(P)).then_inc(brow_in, 16)
                    sp.dma_start(raw_a, W0[bass.ds(idx, 1), :, :].rearrange("a (c p) n -> p (a c) n", p=P)).then_inc(raw_in, 16)

        @block.gpsimd
        def _(pool):
            pool.sem_inc(pn_done, CREDIT)
            pool.memset(ident[:, :], 0.0).then_inc(consts, 1)
            pool.memset(neg_half[:, :], -0.5).then_inc(consts, 1)
            pool.wait_ge(consts, 1)
            pool.affine_select(out=ident[:, :], in_=ident[:, :], compare_op=ALU.not_equal, fill=1.0, base=0,
                               pattern=[[-1, P]], channel_multiplier=1).then_inc(consts, 1)
            pool.memset(pn[:, :, :], 0.0).then_inc(consts, 1)
            pool.wait_ge(consts, 4)

            def rstd_of(ln):
                pool.wait_ge(aggr_done, (ln + 1) * SUB)
                pool.tensor_tensor(vareps[:, :], vareps[:, :], meanvar[:, :, 1], ALU.add).then_inc(eps_done, 1)
                pool.wait_ge(eps_done, ln + 1)
                pool.tensor_tensor(rstd[:, :], vareps[:, :], neg_half[:, :], ALU.pow).then_inc(rstd_done, 1)

            def pre_add(ln, n, first):
                if first:
                    pool.wait_ge(xn_ready, (ln + 1) * SUB)
                pool.tensor_tensor(tile_of(n), tile_of(n), bo_row[:, :], ALU.add).then_inc(pre_added, 1)

            for l in range(LAYERS):
                for b in range(B):
                    _, _, att0, ln0 = att_at[l, b]
                    pool.wait_ge(bo_scaled, 2 * l + 1)
                    with pool.Fori(0, STEPS_B) as it:
                        rstd_of(it + ln0)
                        for k in range(UNITS):
                            unit = (it + att0) * UNITS + k
                            pool.wait_ge(rec_done, unit + 1)
                            pool.wait_ge(t_full, (it + att0) * UNITS + (max(k - 1, 0) + CREDIT))
                            g = k % 2
                            r = rec[:, g, :, None]
                            pool.tensor_tensor(pn[:, g, 0:HPG * P].rearrange("p (h k) -> p h k", h=HPG),
                                               pr[:, g, :, 0:P], r.broadcast_to([P, HPG, P]), ALU.mult)
                            pool.tensor_tensor(pn[:, g, HPG * P:].rearrange("p (h k) -> p h k", h=HPG)[:, :, 0:REM],
                                               pr[:, g, :, P:KEYS], r.broadcast_to([P, HPG, REM]),
                                               ALU.mult).then_inc(pn_done, 1)
                            if k % SUB == SUB - 1:
                                pre_add(it + ln0, it * SUB + (b * STEPS_B * SUB + k // SUB), k == SUB - 1)
                if l == 0:
                    _, _, ln0 = ffn_at
                    pool.wait_ge(bo_scaled, 2)
                    with pool.Fori(0, STEPS) as it:
                        rstd_of(it + ln0)
                        for s in range(SUB):
                            pre_add(it + ln0, it * SUB + s, s == 0)

        @block.scalar
        def _(act):
            act.sem_inc(ptm_out, CREDIT)
            act.sem_inc(ptr_out, CREDIT)
            act.wait_ge(small_in, 144)
            act.activation(gate[:, :], gate_raw[:, :], ACT.Tanh).then_inc(act_prep, 1)
            for l in range(LAYERS):
                act.activation(bk_scaled[:, l, :], bias_cols[:, 2 * l + 1, :], ACT.Copy, scale=SCALE).then_inc(act_prep, 1)
            act.activation(gum[0:1, 2, :], gum[0:1, 0, :], ACT.Ln).then_inc(pick, 1)
            act.wait_ge(pick, 1)
            act.activation(gum[0:1, 3, :], gum[0:1, 2, :], ACT.Ln, scale=-1.0).then_inc(pick, 1)
            act.wait_ge(pick, 4)
            act.activation(gum[0:1, 5, :], gum[0:1, 4, :], ACT.Exp, accum_out=gum[0:1, 6, 0:1]).then_inc(pick, 1)
            act.wait_ge(pick, 5)
            act.activation(gum[0:1, 6, 1:2], gum[0:1, 6, 0:1], ACT.Ln).then_inc(pick, 1)

            def upper_of_weights(n, done, pairs):
                act.wait_ge(raw_in, n)
                for dst, src in pairs:
                    done += 1
                    act.activation(dst, src, ACT.Copy).then_inc(split_hi, 1)

            def upper(use, dst, bias=None):
                act.wait_ge(a_full, use + 1)
                if bias is None:
                    act.activation(dst, work_now, ACT.Copy).then_inc(hi_done, 1)
                else:
                    act.activation(dst, work_now, ACT.Identity, bias=bias).then_inc(hi_done, 1)

            def exps(l, b, att0, it, k):
                unit = (it + att0) * UNITS + k
                act.wait_ge(pn_done, (it + att0) * UNITS + (max(k - 1, 0) + CREDIT))
                for h in range(HPG):
                    if l == 0:
                        if h == 0:
                            act.wait_ge(max_done, unit + 1)
                        src = sc[:, k % 2, h, :]
                    else:
                        if h % 2 == 0:
                            act.wait_ge(max_done, STEPS * UNITS + (unit - STEPS * UNITS) * 2 + h // 2 + 1)
                        src = score_bank(2 * k + h // 2)[:, (h % 2) * KEYS:(h % 2 + 1) * KEYS]
                    i = act.activation(pr[:, k % 2, h, :], src, ACT.Exp, bias=nmax[:, k % 2, h:h + 1],
                                       accum_out=rsum[:, k % 2, h:h + 1])
                    if l == 1 and h % 2:
                        i.then_inc(s_free, 1)
                    if l == 0 and h == HPG - 1:
                        i.then_inc(exp_done, 1)

            def copy_pT(att0, it, k):
                unit = (it + att0) * UNITS + k
                g, s = k // SUB, k % SUB
                act.wait_ge(t_full, unit + (1 + CREDIT))
                act.activation(pT[:, g % 2, 0:HPG, s * P:(s + 1) * P], PTM.rearrange("p (h q) -> p h q", h=HPG),
                               ACT.Copy).then_inc(ptm_out, 1)
                if s == SUB - 1:
                    act.activation(pT[:, g % 2, HPG, :], PTR, ACT.Copy).then_inc(ptr_out, 1)

            raws = 32
            upper_of_weights(raws, 0, ((wa_hi[:, :, :], raw_a), (wo_hi[:, :, :], raw_b)))
            for l in range(LAYERS):
                if l:
                    raws += 32
                    upper_of_weights(raws, 0, ((wa_hi[:, :, :], raw_a), (wo_hi[:, :, :], raw_b)))
                for b in range(B):
                    raws += 32
                    a0, h0 = kv_at[l, b]
                    if (l, b) == (0, 0):
                        act.wait_ge(zeroed, 2)
                        act.wait_ge(act_prep, 3)
                    for g in range(CH):
                        act.wait_ge(a_full, a0 + g + 1)
                        act.activation(k_tmp[:, g, :], work(a0 + g)[:, 0:KEYS], ACT.Identity, scale=SCALE,
                                       bias=bk_scaled[:, l, g:g + 1]).then_inc(k_tmp_done, 1)
                        act.wait_ge(k_tmp_done, kv_count(l, b) * CH + g + 1)
                        for h in range(HPG):
                            q = slice(h * HD, (h + 1) * HD)
                            i = act.activation(k_hi[q, g, h * KEYS:(h + 1) * KEYS], k_tmp[q, g, :], ACT.Copy)
                        i.then_inc(hi_done, 1)
                    a0, h0, att0, ln0 = att_at[l, b]
                    with act.Fori(0, STEPS_B) as it:
                        use = it * ATT_USES + a0
                        for c in range(CH):
                            work_now = work(c)
                            upper(use + (XT + c), xt_hi[:, c, :])
                        for m in range(CH):
                            work_now = work(m)
                            upper(use + (QP + m), q_hi[:, m, :], bias_cols[:, 2 * l, m:m + 1])
                        for k in range(UNITS + LAG_T + 2):
                            if k < UNITS:
                                exps(l, b, att0, it, k)
                            if l == 0 and 0 <= k - LAG_T < UNITS:
                                copy_pT(att0, it, k - LAG_T)
                            if k >= SUB + LAG_O and (k - LAG_O) % SUB == 0:
                                g = (k - LAG_O) // SUB - 1
                                work_now = work(g)
                                upper(use + (PV + g), xt_hi[:, g, :])
                if l == 0:
                    raws += 16
                    upper_of_weights(raws, 0, ((wa_hi[:, :, :], raw_a),))
                    a0, h0, ln0 = ffn_at
                    with act.Fori(0, STEPS) as it:
                        for c in range(CH):
                            work_now = work(c)
                            upper(it * FFN_USES + (a0 + c), xt_hi[:, c, :])

        @block.vector
        def _(dve):
            dve.sem_inc(s_free, CREDIT)
            dve.memset(k_hi[:, :, :].bitcast(FP32), 0.0).then_inc(zeroed, 1)
            dve.memset(k_lo[:, :, :].bitcast(FP32), 0.0).then_inc(zeroed, 1)
            dve.memset(v_rem[:, :, :], 0.0).then_inc(prep, 1)
            dve.wait_ge(small_in, 144)
            dve.tensor_reduce(gum[0:1, 7, 0:1], gum[0:1, 1, :], axis=AX.X, op=ALU.max).then_inc(prep, 1)
            dve.wait_ge(prep, 2)
            dve.wait_ge(pick, 2)
            dve.tensor_scalar(gum[0:1, 4, :], gum[0:1, 1, :], gum[0:1, 7, 0:1], None, ALU.subtract).then_inc(pick, 2)
            dve.tensor_copy(mask_f[:, :, :], mask_i[:, :, :]).then_inc(prep, 1)
            dve.wait_ge(prep, 3)
            dve.tensor_scalar(mask_add[:, :, :], mask_f[:, :, :], 0.0, NEG_FILL, ALU.is_equal, ALU.mult).then_inc(prep, 1)
            dve.wait_ge(prep, 4)
            dve.tensor_tensor(mask_add[:, :, :], mask_add[:, :, :], mask_f[:, :, :], ALU.add).then_inc(prep, 1)
            dve.wait_ge(pick, 6)
            dve.tensor_scalar(gum[0:1, 7, :], gum[0:1, 4, :], gum[0:1, 6, 1:2], None, ALU.subtract).then_inc(pick, 1)
            dve.wait_ge(pick, 7)
            dve.tensor_tensor(gum[0:1, 7, :], gum[0:1, 7, :], gum[0:1, 3, :], ALU.subtract).then_inc(pick, 1)
            dve.wait_ge(pick, 8)
            dve.max(gmax[0:1, :], gum[0:1, 7, :]).then_inc(pick, 1)
            dve.wait_ge(pick, 9)
            dve.max_index(gidx[0:1, :], gmax[0:1, :], gum[0:1, 7, :]).then_inc(pick, 1)
            dve.wait_ge(prep, 5)
            dve.wait_ge(act_prep, 3)
            dve.wait_ge(brow_in, 32)
            dve.tensor_scalar(bo_row[:, :], bo_row[:, :], gate[:, 0:1], None, ALU.mult).then_inc(bo_scaled, 1)

            def lower_of_weights(n, done, pairs):
                dve.wait_ge(raw_in, n)
                for j, (dst, src, hi) in enumerate(pairs):
                    dve.wait_ge(split_hi, done + j + 1)
                    dve.tensor_tensor(dst, src, hi.bitcast(FP32), ALU.subtract).then_inc(split_lo, 1)

            def layer_norm(ln, n0):
                for s in range(SUB):
                    dve.bn_stats(stats[:, s, :], tile_of(n0 + s)).then_inc(stats_done, 1)
                dve.wait_ge(stats_done, (ln + 1) * SUB)
                dve.memset(vareps[:, :], LN_EPS)
                for s in range(SUB):
                    dve.bn_aggr(meanvar[:, s, :], stats[:, s, :]).then_inc(aggr_done, 1)
                dve.wait_ge(rstd_done, ln + 1)
                for s in range(SUB):
                    dve.tensor_scalar(xn[:, s, :], tile_of(n0 + s), meanvar[:, s, 0:1], rstd[:, s:s + 1],
                                      ALU.subtract, ALU.mult).then_inc(xn_ready, 1)

            def lower(hi_count, bank, dst, hi, bias=None):
                dve.wait_ge(hi_done, hi_count)
                if bias is None:
                    dve.tensor_tensor(dst, bank, hi.bitcast(FP32), ALU.subtract).then_inc(a_free, 1)
                else:
                    dve.scalar_tensor_tensor(out=dst, in0=bank, scalar=bias, in1=hi.bitcast(FP32),
                                             op0=ALU.add, op1=ALU.subtract).then_inc(a_free, 1)

            def residual(use, bank, n, gate_col, pre):
                dve.wait_ge(a_full, use)
                dve.wait_ge(pre_added, pre)
                dve.scalar_tensor_tensor(out=tile_of(n), in0=bank, scalar=gate[:, gate_col:gate_col + 1],
                                         in1=tile_of(n), op0=ALU.mult, op1=ALU.add).then_inc(a_free, 1)

            def maxima(l, b, att0, it, k):
                unit = (it + att0) * UNITS + k
                for half in range(2):
                    v = 2 * k + half
                    dve.wait_ge(s_full, (it + att0) * (2 * UNITS) + (v + 1))
                    if l == 0:
                        dve.tensor_scalar(sc[:, k % 2, 2 * half:2 * half + 2, :],
                                          score_bank(v).rearrange("p (h k) -> p h k", h=2),
                                          CLAMP, -CLAMP, ALU.min, ALU.max).then_inc(s_free, 1)
                    else:
                        dve.tensor_reduce(nmax[:, k % 2, 2 * half:2 * half + 2],
                                          score_bank(v).rearrange("p (h k) -> p h k", h=2), axis=AX.X,
                                          op=ALU.max, negate=True).then_inc(max_done, 1)
                if l == 0:
                    dve.wait_ge(s_free, (it + att0) * (2 * UNITS) + (2 * k + 2 + CREDIT))
                    dve.memset(wait_pad[:, :], 0.0)
                    for h in range(HPG):
                        i = dve.tensor_tensor_reduce(out=sc[:, k % 2, h, :], in0=sc[:, k % 2, h, :],
                                                     in1=mask_add[:, b, :], scale=1.0, scalar=-3.0e38,
                                                     op0=ALU.add, op1=ALU.max, accum_out=smax[:, k % 2, h:h + 1])
                    i.then_inc(masked, 1)
                    dve.wait_ge(masked, unit + 1)
                    dve.tensor_scalar(nmax[:, k % 2, :], smax[:, k % 2, :], -1.0, None, ALU.mult).then_inc(max_done, 1)

            def reciprocals(l, att0, it, k):
                unit = (it + att0) * UNITS + k
                if l == 0:
                    dve.wait_ge(exp_done, unit + 1)
                else:
                    dve.wait_ge(s_free, unit * 2 + (2 + CREDIT))
                dve.reciprocal(rec[:, k % 2, :], rsum[:, k % 2, :]).then_inc(rec_done, 1)

            def copy_pT(att0, it, k):
                unit = (it + att0) * UNITS + k
                g, s = k // SUB, k % SUB
                dve.wait_ge(t_full, unit + (1 + CREDIT))
                dve.tensor_copy(pT[:, g % 2, 0:HPG, s * P:(s + 1) * P],
                                PTM.rearrange("p (h q) -> p h q", h=HPG)).then_inc(ptm_out, 1)
                if s == SUB - 1:
                    dve.tensor_copy(pT[:, g % 2, HPG, :], PTR).then_inc(ptr_out, 1)

            raws, brows, splits = 32, 32, 2
            lower_of_weights(raws, 0, ((wa_lo[:, :, :], raw_a, wa_hi[:, :, :]), (wo_lo[:, :, :], raw_b, wo_hi[:, :, :])))
            for l in range(LAYERS):
                if l:
                    brows += 32
                    dve.wait_ge(brow_in, brows)
                    dve.tensor_scalar(bo_row[:, :], bo_row[:, :], gate[:, 2 * l:2 * l + 1], None, ALU.mult).then_inc(bo_scaled, 1)
                    raws += 32
                    lower_of_weights(raws, splits, ((wa_lo[:, :, :], raw_a, wa_hi[:, :, :]), (wo_lo[:, :, :], raw_b, wo_hi[:, :, :])))
                    splits += 2
                for b in range(B):
                    a0, h0 = kv_at[l, b]
                    raws += 32
                    for g in range(CH):
                        dve.wait_ge(hi_done, h0 + g + 1)
                        for h in range(HPG):
                            q = slice(h * HD, (h + 1) * HD)
                            blk = k_lo[q, g, h * KEYS:(h + 1) * KEYS]
                            i = dve.tensor_tensor(blk, k_tmp[q, g, :], k_hi[q, g, h * KEYS:(h + 1) * KEYS].bitcast(FP32),
                                                  ALU.subtract)
                        i.then_inc(a_free, 1)
                    dve.wait_ge(a_full, a0 + CH + 1)
                    dve.tensor_tensor(v_main[:, :], work(a0 + CH), bv_row[:, :], ALU.add).then_inc(a_free, 1)
                    dve.wait_ge(a_full, a0 + CH + 2)
                    for h in range(HPG):
                        q = slice(h * HD, h * HD + REM)
                        i = dve.tensor_tensor(v_rem[q, :, h * HD:(h + 1) * HD],
                                              work(a0 + CH + 1)[q, 0:P].rearrange("p (g d) -> p g d", g=CH),
                                              bv_row[q, :].rearrange("p (g h d) -> p g h d", g=CH, h=HPG)[:, :, h, :],
                                              ALU.add)
                    i.then_inc(a_free, 1)
                    a0, h0, att0, ln0 = att_at[l, b]
                    if l == 0:
                        dve.wait_ge(x_in0 if b == 0 else x_in1, 16)
                    dve.wait_ge(a_free, a0)
                    with dve.Fori(0, STEPS_B) as it:
                        use = it * ATT_USES + a0
                        his = it * (3 * CH) + h0
                        n0 = it * SUB + b * STEPS_B * SUB
                        layer_norm(it + ln0, n0)
                        for c in range(CH):
                            lower(his + (c + 1), work(c), xt_lo[:, c, :], xt_hi[:, c, :])
                        for m in range(CH):
                            lower(his + (CH + m + 1), work(m), q_lo[:, m, :], q_hi[:, m, :],
                                  bias_cols[:, 2 * l, m:m + 1])
                        for k in range(UNITS + LAG_T + 2):
                            if k < UNITS:
                                maxima(l, b, att0, it, k)
                            if 0 <= k - 1 < UNITS:
                                reciprocals(l, att0, it, k - 1)
                            if l == 1 and 0 <= k - LAG_T < UNITS:
                                copy_pT(att0, it, k - LAG_T)
                            if k >= SUB + LAG_O and (k - LAG_O) % SUB == 0:
                                g = (k - LAG_O) // SUB - 1
                                lower(his + (2 * CH + g + 1), work(g), xt_lo[:, g, :], xt_hi[:, g, :])
                        for s in range(SUB):
                            residual(use + (WO + s + 1), work(s), n0 + s, 2 * l, it * SUB + (ln0 * SUB + s + 1))
                if l == 0:
                    a0, h0, ln0 = ffn_at
                    brows += 16
                    dve.wait_ge(brow_in, brows)
                    dve.wait_ge(a_free, a0)
                    dve.tensor_scalar(bo_row[:, :], bo_row[:, :], gate[:, 1:2], None, ALU.mult).then_inc(bo_scaled, 1)
                    raws += 16
                    lower_of_weights(raws, splits, ((wa_lo[:, :, :], raw_a, wa_hi[:, :, :]),))
                    splits += 1
                    with dve.Fori(0, STEPS) as it:
                        use = it * FFN_USES + a0
                        layer_norm(it + ln0, it * SUB)
                        for c in range(CH):
                            lower(it * CH + (h0 + c + 1), work(c), xt_lo[:, c, :], xt_hi[:, c, :])
                        for s in range(SUB):
                            residual(use + (CH + s + 1), work(s), it * SUB + s, 1, it * SUB + (ln0 * SUB + s + 1))

        @block.tensor
        def _(pe):
            pe.sem_inc(t_full, CREDIT)
            pe.wait_ge(consts, 4)

            def three_passes(out, pairs):
                n = 3 * len(pairs)
                j = 0
                for (w_hi, w_lo), (m_hi, m_lo) in pairs:
                    for w, m in ((w_hi, m_hi), (w_hi, m_lo), (w_lo, m_hi)):
                        last = nc.tensor.matmul(out, w, m, start=(j == 0), stop=(j == n - 1))
                        j += 1
                return last

            def transposes(use, ln, bank_of):
                for c in range(CH):
                    pe.wait_ge(a_free, use + (c - 1))
                    for s in range(SUB):
                        if c == 0:
                            pe.wait_ge(xn_ready, ln * SUB + (s + 1))
                        last = nc.tensor.transpose(work(c)[:, s * P:(s + 1) * P], xn[:, s, c * P:(c + 1) * P], ident[:, :])
                    last.then_inc(a_full, 1)

            def out_rows(use, s, hi, lo):
                q = slice(s * P, (s + 1) * P)
                three_passes(work(s), [((xt_hi[:, c, q], xt_lo[:, c, q]), (hi[:, c, :], lo[:, c, :])) for c in range(CH)])\
                    .then_inc(a_full, 1)

            raws = 32
            for l in range(LAYERS):
                if l:
                    raws += 32
                for b in range(B):
                    raws += 32
                    a0, _ = kv_at[l, b]
                    pe.wait_ge(raw_in, raws)
                    if (l, b) == (0, 0):
                        pe.wait_ge(small_in, 144)
                    kv = slice(b * KEYS, (b + 1) * KEYS)
                    for g in range(CH):
                        if a0 + g >= 2:
                            pe.wait_ge(a_free, a0 + g - 1)
                        for c in range(CH):
                            last = nc.tensor.matmul(work(a0 + g)[:, 0:KEYS], raw_a[:, c, g * P:(g + 1) * P],
                                                    ctx_t[:, c, kv], start=(c == 0), stop=(c == CH - 1))
                        last.then_inc(a_full, 1)
                    pe.wait_ge(a_free, a0 + CH - 1)
                    for c in range(CH):
                        last = nc.tensor.matmul(work(a0 + CH), ctx_t[:, c, b * KEYS:b * KEYS + P], raw_b[:, c, :],
                                                start=(c == 0), stop=(c == CH - 1))
                    last.then_inc(a_full, 1)
                    pe.wait_ge(a_free, a0 + CH)
                    for h in range(HPG):
                        for c in range(CH):
                            last = nc.tensor.matmul(
                                work(a0 + CH + 1)[h * HD:h * HD + REM, 0:P], ctx_t[:, c, b * KEYS + P:(b + 1) * KEYS],
                                raw_b[:, c, :].rearrange("p (g h d) -> p g h d", g=CH, h=HPG)[:, :, h, :],
                                start=(c == 0), stop=(c == CH - 1))
                    last.then_inc(a_full, 1)
                    a0, _, att0, ln0 = att_at[l, b]
                    pe.wait_ge(split_lo, 3 * l + 2)
                    with pe.Fori(0, STEPS_B) as it:
                        use = it * ATT_USES + a0
                        transposes(use, it + ln0, 0)
                        pe.wait_ge(a_free, use + CH)
                        for m in range(CH):
                            if m >= 2:
                                pe.wait_ge(a_free, use + (QP + m - 1))
                            ms = slice(m * P, (m + 1) * P)
                            three_passes(work(m), [((wa_hi[:, c, ms], wa_lo[:, c, ms]), (xt_hi[:, c, :], xt_lo[:, c, :]))
                                                   for c in range(CH)]).then_inc(a_full, 1)
                        for k in range(UNITS + LAG_T + 2):
                            if k < UNITS:
                                g, s = k // SUB, k % SUB
                                if s == 0:
                                    pe.wait_ge(a_free, use + (QP + g + 1))
                                q = slice(s * P, (s + 1) * P)
                                for half in range(2):
                                    v = 2 * k + half
                                    pe.wait_ge(s_free, (it + att0) * (2 * UNITS) + (max(v - 3, 0) + CREDIT))
                                    cs = slice(half * HALF, (half + 1) * HALF)
                                    three_passes(score_bank(v), [((q_hi[:, g, q], q_lo[:, g, q]),
                                                                  (k_hi[:, g, cs], k_lo[:, g, cs]))]).then_inc(s_full, 1)
                            t = k - LAG_T
                            if 0 <= t < UNITS:
                                g, s = t // SUB, t % SUB
                                unit = (it + att0) * UNITS + t
                                pe.wait_ge(pn_done, unit + (1 + CREDIT))
                                pe.wait_ge(ptm_out, unit + CREDIT)
                                if s == 0:
                                    pe.wait_ge(ptr_out, (it + att0) * CH + (g + CREDIT))
                                nc.tensor.transpose(PTR[:, s * P:(s + 1) * P], pn[:, t % 2, HPG * P:], ident[:, :])
                                for h in range(HPG):
                                    last = nc.tensor.transpose(PTM[:, h * P:(h + 1) * P],
                                                               pn[:, t % 2, h * P:(h + 1) * P], ident[:, :])
                                last.then_inc(t_full, 1)
                            if t >= SUB and t % SUB == 0:
                                g = t // SUB - 1
                                pe.wait_ge(ptm_out, (it + att0) * UNITS + ((g + 1) * SUB + CREDIT))
                                pe.wait_ge(ptr_out, (it + att0) * CH + (g + 1 + CREDIT))
                                pe.wait_ge(a_free, use + (PV + g - 1))
                                nc.tensor.matmul(work(g), v_rem[:, g, :], pT[:, g % 2, HPG, :], start=True, stop=False,
                                                 skip_group_check=True)
                                for h in range(HPG):
                                    last = nc.tensor.matmul(work(g)[h * HD:(h + 1) * HD, :],
                                                            v_main[:, (g * HPG + h) * HD:(g * HPG + h + 1) * HD],
                                                            pT[:, g % 2, h, :], start=False, stop=(h == HPG - 1),
                                                            skip_group_check=True)
                                last.then_inc(a_full, 1)
                        pe.wait_ge(a_free, use + WO)
                        for s in range(SUB):
                            if s >= 2:
                                pe.wait_ge(a_free, use + (WO + s - 1))
                            out_rows(use, s, wo_hi, wo_lo)
                if l == 0:
                    a0, _, ln0 = ffn_at
                    raws += 16
                    pe.wait_ge(split_lo, 3)
                    with pe.Fori(0, STEPS) as it:
                        use = it * FFN_USES + a0
                        transposes(use, it + ln0, 0)
                        pe.wait_ge(a_free, use + CH)
                        for s in range(SUB):
                            if s >= 2:
                                pe.wait_ge(a_free, use + (CH + s - 1))
                            out_rows(use, s, wa_hi, wa_lo)


def kv_count(l, b):
    return l * B + b


def quantised_ffn(nc, w1, b1_cols, w2, b2_row, gates, out, X, ident):
    PIECES = 2 * FC
    HB = 4
    ctx = ExitStack()
    with ctx:
        def sb(name, shape, dt):
            return ctx.enter_context(nc.sbuf_tensor(name, shape, dt))

        def sem(name):
            return ctx.enter_context(nc.semaphore(name))

        xq_t = sb("xq_t", [P, CH, B * S], BF16)
        w1_t = sb("w1_t", [P, CH, F], BF16)
        w2_t = sb("w2_t", [P, FC, D], BF16)
        raw = sb("raw", [P, FC, D], FP32)
        h_relu = sb("h_relu", [P, HB, TOK], FP32)
        rounded = sb("rounded", [P, 2, D], BF16)
        diag = sb("diag", [P, P], FP32)
        ones = sb("ones", [P, P], FP32)
        ident_b = sb("ident_b", [P, P], BF16)
        magic = sb("magic", [P, 1], FP32)
        s_w = sb("s_w", [P, 2, FC], FP32)
        r_w = sb("r_w", [P, 2, FC], FP32)
        stats = sb("stats2", [P, TILES, 6], FP32)
        meanvar = sb("meanvar2", [P, TILES, 2], FP32)
        vareps = sb("vareps2", [P, TILES], FP32)
        rstd = sb("rstd2", [P, TILES], FP32)
        neg_half = sb("neg_half2", [P, TILES], FP32)
        row_max = sb("row_max", [P, TILES], FP32)
        x_bias = sb("x_bias", [P, TILES], FP32)
        x_scale = sb("x_scale", [P, TILES], FP32)
        h_max = sb("h_max", [P, STEPS, FC], FP32)
        col = sb("col", [P, 12, FC], FP32)
        one = sb("one", [P, 16], FP32)
        b1_c = sb("b1_c", [P, FC], FP32)
        b2_r = sb("b2_r", [P, D], FP32)
        s2_r = sb("s2_r", [P, D], FP32)
        row_tmp = sb("row_tmp", [P, 3, D], FP32)
        gate_raw = sb("gate_raw2", [P, 4], FP32)
        gate = sb("gate2", [P, 4], FP32)
        ps = ctx.enter_context(nc.psum_tensor("ps2", [P, 8, 512], FP32))
        consts = sem("q_consts")
        w1_in = sem("q_w1_in")
        w2_in = sem("q_w2_in")
        small_in = sem("q_small")
        vec = sem("q_vec")
        w_scaled = sem("q_ws")
        w_magic = sem("q_wm")
        w_rounded = sem("q_wr")
        w_turned = sem("q_wt")
        w_out = sem("q_wo")
        gate_done = sem("q_gate")
        diag_done = sem("q_diag")
        srow_full = sem("q_srow")
        aggr_done = sem("q_aggr")
        rstd_done = sem("q_rstd")
        part_max = sem("q_pmax")
        global_max = sem("q_gmax")
        x_scaled = sem("q_xs")
        x_relu = sem("q_xr")
        x_rounded = sem("q_xi")
        x_turned = sem("q_xt")
        x_out = sem("q_xo")
        m_full = sem("q_mf")
        m_free = sem("q_mr")
        h_scaled = sem("q_hs")
        rows_done = sem("q_rows")
        h_full = sem("q_hf")
        h_relued = sem("q_hr")
        h_rounded = sem("q_hi")
        o_full = sem("q_of")
        o_scaled = sem("q_os")
        o_done = sem("q_od")
        pre_added = sem("q_pre")
        stored = sem("q_st")
        block = ctx.enter_context(nc.Block())
        h_q = raw[:, 0:FC // 2, :].rearrange("p f d -> p (f d)").bitcast(BF16).rearrange("p (f n) -> p f n", f=FC)

        def psum_bf16(bank):
            return ps[:, bank, 0:TOK // 2].bitcast(BF16)

        def tile_of(n):
            return flat(X[:, bass.ds(n, 1), :])

        @block.sync
        def _(sp):
            sp.dma_start(raw[:, :, :], w1.rearrange("(f p) d -> p f d", p=P)).then_inc(w1_in, 16)
            sp.dma_start(b1_c[:, :], b1_cols).then_inc(small_in, 16)
            sp.dma_start(b2_r[:, :], b2_row.partition_broadcast(P)).then_inc(small_in, 16)
            sp.dma_start(gate_raw[:, :], gates.partition_broadcast(P)).then_inc(small_in, 16)
            sp.wait_ge(w_magic, FC)
            sp.dma_start(raw[:, :, :].rearrange("p (c r) d -> p c (r d)", c=CH),
                         w2.rearrange("(c p) f -> p c f", p=P)).then_inc(w2_in, 16)
            ov = out.rearrange("(t p) n -> p t n", p=P)
            with sp.Fori(0, STEPS) as it:
                sp.wait_ge(o_done, it * SUB + SUB)
                sp.dma_start(ov[:, bass.ds(it * SUB, SUB), :], X[:, bass.ds(it * SUB, SUB), :]).then_inc(stored, 16)
            sp.wait_ge(stored, 16 * STEPS)

        @block.gpsimd
        def _(pool):
            pool.memset(ones[:, :], 1.0).then_inc(consts, 1)
            pool.memset(magic[:, :], MAGIC).then_inc(consts, 1)
            pool.memset(neg_half[:, :], -0.5).then_inc(consts, 1)
            pool.tensor_copy(ident_b[:, :], ident[:, :]).then_inc(consts, 1)
            pool.wait_ge(consts, 3)
            pool.wait_ge(aggr_done, 1)
            pool.tensor_scalar(vareps[:, :], meanvar[:, :, 1], LN_EPS, None, ALU.add).then_inc(rstd_done, 1)
            pool.wait_ge(rstd_done, 1)
            pool.tensor_tensor(rstd[:, :], vareps[:, :], neg_half[:, :], ALU.pow).then_inc(rstd_done, 1)
            pool.wait_ge(rows_done, 2)
            with pool.Fori(0, TILES) as n:
                pool.tensor_tensor(tile_of(n), tile_of(n), b2_r[:, :], ALU.add).then_inc(pre_added, 1)

        @block.scalar
        def _(act):
            act.sem_inc(h_relued, CREDIT)
            act.wait_ge(small_in, 48)
            act.activation(gate[:, :], gate_raw[:, :], ACT.Tanh).then_inc(gate_done, 1)
            act.wait_ge(consts, 4)

            def copy_piece(p):
                act.wait_ge(w_turned, p + 1)
                src = psum_bf16(p % 2).rearrange("p (i q) -> p i q", i=4)
                if p < FC:
                    dst = w1_t[:, :, p * P:(p + 1) * P]
                else:
                    c, r = (p - FC) // 4, (p - FC) % 4
                    dst = w2_t[:, 4 * r:4 * r + 4, c * P:(c + 1) * P]
                act.activation(dst, src, ACT.Copy).then_inc(w_out, 1)

            for p in range(PIECES):
                if p % FC == 0:
                    act.wait_ge(w_scaled, p // FC + 1)
                c = p if p < FC else (p - FC) // 4
                if p >= 2:
                    act.wait_ge(w_rounded, p - 1)
                act.activation(h_relu[:, p % 2, :], raw[:, p % FC, :], ACT.Identity, scale=r_w[:, p // FC, c:c + 1],
                               bias=magic[:, :]).then_inc(w_magic, 1)
                if p >= 2:
                    copy_piece(p - 2)
            copy_piece(PIECES - 2)
            copy_piece(PIECES - 1)
            act.wait_ge(x_scaled, 1)
            act.wait_ge(w_rounded, PIECES)
            for n in range(TILES):
                if n >= 2:
                    act.wait_ge(x_rounded, n - 1)
                act.activation(h_relu[:, n % 2, :], X[:, n, :], ACT.Relu, scale=x_scale[:, n:n + 1],
                               bias=x_bias[:, n:n + 1]).then_inc(x_relu, 1)
            act.wait_ge(h_scaled, 1)
            with act.Fori(0, STEPS) as it:
                for f in range(FC):
                    act.wait_ge(h_full, it * FC + (f + 1))
                    act.wait_ge(h_rounded, it * FC + (max(f + 1 - HB, 0) + CREDIT))
                    act.activation(h_relu[:, f % HB, :], ps[:, f % HB, :], ACT.Relu, scale=col[:, 8, f:f + 1],
                                   bias=col[:, 9, f:f + 1]).then_inc(h_relued, 1)

        @block.vector
        def _(dve):
            steps = [0]

            def step(i):
                steps[0] += 1
                i.then_inc(vec, 1)
                dve.wait_ge(vec, steps[0])

            def magic_round(dst, v, tmp, keep):
                step(dve.tensor_scalar(tmp, v, MAGIC, -MAGIC, ALU.add, ALU.add))
                step(dve.tensor_tensor(keep, v, v, ALU.mult))
                step(dve.tensor_scalar(keep, keep, 2.0**44, None, ALU.is_lt))
                step(dve.tensor_tensor(tmp, tmp, v, ALU.subtract))
                step(dve.tensor_tensor(tmp, tmp, keep, ALU.mult))
                step(dve.tensor_tensor(dst, v, tmp, ALU.add))

            for buffers_free in (h_rounded, m_free, o_scaled):
                dve.sem_inc(buffers_free, CREDIT)
            for n in range(TILES):
                dve.bn_stats(stats[:, n, :], X[:, n, :])
            step(dve.tensor_reduce(row_max[:, :], X[:, :, :], axis=AX.X, op=ALU.max))
            for n in range(TILES):
                i = dve.bn_aggr(meanvar[:, n, :], stats[:, n, :])
            i.then_inc(aggr_done, 1)
            for j, arrived in enumerate((w1_in, w2_in)):
                n = FC if j == 0 else CH
                dve.wait_ge(arrived, 16)
                src = raw[:, :, :] if j == 0 else raw[:, :, :].rearrange("p (c r) d -> p c (r d)", c=CH)
                step(dve.tensor_reduce(s_w[:, j, 0:n], src, axis=AX.X, op=ALU.max, apply_absolute_value=True))
                step(dve.tensor_scalar(s_w[:, j, 0:n], s_w[:, j, 0:n], Q_EPS, 1.0 / 127.0, ALU.max, ALU.mult))
                dve.reciprocal(r_w[:, j, 0:n], s_w[:, j, 0:n]).then_inc(w_scaled, 1)
                for p in range(j * FC, (j + 1) * FC):
                    dve.wait_ge(w_magic, p + 1)
                    if p >= 2:
                        dve.wait_ge(w_turned, p - 1)
                    dve.tensor_scalar(rounded[:, p % 2, :], h_relu[:, p % 2, :], -MAGIC, None, ALU.add).then_inc(w_rounded, 1)

            def maximum_of_partitions(j):
                dve.tensor_scalar(diag[:, :], ident[:, :], one[:, 2 * j:2 * j + 1], None, ALU.mult).then_inc(part_max, 1)
                dve.wait_ge(global_max, j + 1)
                step(dve.tensor_reduce(one[:, 2 * j + 1:2 * j + 2], ps[:, 6, 0:P], axis=AX.X, op=ALU.max))

            dve.wait_ge(rstd_done, 2)
            step(dve.tensor_tensor(row_max[:, :], row_max[:, :], meanvar[:, :, 0], ALU.subtract))
            step(dve.tensor_tensor(row_max[:, :], row_max[:, :], rstd[:, :], ALU.mult))
            step(dve.tensor_reduce(one[:, 0:1], row_max[:, :], axis=AX.X, op=ALU.max))
            maximum_of_partitions(0)
            step(dve.tensor_scalar(one[:, 4:5], one[:, 1:2], Q_EPS, 1.0 / 255.0, ALU.max, ALU.mult))
            step(dve.reciprocal(one[:, 5:6], one[:, 4:5]))
            step(dve.tensor_scalar(x_scale[:, :], rstd[:, :], one[:, 5:6], None, ALU.mult))
            step(dve.tensor_scalar(x_bias[:, :], meanvar[:, :, 0], -1.0, None, ALU.mult))
            dve.tensor_tensor(x_bias[:, :], x_bias[:, :], x_scale[:, :], ALU.mult).then_inc(x_scaled, 1)
            for c in range(CH):
                if c:
                    dve.wait_ge(srow_full, c)
                dve.tensor_scalar(diag[:, :], ident[:, :], s_w[:, 1, c:c + 1], None, ALU.mult).then_inc(diag_done, 1)
            dve.wait_ge(srow_full, CH)
            dve.tensor_copy(s2_r[:, :], ps[:, 7, :]).then_inc(vec, 1)
            steps[0] += 1

            def copy_x(n):
                dve.wait_ge(x_turned, n + 1)
                dve.tensor_copy(xq_t[:, :, n * P:(n + 1) * P],
                                psum_bf16(2 + n % 2).rearrange("p (i q) -> p i q", i=4)).then_inc(x_out, 1)

            for n in range(TILES):
                dve.wait_ge(x_relu, n + 1)
                if n >= 2:
                    dve.wait_ge(x_turned, n - 1)
                dve.tensor_scalar(rounded[:, n % 2, :], h_relu[:, n % 2, :], MAGIC, -MAGIC, ALU.add, ALU.add).then_inc(x_rounded, 1)
                if n >= 1:
                    copy_x(n - 1)
            copy_x(TILES - 1)
            sc1, bq1, v1, t1, k1 = (col[:, j, :] for j in range(5))
            dve.wait_ge(small_in, 48)
            step(dve.tensor_scalar(sc1, s_w[:, 0, :], one[:, 4:5], None, ALU.mult))
            step(dve.reciprocal(v1, sc1))
            step(dve.tensor_tensor(v1, v1, b1_c[:, :], ALU.mult))
            magic_round(bq1, v1, t1, k1)
            step(dve.tensor_tensor(bq1, bq1, sc1, ALU.mult))
            with dve.Fori(0, STEPS) as it:
                for f in range(0, FC, 2):
                    dve.wait_ge(m_full, it * (FC // 2) + (f // 2 + 1))
                    dve.tensor_reduce(flat(h_max[:, bass.ds(it, 1), f:f + 2]), ps[:, f % 8:f % 8 + 2, :], axis=AX.X,
                                      op=ALU.max).then_inc(m_free, 1)
            dve.wait_ge(m_free, STEPS * FC // 2 + CREDIT)
            step(dve.tensor_reduce(col[:, 5, :], h_max[:, :, :].rearrange("p s f -> p f s"), axis=AX.X, op=ALU.max))
            step(dve.tensor_tensor(col[:, 5, :], col[:, 5, :], sc1, ALU.mult))
            step(dve.tensor_tensor(col[:, 5, :], col[:, 5, :], bq1, ALU.add))
            step(dve.tensor_scalar(col[:, 5, :], col[:, 5, :], 0.0, None, ALU.max))
            step(dve.tensor_reduce(one[:, 2:3], col[:, 5, :], axis=AX.X, op=ALU.max))
            maximum_of_partitions(1)
            step(dve.tensor_scalar(one[:, 6:7], one[:, 3:4], Q_EPS, 1.0 / 255.0, ALU.max, ALU.mult))
            step(dve.reciprocal(one[:, 7:8], one[:, 6:7]))
            step(dve.tensor_scalar(col[:, 8, :], sc1, one[:, 7:8], None, ALU.mult))
            dve.tensor_scalar(col[:, 9, :], bq1, one[:, 7:8], None, ALU.mult).then_inc(h_scaled, 1)
            dve.wait_ge(gate_done, 1)
            v2, t2, k2 = (row_tmp[:, j, :] for j in range(3))
            step(dve.tensor_scalar(s2_r[:, :], s2_r[:, :], one[:, 6:7], None, ALU.mult))
            step(dve.reciprocal(v2, s2_r[:, :]))
            step(dve.tensor_tensor(v2, v2, b2_r[:, :], ALU.mult))
            magic_round(v2, v2, t2, k2)
            step(dve.tensor_tensor(v2, v2, s2_r[:, :], ALU.mult))
            dve.tensor_scalar(b2_r[:, :], v2, gate[:, 3:4], None, ALU.mult).then_inc(rows_done, 1)
            dve.tensor_scalar(s2_r[:, :], s2_r[:, :], gate[:, 3:4], None, ALU.mult).then_inc(rows_done, 1)
            dve.wait_ge(rows_done, 2)
            with dve.Fori(0, STEPS) as it:
                for f in range(FC):
                    dve.wait_ge(h_relued, it * FC + (f + 1 + CREDIT))
                    if f == 0:
                        dve.wait_ge(o_full, it * SUB + CREDIT)
                    dve.tensor_scalar(h_q[:, f, :], h_relu[:, f % HB, :], MAGIC, -MAGIC, ALU.add, ALU.add).then_inc(h_rounded, 1)
                for s in range(SUB):
                    dve.wait_ge(o_full, it * SUB + (s + 1 + CREDIT))
                    dve.wait_ge(pre_added, it * SUB + (s + 1))
                    if s >= 2:
                        dve.wait_ge(o_done, it * SUB + (s - 1))
                    dve.tensor_tensor(row_tmp[:, s % 2, :], ps[:, 4 + s % 2, :], s2_r[:, :], ALU.mult).then_inc(o_scaled, 1)
                    dve.wait_ge(o_scaled, it * SUB + (s + 1 + CREDIT))
                    n = it * SUB + s
                    dve.tensor_tensor(tile_of(n), tile_of(n), row_tmp[:, s % 2, :], ALU.add).then_inc(o_done, 1)

        @block.tensor
        def _(pe):
            pe.sem_inc(o_full, CREDIT)
            pe.wait_ge(consts, 4)
            for p in range(PIECES):
                pe.wait_ge(w_rounded, p + 1)
                if p >= 2:
                    pe.wait_ge(w_out, p - 1)
                for i in range(4):
                    last = nc.tensor.transpose(psum_bf16(p % 2)[:, i * P:(i + 1) * P], rounded[:, p % 2, i * P:(i + 1) * P],
                                               ident_b[:, :])
                last.then_inc(w_turned, 1)

            def spread_maxima(j):
                pe.wait_ge(part_max, j + 1)
                nc.tensor.matmul(ps[:, 6, 0:P], ones[:, :], diag[:, :], start=True, stop=True).then_inc(global_max, 1)

            spread_maxima(0)
            for c in range(CH):
                pe.wait_ge(diag_done, c + 1)
                nc.tensor.matmul(ps[:, 7, c * P:(c + 1) * P], ones[:, :], diag[:, :], start=True, stop=True)\
                    .then_inc(srow_full, 1)
            for n in range(TILES):
                pe.wait_ge(x_rounded, n + 1)
                if n >= 2:
                    pe.wait_ge(x_out, n - 1)
                for i in range(4):
                    last = nc.tensor.transpose(psum_bf16(2 + n % 2)[:, i * P:(i + 1) * P],
                                               rounded[:, n % 2, i * P:(i + 1) * P], ident_b[:, :])
                last.then_inc(x_turned, 1)

            def h_chunk(bank, it, f):
                for c in range(CH):
                    last = nc.tensor.matmul(ps[:, bank, :], w1_t[:, c, f * P:(f + 1) * P],
                                            xq_t[:, c, bass.ds(it * TOK, TOK)], start=(c == 0), stop=(c == CH - 1))
                return last

            pe.wait_ge(x_out, TILES)
            pe.wait_ge(w_out, PIECES)
            with pe.Fori(0, STEPS) as it:
                for f in range(FC):
                    if f % 2 == 0:
                        pe.wait_ge(m_free, it * (FC // 2) + (max(f // 2 - 3, 0) + CREDIT))
                    last = h_chunk(f % 8, it, f)
                    if f % 2:
                        last.then_inc(m_full, 1)
            pe.wait_ge(m_free, STEPS * FC // 2 + CREDIT)
            spread_maxima(1)
            with pe.Fori(0, STEPS) as it:
                for f in range(FC):
                    pe.wait_ge(h_relued, it * FC + (max(f + 1 - HB, 0) + CREDIT))
                    h_chunk(f % HB, it, f).then_inc(h_full, 1)
                for s in range(SUB):
                    pe.wait_ge(o_scaled, it * SUB + (max(s - 1, 0) + CREDIT))
                    for f in range(FC):
                        if s == 0:
                            pe.wait_ge(h_rounded, it * FC + (f + 1 + CREDIT))
                        last = nc.tensor.matmul(ps[:, 4 + s % 2, :], h_q[:, f, s * P:(s + 1) * P], w2_t[:, f, :],
                                                start=(f == 0), stop=(f == FC - 1))
                    last.then_inc(o_full, 1)


def flamingo(nc, x, ctxT, mask, gates, cols, rows, weights, W0, logits, u, w1, b1_cols, w2, b2_row, out):
    ctx = ExitStack()
    with ctx:
        def sb(name, shape, dt):
            return ctx.enter_context(nc.sbuf_tensor(name, shape, dt))

        def sem(name):
            return ctx.enter_context(nc.semaphore(name))

        X = sb("X", [P, TILES, D], FP32)
        ident = sb("ident", [P, P], FP32)
        attention_layers(nc, x, ctxT, mask, gates, cols, rows, weights, W0, logits, u, X, ident)
        quantised_ffn(nc, w1, b1_cols, w2, b2_row, gates, out, X, ident)


def kernel(**inputs):
    import concourse.bacc as bacc
    from concourse.bass_utils import run_bass_kernel_spmd

    nc = bacc.Bacc("TRN2", target_bir_lowering=False, num_devices=1)
    arrays = {}

    def give(name, a):
        a = np.ascontiguousarray(a)
        arrays[name] = a
        return nc.dram_tensor(name, a.shape, mybir.dt.from_np(a.dtype), kind="ExternalInput").ap()

    i = {k: np.asarray(v) for k, v in inputs.items()}

    def columns(name, a):
        return give(name, a.reshape(-1, P).T)

    x = give("x_in", i["x"].reshape(B * S, D))
    ctxT = give("ctx_T", i["ctx_1024"].reshape(B * KEYS, D).T)
    mask = give("mask_in", i["mask_BxS2_ik0"].reshape(B * KEYS))
    gates = give("gates", np.stack([i["g_xattn"], i["g_ffn"]], axis=1).reshape(4))
    cols, rows, weights = [], [], []
    for l in range(LAYERS):
        pre = f"L{l}_xattn_"
        cols.append([columns(f"bq{l}", i[pre + "bq"]), columns(f"bk{l}", i[pre + "bk"])])
        rows.append([give(f"bv{l}", i[pre + "bv"]), give(f"bo{l}", i[pre + "bo"])])
        weights.append([give(f"W{n}T{l}", i[pre + "W" + n].T) for n in "qkvo"])
    rows.append(give("b0", i["L0_ffn_b"]))
    W0 = give("W0", i["L0_ffn_W"])
    logits = give("logits", i["L0_ffn_logits"].reshape(1, OPS))
    u = give("u", i["L0_ffn_u"].reshape(1, OPS))
    w1, w2 = give("w1", i["L1_ffn_w1"]), give("w2", i["L1_ffn_w2"])
    b1_cols, b2_row = columns("b1", i["L1_ffn_b1"]), give("b2", i["L1_ffn_b2"])
    out = nc.dram_tensor("out", (B * S, D), FP32, kind="ExternalOutput").ap()
    flamingo(nc, x, ctxT, mask, gates, cols, rows, weights, W0, logits, u, w1, b1_cols, w2, b2_row, out)
    r = run_bass_kernel_spmd(nc, [arrays], core_ids=[0])
    return r.results[0]["out"].reshape(B, S, D)
```

```python
from contextlib import ExitStack

import numpy as np
import concourse.bass as bass
from concourse import mybir

FP32 = mybir.dt.float32
FP32R = mybir.dt.float32r
BF16 = mybir.dt.bfloat16
I32 = mybir.dt.int32
U32 = mybir.dt.uint32
ALU = mybir.AluOpType
ACT = mybir.ActivationFunctionType
AX = mybir.AxisListType

P = 128
B, S, D = 2, 2048, 512
KEYS = 154
HEADS = 16
HD = D // HEADS
F = 2048
OPS = 8
LAYERS = 2
CH = D // P
HPG = P // HD
TOK = 512
SUB = TOK // P
TILES = B * S // P
STEPS_B = S // TOK
STEPS = B * STEPS_B
UNITS = CH * SUB
REM = KEYS - P
HALF = 2 * KEYS
FC = F // P
SCALE = float(HD) ** -0.5
CLAMP = 50000.0
NEG_FILL = -9.0e15
LN_EPS = 1e-5
Q_EPS = 1e-8
MAGIC = 12582912.0

CREDIT = 1
LAG_T = 3

WINDOW = {0: [("Q", 2)], 1: [("Q", 3)], 3: [("PV", 3)], 4: [("WO", 0)], 5: [("WO", 1)], 6: [("WO", 2), ("WO", 3)],
          7: [("PV", 0)], 8: [("XT", 0)], 9: [("XT", 1)], 10: [("XT", 2), ("XT", 3)], 11: [("PV", 1)],
          13: [("Q", 0)], 14: [("Q", 1)], 15: [("PV", 2)]}
DRAIN = {16: [("Q", 2)], 17: [("Q", 3)], 19: [("PV", 3)], 20: [("WO", 0)], 21: [("WO", 1)], 22: [("WO", 2)],
         23: [("WO", 3)]}
OF_BEFORE = (("Q", 2), ("Q", 3), ("PV", 3), ("WO", 0), ("WO", 1), ("WO", 2), ("WO", 3))
OF_NEXT = (("XT", 0), ("XT", 1), ("XT", 2), ("XT", 3), ("Q", 0), ("Q", 1))


def select(table, leave_out):
    events, uses, his = {}, 0, 0
    for k in sorted(table):
        events[k] = []
        for kind, i in table[k]:
            if (kind, i) not in leave_out:
                events[k].append((kind, i, uses, his))
                uses, his = uses + 1, his + (kind != "WO")
    return events, uses, his


EVENTS = {"first": select(WINDOW, OF_BEFORE),
          "full": select(WINDOW, ()),
          "last": select(WINDOW, OF_NEXT),
          "drain": select(DRAIN, ()),
          "end": select(DRAIN, (("Q", 2), ("Q", 3)))}
CARRIED = ("PV", 2, -1, -1)

KV_USES, KV_HIS = CH + 2, CH
PROLOGUE = 2 * CH
FULL_USES, FULL_HIS = EVENTS["full"][1:]
DENSE = [("OUT", 0), ("XT", 0), ("XT", 1), ("OUT", 1), ("XT", 2), ("XT", 3), ("OUT", 2), ("OUT", 3)]
DENSE_USES = len(DENSE)


def flat(ap):
    return ap.rearrange("p a n -> p (a n)")


def attention_layers(nc, x, ctxT, mask, gates, cols, rows, weights, W0, logits, u, X, ident):
    ctx = ExitStack()
    with ctx:
        def sb(name, shape, dt):
            return ctx.enter_context(nc.sbuf_tensor(name, shape, dt))

        def sem(name):
            return ctx.enter_context(nc.semaphore(name))

        wa_hi = sb("wa_hi", [P, CH, D], FP32R)
        wa_lo = sb("wa_lo", [P, CH, D], FP32R)
        wo_hi = sb("wo_hi", [P, CH, D], FP32R)
        wo_lo = sb("wo_lo", [P, CH, D], FP32R)
        k_hi = sb("k_hi", [P, CH, HPG * KEYS], FP32R)
        k_lo = sb("k_lo", [P, CH, HPG * KEYS], FP32R)
        v_main = sb("v_main", [P, D], FP32)
        v_rem = sb("v_rem", [P, CH, P], FP32)
        xt_hi = sb("xt_hi", [P, CH, TOK], FP32R)
        xt_lo = sb("xt_lo", [P, CH, TOK], FP32R)
        ot_hi = sb("ot_hi", [P, CH, TOK], FP32R)
        ot_lo = sb("ot_lo", [P, CH, TOK], FP32R)
        q_hi = sb("q_hi", [P, CH, TOK], FP32R)
        q_lo = sb("q_lo", [P, CH, TOK], FP32R)
        xn = sb("xn", [P, SUB, D], FP32)
        sc = sb("sc", [P, 2, HPG, KEYS], FP32)
        soft = sb("soft", [P, 2 * HPG * KEYS + 2 * HPG * P], FP32)
        pn_rem = sb("pn_rem", [P, 2, P], FP32)
        pT = sb("pT", [P, HPG + 1, TOK], FP32)
        bias_cols = sb("bias_cols", [P, 3 * LAYERS, CH], FP32)
        bk_scaled = sb("bk_scaled", [P, LAYERS, CH], FP32)
        bo_row = sb("bo_row", [P, D], FP32)
        mask_add = sb("mask_add", [P, B, KEYS], FP32)
        gate_raw = sb("gate_raw", [P, 4], FP32)
        gate = sb("gate", [P, 4], FP32)
        stats = sb("stats", [P, SUB, 6], FP32)
        meanvar = sb("meanvar", [P, SUB, 2], FP32)
        vareps = sb("vareps", [P, SUB], FP32)
        rstd = sb("rstd", [P, SUB], FP32)
        neg_half = sb("neg_half", [P, SUB], FP32)
        smax = sb("smax", [P, 2, HPG], FP32)
        nmax = sb("nmax", [P, 2, HPG], FP32)
        rsum = sb("rsum", [P, 2, HPG], FP32)
        wait_pad = sb("wait_pad", [P, 1], FP32)
        rec = sb("rec", [P, 2, HPG], FP32)
        gum = sb("gum", [1, 8, OPS], FP32)
        gmax = sb("gmax", [1, OPS], FP32)
        gidx = sb("gidx", [1, OPS], U32)
        ps = ctx.enter_context(nc.psum_tensor("ps", [P, 8, 512], FP32))
        consts = sem("consts")
        zeroed = sem("zeroed")
        small_in = sem("small_in")
        x_in0 = sem("x_in0")
        x_in1 = sem("x_in1")
        raw_in = sem("raw_in")
        brow_in = sem("brow_in")
        prep = sem("prep")
        act_prep = sem("act_prep")
        bo_scaled = sem("bo_scaled")
        pick = sem("pick")
        split_hi = sem("split_hi")
        split_lo = sem("split_lo")
        stats_done = sem("stats_done")
        aggr_done = sem("aggr_done")
        eps_done = sem("eps_done")
        rstd_done = sem("rstd_done")
        xn_ready = sem("xn_ready")
        pre_added = sem("pre_added")
        a_full = sem("a_full")
        a_free = sem("a_free")
        hi_done = sem("hi_done")
        k_tmp_done = sem("k_tmp_done")
        s_full = sem("s_full")
        s_free = sem("s_free")
        masked = sem("masked")
        max_done = sem("max_done")
        exp_done = sem("exp_done")
        rec_done = sem("rec_done")
        pn_done = sem("pn_done")
        t_full = sem("t_full")
        ptm_out = sem("ptm_out")
        ptr_out = sem("ptr_out")
        block = ctx.enter_context(nc.Block())

        pr = soft[:, 0:2 * HPG * KEYS].rearrange("p (b h k) -> p b h k", b=2, h=HPG)
        pn_main = soft[:, 2 * HPG * KEYS:].rearrange("p (b h k) -> p b h k", b=2, h=HPG)
        raw_a = pT[:, 0:CH, :]
        raw_b = soft[:, 0:CH * D].rearrange("p (c n) -> p c n", c=CH)
        scf = sc[:, :, :, :].rearrange("p b h k -> p (b h k)")
        ctx_t = scf[:, 0:CH * KEYS].rearrange("p (c k) -> p c k", c=CH)
        k_tmp = scf[:, CH * KEYS:2 * CH * KEYS].rearrange("p (c k) -> p c k", c=CH)
        mask_i = scf[:, CH * KEYS:(CH + B) * KEYS].bitcast(I32).rearrange("p (b k) -> p b k", b=B)
        mask_f = scf[:, (CH + B) * KEYS:(CH + 2 * B) * KEYS].rearrange("p (b k) -> p b k", b=B)

        def work(a):
            return ps[:, a % 2, :]

        def score_bank(v):
            return ps[:, 2 + v % 4, 0:HALF]

        PTM, PTR = ps[:, 6, :], ps[:, 7, :]

        def tile_of(n):
            return flat(X[:, bass.ds(n, 1), :])

        at = {}
        uses = his = 0

        def part(name, part_uses, part_his):
            nonlocal uses, his
            at[name] = (uses, his)
            uses, his = uses + part_uses, his + part_his

        for l in range(LAYERS):
            part(("kv", l, 0), KV_USES, KV_HIS)
            if l:
                part("dense end", 2 * DENSE_USES - CH, CH)
            part(("prologue", l), PROLOGUE, PROLOGUE)
            part(("first", l, 0), *EVENTS["first"][1:])
            part(("full", l, 0), (STEPS_B - 1) * FULL_USES, (STEPS_B - 1) * FULL_HIS)
            part(("drain", l, 0), *EVENTS["drain"][1:])
            part(("kv", l, 1), KV_USES, KV_HIS)
            part(("first", l, 1), *EVENTS["first"][1:])
            part(("full", l, 1), (STEPS_B - 2) * FULL_USES, (STEPS_B - 2) * FULL_HIS)
            part(("last", l, 1), *EVENTS["last"][1:])
            part(("end", l, 1), *EVENTS["end"][1:])
            if l == 0:
                part("dense start", CH, CH)
                part("dense", (STEPS - 2) * DENSE_USES, (STEPS - 2) * CH)
        part("end", 0, 0)
        LN = (0, 2 * STEPS)
        LN_DENSE = STEPS

        def layer_program(eng, l, kv, prologue, units):
            def one(kind, b, step):
                a, h = at[kind, l, b]
                units(l, b, step, a, h, kind, a)

            def full(b, step, count):
                a, h = at["full", l, b]
                with eng.Fori(0, count) as it:
                    units(l, b, it + step, it * FULL_USES + a, it * FULL_HIS + h, "full", a)

            if l == 0:
                kv(l, 0)
            prologue(l)
            one("first", 0, 0)
            full(0, 1, STEPS_B - 1)
            one("drain", 0, STEPS_B - 1)
            kv(l, 1)
            one("first", 1, STEPS_B)
            full(1, STEPS_B + 1, STEPS_B - 2)
            one("last", 1, STEPS - 1)
            one("end", 1, STEPS - 1)

        def schedule(kind):
            events = EVENTS[kind][0]
            draining = kind in ("drain", "end")
            ks = range(UNITS, max(DRAIN) + 2) if draining else range(UNITS)
            carried = kind != "first"

            def events_of(k):
                if k == ks[0] - 1:
                    return [CARRIED] if carried else []
                return events.get(k, [])

            return ks, draining, carried, events_of

        @block.sync
        def _(sp):
            def load_raw(dst, src):
                sp.dma_start(dst, src.rearrange("(c p) n -> p c n", p=P)).then_inc(raw_in, 16)

            def load_kv(l, b):
                load_raw(ctx_t, ctxT[:, b * KEYS:(b + 1) * KEYS])
                load_raw(raw_a, weights[l][1])
                load_raw(raw_b, weights[l][2])

            def load_qo(l):
                sp.wait_ge(a_free, at["kv", l, 0][0] + KV_USES)
                load_raw(raw_a, weights[l][0])
                load_raw(raw_b, weights[l][3])

            def after_values(l, b):
                kind = "end" if b else "drain"
                return at[kind, l, b][0] + EVENTS[kind][0][19][0][2] + 1

            load_kv(0, 0)
            xv = x.rearrange("(t p) n -> p t n", p=P)
            early = 2 * SUB
            sp.dma_start(X[:, 0:early, :], xv[:, 0:early, :]).then_inc(x_in0, 16)
            for l in range(LAYERS):
                for k in range(3):
                    sp.dma_start(bias_cols[:, 3 * l + k, :], cols[l][k]).then_inc(small_in, 16)
            sp.dma_start(flat(mask_i), mask.partition_broadcast(P)).then_inc(small_in, 16)
            sp.dma_start(gate_raw[:, :], gates.partition_broadcast(P)).then_inc(small_in, 16)
            sp.dma_start(gum[0:1, 0, :], u).then_inc(small_in, 16)
            sp.dma_start(gum[0:1, 1, :], logits).then_inc(small_in, 16)
            sp.dma_start(bo_row[:, :], rows[0].partition_broadcast(P)).then_inc(brow_in, 16)
            load_qo(0)
            sp.dma_start(X[:, early:TILES, :], xv[:, early:TILES, :]).then_inc(x_in1, 16)
            sp.wait_ge(a_free, after_values(0, 0))
            load_kv(0, 1)
            sp.wait_ge(pick, 10)
            sp.wait_ge(a_free, after_values(0, 1))
            idx = sp.value_load(gidx[0:1, 0:1], min_val=0, max_val=OPS - 1)
            sp.dma_start(raw_a, W0[bass.ds(idx, 1), :, :].rearrange("a (c p) n -> p (a c) n", p=P)).then_inc(raw_in, 16)
            sp.wait_ge(pre_added, STEPS * SUB)
            sp.dma_start(bo_row[:, :], rows[LAYERS][bass.ds(idx, 1), :].partition_broadcast(P)).then_inc(brow_in, 16)
            sp.wait_ge(split_lo, 3)
            load_kv(1, 0)
            load_qo(1)
            sp.wait_ge(pre_added, 2 * STEPS * SUB)
            sp.dma_start(bo_row[:, :], rows[1].partition_broadcast(P)).then_inc(brow_in, 16)
            sp.wait_ge(a_free, after_values(1, 0))
            load_kv(1, 1)

        @block.gpsimd
        def _(pool):
            pool.sem_inc(pn_done, CREDIT)
            pool.memset(ident[:, :], 0.0).then_inc(consts, 1)
            pool.memset(neg_half[:, :], -0.5).then_inc(consts, 1)
            pool.wait_ge(consts, 1)
            pool.affine_select(out=ident[:, :], in_=ident[:, :], compare_op=ALU.not_equal, fill=1.0, base=0,
                               pattern=[[-1, P]], channel_multiplier=1).then_inc(consts, 1)
            pool.memset(pn_rem[:, :, :], 0.0).then_inc(consts, 1)
            pool.wait_ge(consts, 4)

            def rstd_of(ln):
                pool.wait_ge(aggr_done, (ln + 1) * SUB)
                pool.tensor_tensor(vareps[:, :], vareps[:, :], meanvar[:, :, 1], ALU.add).then_inc(eps_done, 1)
                pool.wait_ge(eps_done, ln + 1)
                pool.tensor_tensor(rstd[:, :], vareps[:, :], neg_half[:, :], ALU.pow).then_inc(rstd_done, 1)

            def pre_add(ln, n, s):
                if s == 0:
                    pool.wait_ge(xn_ready, (ln + 1) * SUB)
                pool.tensor_tensor(tile_of(n + s), tile_of(n + s), bo_row[:, :], ALU.add).then_inc(pre_added, 1)

            def normalise(unit, unit_before, slot):
                pool.wait_ge(rec_done, unit + 1)
                pool.wait_ge(t_full, unit_before + CREDIT)
                r = rec[:, slot, :, None]
                pool.tensor_tensor(pn_main[:, slot, :, :], pr[:, slot, :, 0:P], r.broadcast_to([P, HPG, P]), ALU.mult)
                pool.tensor_tensor(pn_rem[:, slot, :].rearrange("p (h k) -> p h k", h=HPG)[:, :, 0:REM],
                                   pr[:, slot, :, P:KEYS], r.broadcast_to([P, HPG, REM]), ALU.mult).then_inc(pn_done, 1)

            def prologue(l):
                rstd_of(LN[l])
                pool.wait_ge(bo_scaled, 2 * l + 1)
                for s in range(SUB):
                    pre_add(LN[l], 0, s)

            def units(l, b, step, a, h, kind, a_static):
                ks, draining, carried, _ = schedule(kind)
                if draining:
                    return
                unit0 = (step + l * STEPS) * UNITS
                for k in ks:
                    if k == 1 and kind != "last":
                        rstd_of(step + (LN[l] + 1))
                    normalise(unit0 + k, unit0 + (k - 1 if carried else max(k - 1, 0)), k % 2)
                    if k in (5, 7, 9, 11) and kind != "last":
                        pre_add(step + (LN[l] + 1), (step + 1) * SUB, (k - 5) // 2)

            layer_program(pool, 0, lambda l, b: None, prologue, units)
            rstd_of(LN_DENSE)
            pool.wait_ge(bo_scaled, 2)
            for s in range(SUB):
                pre_add(LN_DENSE, 0, s)
            rstd_of(LN_DENSE + 1)
            for s in range(SUB):
                pre_add(LN_DENSE + 1, SUB, s)
            with pool.Fori(0, STEPS - 2) as it:
                rstd_of(it + (LN_DENSE + 2))
                for s in range(SUB):
                    pre_add(it + (LN_DENSE + 2), (it + 2) * SUB, s)
            layer_program(pool, 1, lambda l, b: None, prologue, units)

        @block.scalar
        def _(act):
            act.sem_inc(ptm_out, CREDIT)
            act.sem_inc(ptr_out, CREDIT)
            act.wait_ge(small_in, 160)
            for l in range(LAYERS):
                act.activation(bk_scaled[:, l, :], bias_cols[:, 3 * l + 1, :], ACT.Copy, scale=SCALE).then_inc(act_prep, 1)
            act.activation(gate[:, :], gate_raw[:, :], ACT.Tanh).then_inc(act_prep, 1)
            act.activation(gum[0:1, 2, :], gum[0:1, 0, :], ACT.Ln).then_inc(pick, 1)
            act.wait_ge(pick, 1)
            act.activation(gum[0:1, 3, :], gum[0:1, 2, :], ACT.Ln, scale=-1.0).then_inc(pick, 1)
            act.wait_ge(pick, 4)
            act.activation(gum[0:1, 5, :], gum[0:1, 4, :], ACT.Exp, accum_out=gum[0:1, 6, 0:1]).then_inc(pick, 1)
            act.wait_ge(pick, 5)
            act.activation(gum[0:1, 6, 1:2], gum[0:1, 6, 0:1], ACT.Ln).then_inc(pick, 1)
            act.wait_ge(zeroed, 2)
            act.wait_ge(act_prep, 3)
            act.wait_ge(prep, 5)

            def upper_of_weights(n, pairs):
                act.wait_ge(raw_in, n)
                for dst, src in pairs:
                    act.activation(dst, src, ACT.Copy).then_inc(split_hi, 1)

            def upper(use, bank, dst, bias=None):
                act.wait_ge(a_full, use + 1)
                if bias is None:
                    act.activation(dst, bank, ACT.Copy).then_inc(hi_done, 1)
                else:
                    act.activation(dst, bank, ACT.Identity, bias=bias).then_inc(hi_done, 1)

            def exps(l, unit0, k, carried):
                act.wait_ge(pn_done, unit0 + ((k - 1 if carried else max(k - 1, 0)) + CREDIT))
                for h in range(HPG):
                    if l == 0:
                        if h == 0:
                            act.wait_ge(max_done, unit0 + (k + 1))
                        src = sc[:, k % 2, h, :]
                    else:
                        if h % 2 == 0:
                            act.wait_ge(max_done, unit0 * 2 + (2 * k + h // 2 + 1 - STEPS * UNITS))
                        src = score_bank(2 * k + h // 2)[:, (h % 2) * KEYS:(h % 2 + 1) * KEYS]
                    i = act.activation(pr[:, k % 2, h, :], src, ACT.Exp, bias=nmax[:, k % 2, h:h + 1],
                                       accum_out=rsum[:, k % 2, h:h + 1])
                    if l == 1 and h % 2:
                        i.then_inc(s_free, 1)
                    if l == 0 and h == HPG - 1:
                        i.then_inc(exp_done, 1)

            def copy_pT(unit0, k):
                g, s = k // SUB, k % SUB
                act.wait_ge(t_full, unit0 + (k + 1 + CREDIT))
                act.activation(pT[:, 0:HPG, s * P:(s + 1) * P], PTM.rearrange("p (h q) -> p h q", h=HPG),
                               ACT.Copy).then_inc(ptm_out, 1)
                if s == SUB - 1:
                    act.activation(pT[:, HPG, :], PTR, ACT.Copy).then_inc(ptr_out, 1)

            def event(l, kind, i, bank, use):
                if kind == "XT":
                    upper(use, bank, xt_hi[:, i, :])
                elif kind == "Q":
                    upper(use, bank, q_hi[:, i, :], bias_cols[:, 3 * l, i:i + 1])
                elif kind == "PV":
                    upper(use, bank, ot_hi[:, i, :], bias_cols[:, 3 * l + 2, i:i + 1])

            def kv(l, b):
                a0, _ = at["kv", l, b]
                for g in range(CH):
                    act.wait_ge(a_full, a0 + g + 1)
                    act.activation(k_tmp[:, g, :], work(a0 + g)[:, 0:KEYS], ACT.Identity, scale=SCALE,
                                   bias=bk_scaled[:, l, g:g + 1]).then_inc(k_tmp_done, 1)
                    act.wait_ge(k_tmp_done, (l * B + b) * CH + g + 1)
                    for h in range(HPG):
                        q = slice(h * HD, (h + 1) * HD)
                        i = act.activation(k_hi[q, g, h * KEYS:(h + 1) * KEYS], k_tmp[q, g, :], ACT.Copy)
                    i.then_inc(hi_done, 1)

            def prologue(l):
                if l:
                    act.wait_ge(a_full, at["prologue", l][0])
                upper_of_weights((80, 224)[l], ((wa_hi[:, :, :], raw_a), (wo_hi[:, :, :], raw_b)))
                a0, _ = at["prologue", l]
                for i in range(PROLOGUE):
                    event(l, "XT" if i < CH else "Q", i % CH, work(a0 + i), a0 + i)

            def units(l, b, step, a, h, kind, a_static):
                unit0 = (step + l * STEPS) * UNITS
                ks, draining, carried, events_of = schedule(kind)
                for k in ks:
                    for name, i, use, _ in events_of(k - 1):
                        event(l, name, i, work(a_static + use), a + use)
                    if not draining:
                        exps(l, unit0, k, carried)
                    if l == 0 and (carried or k >= LAG_T) and k - LAG_T < UNITS:
                        copy_pT(unit0, k - LAG_T)

            layer_program(act, 0, kv, prologue, units)
            upper_of_weights(144, ((wa_hi[:, :, :], raw_a),))
            bufs = (xt_hi, ot_hi)

            def dense_step(a, j, turned):
                for n, (kind, i) in enumerate(DENSE):
                    if kind == "XT" and turned:
                        upper(a + n, work(n), bufs[1 - j][:, i, :])

            a0, _ = at["dense start"]
            for c in range(CH):
                upper(a0 + c, work(c), xt_hi[:, c, :])
            a0, _ = at["dense"]
            with act.Fori(0, (STEPS - 2) // 2) as it:
                for j in range(2):
                    dense_step(it * (2 * DENSE_USES) + (a0 + j * DENSE_USES), j, True)
            kv(1, 0)
            dense_step(at["dense end"][0], 0, True)
            layer_program(act, 1, kv, prologue, units)

        @block.vector
        def _(dve):
            dve.sem_inc(s_free, CREDIT)
            dve.memset(k_hi[:, :, :].bitcast(FP32), 0.0).then_inc(zeroed, 1)
            dve.memset(k_lo[:, :, :].bitcast(FP32), 0.0).then_inc(zeroed, 1)
            dve.memset(v_rem[:, :, :], 0.0).then_inc(prep, 1)
            dve.wait_ge(small_in, 160)
            dve.tensor_reduce(gum[0:1, 7, 0:1], gum[0:1, 1, :], axis=AX.X, op=ALU.max).then_inc(prep, 1)
            dve.tensor_copy(mask_f, mask_i).then_inc(prep, 1)
            dve.wait_ge(prep, 3)
            dve.wait_ge(pick, 2)
            dve.tensor_scalar(gum[0:1, 4, :], gum[0:1, 1, :], gum[0:1, 7, 0:1], None, ALU.subtract).then_inc(pick, 2)
            dve.tensor_scalar(mask_add[:, :, :], mask_f, 0.0, NEG_FILL, ALU.is_equal, ALU.mult).then_inc(prep, 1)
            dve.wait_ge(prep, 4)
            dve.tensor_tensor(mask_add[:, :, :], mask_add[:, :, :], mask_f, ALU.add).then_inc(prep, 1)
            dve.wait_ge(pick, 6)
            dve.tensor_scalar(gum[0:1, 7, :], gum[0:1, 4, :], gum[0:1, 6, 1:2], None, ALU.subtract).then_inc(pick, 1)
            dve.wait_ge(pick, 7)
            dve.tensor_tensor(gum[0:1, 7, :], gum[0:1, 7, :], gum[0:1, 3, :], ALU.subtract).then_inc(pick, 1)
            dve.wait_ge(pick, 8)
            dve.max(gmax[0:1, :], gum[0:1, 7, :]).then_inc(pick, 1)
            dve.wait_ge(pick, 9)
            dve.max_index(gidx[0:1, :], gmax[0:1, :], gum[0:1, 7, :]).then_inc(pick, 1)
            dve.wait_ge(prep, 5)
            dve.wait_ge(act_prep, 3)

            def scale_row(n, gate_col):
                dve.wait_ge(brow_in, 16 * n)
                dve.tensor_scalar(bo_row[:, :], bo_row[:, :], gate[:, gate_col:gate_col + 1], None, ALU.mult)\
                    .then_inc(bo_scaled, 1)

            def lower_of_weights(n, done, pairs):
                dve.wait_ge(raw_in, n)
                for j, (dst, src, hi) in enumerate(pairs):
                    dve.wait_ge(split_hi, done + j + 1)
                    dve.tensor_tensor(dst, src, hi.bitcast(FP32), ALU.subtract).then_inc(split_lo, 1)

            def statistics(n, which):
                for s in which:
                    dve.bn_stats(stats[:, s, :], tile_of(n + s)).then_inc(stats_done, 1)

            def aggregates(ln):
                dve.wait_ge(stats_done, (ln + 1) * SUB)
                dve.memset(vareps[:, :], LN_EPS)
                for s in range(SUB):
                    dve.bn_aggr(meanvar[:, s, :], stats[:, s, :]).then_inc(aggr_done, 1)

            def normalised(ln, n, which):
                for s in which:
                    if s == 0:
                        dve.wait_ge(rstd_done, ln + 1)
                    dve.tensor_scalar(xn[:, s, :], tile_of(n + s), meanvar[:, s, 0:1], rstd[:, s:s + 1],
                                      ALU.subtract, ALU.mult).then_inc(xn_ready, 1)

            def layer_norm(ln, n):
                statistics(n, range(SUB))
                aggregates(ln)
                normalised(ln, n, range(SUB))

            def lower(hi_count, bank, dst, hi, bias=None):
                dve.wait_ge(hi_done, hi_count)
                if bias is None:
                    dve.tensor_tensor(dst, bank, hi.bitcast(FP32), ALU.subtract).then_inc(a_free, 1)
                else:
                    dve.scalar_tensor_tensor(out=dst, in0=bank, scalar=bias, in1=hi.bitcast(FP32),
                                             op0=ALU.add, op1=ALU.subtract).then_inc(a_free, 1)

            def residual(use, bank, n, gate_col, pre):
                dve.wait_ge(a_full, use + 1)
                dve.wait_ge(pre_added, pre)
                dve.scalar_tensor_tensor(out=tile_of(n), in0=bank, scalar=gate[:, gate_col:gate_col + 1],
                                         in1=tile_of(n), op0=ALU.mult, op1=ALU.add).then_inc(a_free, 1)

            def maxima(l, b, unit0, k):
                for half in range(2):
                    v = 2 * k + half
                    dve.wait_ge(s_full, unit0 * 2 + (v + 1))
                    bank = score_bank(v).rearrange("p (h k) -> p h k", h=2)
                    if l == 0:
                        dve.tensor_scalar(sc[:, k % 2, 2 * half:2 * half + 2, :], bank, CLAMP, -CLAMP,
                                          ALU.min, ALU.max).then_inc(s_free, 1)
                    else:
                        dve.tensor_reduce(nmax[:, k % 2, 2 * half:2 * half + 2], bank, axis=AX.X,
                                          op=ALU.max, negate=True).then_inc(max_done, 1)
                if l == 0:
                    dve.wait_ge(s_free, unit0 * 2 + (2 * k + 2 + CREDIT))
                    dve.memset(wait_pad[:, :], 0.0)
                    for h in range(HPG):
                        i = dve.tensor_tensor_reduce(out=sc[:, k % 2, h, :], in0=sc[:, k % 2, h, :],
                                                     in1=mask_add[:, b, :], scale=1.0, scalar=-3.0e38,
                                                     op0=ALU.add, op1=ALU.max, accum_out=smax[:, k % 2, h:h + 1])
                    i.then_inc(masked, 1)
                    dve.wait_ge(masked, unit0 + (k + 1))
                    dve.tensor_scalar(nmax[:, k % 2, :], smax[:, k % 2, :], -1.0, None, ALU.mult).then_inc(max_done, 1)

            def reciprocals(l, unit0, k):
                if l == 0:
                    dve.wait_ge(exp_done, unit0 + (k + 1))
                else:
                    dve.wait_ge(s_free, unit0 * 2 + (2 * k + 2 + CREDIT))
                dve.reciprocal(rec[:, k % 2, :], rsum[:, k % 2, :]).then_inc(rec_done, 1)

            def copy_pT(unit0, k):
                g, s = k // SUB, k % SUB
                dve.wait_ge(t_full, unit0 + (k + 1 + CREDIT))
                dve.tensor_copy(pT[:, 0:HPG, s * P:(s + 1) * P],
                                PTM.rearrange("p (h q) -> p h q", h=HPG)).then_inc(ptm_out, 1)
                if s == SUB - 1:
                    dve.tensor_copy(pT[:, HPG, :], PTR).then_inc(ptr_out, 1)

            def event(l, kind, i, bank, use, hi_count, step):
                if kind == "XT":
                    lower(hi_count, work(bank), xt_lo[:, i, :], xt_hi[:, i, :])
                elif kind == "Q":
                    lower(hi_count, work(bank), q_lo[:, i, :], q_hi[:, i, :], bias_cols[:, 3 * l, i:i + 1])
                elif kind == "PV":
                    lower(hi_count, work(bank), ot_lo[:, i, :], ot_hi[:, i, :], bias_cols[:, 3 * l + 2, i:i + 1])
                else:
                    residual(use, work(bank), step * SUB + (i - SUB), 2 * l, step * SUB + ((LN[l] - 1) * SUB + i + 1))

            def kv(l, b):
                a0, h0 = at["kv", l, b]
                for g in range(CH):
                    dve.wait_ge(hi_done, h0 + g + 1)
                    for h in range(HPG):
                        q = slice(h * HD, (h + 1) * HD)
                        blk = slice(h * KEYS, (h + 1) * KEYS)
                        i = dve.tensor_tensor(k_lo[q, g, blk], k_tmp[q, g, :], k_hi[q, g, blk].bitcast(FP32), ALU.subtract)
                    i.then_inc(a_free, 1)
                dve.wait_ge(a_full, a0 + CH + 1)
                dve.tensor_copy(v_main[:, :], work(a0 + CH)).then_inc(a_free, 1)
                dve.wait_ge(a_full, a0 + CH + 2)
                for h in range(HPG):
                    q = slice(h * HD, h * HD + REM)
                    i = dve.tensor_copy(v_rem[q, :, h * HD:(h + 1) * HD],
                                        work(a0 + CH + 1)[q, 0:P].rearrange("p (g d) -> p g d", g=CH))
                i.then_inc(a_free, 1)

            def prologue(l):
                scale_row(2 * l + 1, 2 * l)
                if l == 0:
                    dve.wait_ge(x_in0, 16)
                    layer_norm(LN[l], 0)
                lower_of_weights((80, 224)[l], 3 * l, ((wa_lo[:, :, :], raw_a, wa_hi[:, :, :]),
                                                      (wo_lo[:, :, :], raw_b, wo_hi[:, :, :])))
                a0, h0 = at["prologue", l]
                for i in range(PROLOGUE):
                    event(l, "XT" if i < CH else "Q", i % CH, a0 + i, a0 + i, h0 + i + 1, 0)

            def units(l, b, step, a, h, kind, a_static):
                unit0 = (step + l * STEPS) * UNITS
                ks, draining, carried, events_of = schedule(kind)
                ln, n_next = step + (LN[l] + 1), (step + 1) * SUB
                for k in ks:
                    if not draining:
                        maxima(l, b, unit0, k)
                    if (carried or k >= 1) and k - 1 < UNITS:
                        reciprocals(l, unit0, k - 1)
                    for name, i, use, hi in events_of(k - 1):
                        event(l, name, i, a_static + use, a + use, h + (hi + 1), step + 1 if draining else step)
                    if l == 1 and (carried or k >= LAG_T) and k - LAG_T < UNITS:
                        copy_pT(unit0, k - LAG_T)
                    if kind in ("first", "full"):
                        if k < 2:
                            statistics(n_next, (2 * k, 2 * k + 1))
                        if k == 1:
                            aggregates(ln)
                        if k in (2, 3):
                            normalised(ln, n_next, (2 * k - 4, 2 * k - 3))
                if (l, kind, b) == (0, "first", 0):
                    dve.wait_ge(x_in1, 16)

            layer_program(dve, 0, kv, prologue, units)
            dve.wait_ge(a_free, at["dense start"][0])
            layer_norm(LN_DENSE, 0)
            lower_of_weights(144, 2, ((wa_lo[:, :, :], raw_a, wa_hi[:, :, :]),))
            scale_row(2, 1)
            hi_bufs, lo_bufs = (xt_hi, ot_hi), (xt_lo, ot_lo)
            a0, h0 = at["dense start"]
            for c in range(CH):
                lower(h0 + c + 1, work(c), xt_lo[:, c, :], xt_hi[:, c, :])
            layer_norm(LN_DENSE + 1, SUB)

            def dense_step(step, a, h, j, turned, norm):
                hi = 0
                for n, (kind, i) in enumerate(DENSE if turned else [e for e in DENSE if e[0] == "OUT"]):
                    if kind == "XT":
                        hi += 1
                        lower(h + hi, work(n), lo_bufs[1 - j][:, i, :], hi_bufs[1 - j][:, i, :])
                    else:
                        residual(a + n, work(n), step * SUB + i, 1, step * SUB + (LN_DENSE * SUB + i + 1))
                    if norm:
                        ln, tile = norm
                        if (kind, i) == ("XT", 3):
                            statistics(tile, range(SUB))
                        elif (kind, i) == ("OUT", 2):
                            aggregates(ln)
                        elif (kind, i) == ("OUT", 3):
                            normalised(ln, tile, range(SUB))

            a0, h0 = at["dense"]
            with dve.Fori(0, (STEPS - 2) // 2) as it:
                for j in range(2):
                    step = it * 2 + j
                    dense_step(step, it * (2 * DENSE_USES) + (a0 + j * DENSE_USES), it * (2 * CH) + (h0 + j * CH), j, True,
                               (step + (LN_DENSE + 2), (step + 2) * SUB))
            kv(1, 0)
            a0, h0 = at["dense end"]
            dense_step(STEPS - 2, a0, h0, 0, True, (LN[1], 0))
            dense_step(STEPS - 1, a0 + DENSE_USES, h0 + CH, 1, False, None)
            layer_program(dve, 1, kv, prologue, units)

        @block.tensor
        def _(pe):
            pe.sem_inc(t_full, CREDIT)
            pe.wait_ge(consts, 4)

            def three_passes(out, pairs):
                n = 3 * len(pairs)
                j = 0
                for (w_hi, w_lo), (m_hi, m_lo) in pairs:
                    for w, m in ((w_hi, m_hi), (w_hi, m_lo), (w_lo, m_hi)):
                        last = nc.tensor.matmul(out, w, m, start=(j == 0), stop=(j == n - 1))
                        j += 1
                return last

            def transposes(bank, c, ln):
                for s in range(SUB):
                    if c == 0 and s == 0:
                        pe.wait_ge(xn_ready, (ln + 1) * SUB)
                    last = nc.tensor.transpose(work(bank)[:, s * P:(s + 1) * P], xn[:, s, c * P:(c + 1) * P], ident[:, :])
                last.then_inc(a_full, 1)

            def queries(bank, m):
                ms = slice(m * P, (m + 1) * P)
                three_passes(work(bank), [((wa_hi[:, c, ms], wa_lo[:, c, ms]), (xt_hi[:, c, :], xt_lo[:, c, :]))
                                          for c in range(CH)]).then_inc(a_full, 1)

            def out_rows(bank, s, i_hi, i_lo, w_hi, w_lo):
                q = slice(s * P, (s + 1) * P)
                three_passes(work(bank), [((i_hi[:, c, q], i_lo[:, c, q]), (w_hi[:, c, :], w_lo[:, c, :]))
                                          for c in range(CH)]).then_inc(a_full, 1)

            def values(bank, g):
                nc.tensor.matmul(work(bank), v_rem[:, g, :], pT[:, HPG, :], start=True, stop=False, skip_group_check=True)
                for h in range(HPG):
                    last = nc.tensor.matmul(work(bank)[h * HD:(h + 1) * HD, :],
                                            v_main[:, (g * HPG + h) * HD:(g * HPG + h + 1) * HD], pT[:, h, :],
                                            start=False, stop=(h == HPG - 1), skip_group_check=True)
                last.then_inc(a_full, 1)

            def kv(l, b):
                a0, _ = at["kv", l, b]
                pe.wait_ge(raw_in, (48, 128, 192, 272)[l * B + b])
                for g in range(CH):
                    if a0 + g >= 2:
                        pe.wait_ge(a_free, a0 + g - 1)
                    for c in range(CH):
                        last = nc.tensor.matmul(work(a0 + g)[:, 0:KEYS], raw_a[:, c, g * P:(g + 1) * P],
                                                ctx_t[:, c, :], start=(c == 0), stop=(c == CH - 1))
                    last.then_inc(a_full, 1)
                pe.wait_ge(a_free, a0 + CH - 1)
                for c in range(CH):
                    last = nc.tensor.matmul(work(a0 + CH), ctx_t[:, c, 0:P], raw_b[:, c, :],
                                            start=(c == 0), stop=(c == CH - 1))
                last.then_inc(a_full, 1)
                pe.wait_ge(a_free, a0 + CH)
                for h in range(HPG):
                    for c in range(CH):
                        last = nc.tensor.matmul(
                            work(a0 + CH + 1)[h * HD:h * HD + REM, 0:P], ctx_t[:, c, P:KEYS],
                            raw_b[:, c, :].rearrange("p (g h d) -> p g h d", g=CH, h=HPG)[:, :, h, :],
                            start=(c == 0), stop=(c == CH - 1))
                last.then_inc(a_full, 1)

            def prologue(l):
                a0, _ = at["prologue", l]
                for c in range(CH):
                    pe.wait_ge(a_free, a0 + c - 1)
                    transposes(c, c, LN[l])
                pe.wait_ge(a_free, a0 + CH)
                pe.wait_ge(split_lo, 3 * l + 1)
                for m in range(CH):
                    pe.wait_ge(a_free, a0 + CH + max(m - 1, 0))
                    queries(m, m)

            def units(l, b, step, a, h, kind, a_static):
                unit0 = (step + l * STEPS) * UNITS
                group0 = (step + l * STEPS) * CH
                ks, draining, carried, events_of = schedule(kind)
                if (kind, b) == ("first", 0):
                    pe.wait_ge(split_lo, 3 * l + 2)
                for k in ks:
                    if not draining:
                        g, s = k // SUB, k % SUB
                        q = slice(s * P, (s + 1) * P)
                        if k == 0:
                            pe.wait_ge(a_free, a - 2 if carried else a)
                        for half in range(2):
                            v = 2 * k + half
                            pe.wait_ge(s_free, unit0 * 2 + ((v - 3 if carried else max(v - 3, 0)) + CREDIT))
                            cs = slice(half * HALF, (half + 1) * HALF)
                            three_passes(score_bank(v), [((q_hi[:, g, q], q_lo[:, g, q]),
                                                          (k_hi[:, g, cs], k_lo[:, g, cs]))]).then_inc(s_full, 1)
                    for name, i, use, _ in events_of(k):
                        pe.wait_ge(a_free, a + (use if (name, i) == ("WO", 0) else use - 1))
                        bank = a_static + use
                        if name == "WO":
                            out_rows(bank, i, ot_hi, ot_lo, wo_hi, wo_lo)
                        elif name == "XT":
                            transposes(bank, i, step + (LN[l] + 1))
                        elif name == "Q":
                            queries(bank, i)
                        else:
                            back = 1 if i == CH - 1 and not draining else 0
                            pe.wait_ge(ptm_out, unit0 + ((i + 1) * SUB - back * UNITS + CREDIT))
                            pe.wait_ge(ptr_out, group0 + (i + 1 - back * CH + CREDIT))
                            values(bank, i)
                    t = k - LAG_T
                    if (carried or t >= 0) and t < UNITS:
                        pe.wait_ge(pn_done, unit0 + (t + 1 + CREDIT))
                        pe.wait_ge(ptm_out, unit0 + (t + CREDIT))
                        s = t % SUB
                        if s == 0:
                            pe.wait_ge(ptr_out, group0 + (t // SUB + CREDIT))
                        nc.tensor.transpose(PTR[:, s * P:(s + 1) * P], pn_rem[:, t % 2, :], ident[:, :])
                        for h in range(HPG):
                            i = nc.tensor.transpose(PTM[:, h * P:(h + 1) * P], pn_main[:, t % 2, h, :], ident[:, :])
                        i.then_inc(t_full, 1)

            layer_program(pe, 0, kv, prologue, units)
            a0, _ = at["dense start"]
            for c in range(CH):
                pe.wait_ge(a_free, a0 + c - 1)
                transposes(c, c, LN_DENSE)
            pe.wait_ge(split_lo, 3)
            hi_bufs, lo_bufs = (xt_hi, ot_hi), (xt_lo, ot_lo)

            def dense_step(step, a, j, turned):
                for n, (kind, i) in enumerate(DENSE if turned else [e for e in DENSE if e[0] == "OUT"]):
                    pe.wait_ge(a_free, a + (0 if n == 0 else n - 1))
                    if kind == "XT":
                        transposes(n, i, step + (LN_DENSE + 1))
                    else:
                        out_rows(n, i, hi_bufs[j], lo_bufs[j], wa_hi, wa_lo)

            a0, _ = at["dense"]
            with pe.Fori(0, (STEPS - 2) // 2) as it:
                for j in range(2):
                    dense_step(it * 2 + j, it * (2 * DENSE_USES) + (a0 + j * DENSE_USES), j, True)
            kv(1, 0)
            a0, _ = at["dense end"]
            dense_step(STEPS - 2, a0, 0, True)
            dense_step(STEPS - 1, a0 + DENSE_USES, 1, False)
            layer_program(pe, 1, kv, prologue, units)


def quantised_ffn(nc, w1, b1_cols, w2, b2_row, gates, out, X, ident):
    PIECES = 2 * FC
    HB = 4
    ctx = ExitStack()
    with ctx:
        def sb(name, shape, dt):
            return ctx.enter_context(nc.sbuf_tensor(name, shape, dt))

        def sem(name):
            return ctx.enter_context(nc.semaphore(name))

        xq_t = sb("xq_t", [P, CH, B * S], BF16)
        w1_t = sb("w1_t", [P, CH, F], BF16)
        w2_t = sb("w2_t", [P, FC, D], BF16)
        raw = sb("raw", [P, FC, D], FP32)
        h_relu = sb("h_relu", [P, HB, TOK], FP32)
        rounded = sb("rounded", [P, 2, D], BF16)
        diag = sb("diag", [P, P], FP32)
        ones = sb("ones", [P, P], FP32)
        ident_b = sb("ident_b", [P, P], BF16)
        magic = sb("magic", [P, 1], FP32)
        s_w = sb("s_w", [P, 2, FC], FP32)
        r_w = sb("r_w", [P, 2, FC], FP32)
        stats = sb("stats2", [P, TILES, 6], FP32)
        meanvar = sb("meanvar2", [P, TILES, 2], FP32)
        vareps = sb("vareps2", [P, TILES], FP32)
        rstd = sb("rstd2", [P, TILES], FP32)
        neg_half = sb("neg_half2", [P, TILES], FP32)
        row_max = sb("row_max", [P, TILES], FP32)
        x_bias = sb("x_bias", [P, TILES], FP32)
        x_scale = sb("x_scale", [P, TILES], FP32)
        h_max = sb("h_max", [P, STEPS, FC], FP32)
        col = sb("col", [P, 12, FC], FP32)
        one = sb("one", [P, 16], FP32)
        b1_c = sb("b1_c", [P, FC], FP32)
        b2_r = sb("b2_r", [P, D], FP32)
        s2_r = sb("s2_r", [P, D], FP32)
        row_tmp = sb("row_tmp", [P, 3, D], FP32)
        gate_raw = sb("gate_raw2", [P, 4], FP32)
        gate = sb("gate2", [P, 4], FP32)
        ps = ctx.enter_context(nc.psum_tensor("ps2", [P, 8, 512], FP32))
        consts = sem("q_consts")
        w1_in = sem("q_w1_in")
        w2_in = sem("q_w2_in")
        small_in = sem("q_small")
        vec = sem("q_vec")
        w_scaled = sem("q_ws")
        w_magic = sem("q_wm")
        w_rounded = sem("q_wr")
        w_turned = sem("q_wt")
        w_out = sem("q_wo")
        gate_done = sem("q_gate")
        diag_done = sem("q_diag")
        srow_full = sem("q_srow")
        aggr_done = sem("q_aggr")
        rstd_done = sem("q_rstd")
        part_max = sem("q_pmax")
        global_max = sem("q_gmax")
        x_scaled = sem("q_xs")
        x_relu = sem("q_xr")
        x_rounded = sem("q_xi")
        x_turned = sem("q_xt")
        x_out = sem("q_xo")
        m_full = sem("q_mf")
        m_free = sem("q_mr")
        h_scaled = sem("q_hs")
        rows_done = sem("q_rows")
        h_full = sem("q_hf")
        h_relued = sem("q_hr")
        h_rounded = sem("q_hi")
        o_full = sem("q_of")
        o_scaled = sem("q_os")
        o_done = sem("q_od")
        pre_added = sem("q_pre")
        stored = sem("q_st")
        block = ctx.enter_context(nc.Block())
        h_q = raw[:, 0:FC // 2, :].rearrange("p f d -> p (f d)").bitcast(BF16).rearrange("p (f n) -> p f n", f=FC)

        def psum_bf16(bank):
            return ps[:, bank, 0:TOK // 2].bitcast(BF16)

        def tile_of(n):
            return flat(X[:, bass.ds(n, 1), :])

        @block.sync
        def _(sp):
            sp.dma_start(raw[:, :, :], w1.rearrange("(f p) d -> p f d", p=P)).then_inc(w1_in, 16)
            sp.dma_start(b1_c[:, :], b1_cols).then_inc(small_in, 16)
            sp.dma_start(b2_r[:, :], b2_row.partition_broadcast(P)).then_inc(small_in, 16)
            sp.dma_start(gate_raw[:, :], gates.partition_broadcast(P)).then_inc(small_in, 16)
            sp.wait_ge(w_magic, FC)
            sp.dma_start(raw[:, :, :].rearrange("p (c r) d -> p c (r d)", c=CH),
                         w2.rearrange("(c p) f -> p c f", p=P)).then_inc(w2_in, 16)
            ov = out.rearrange("(t p) n -> p t n", p=P)
            with sp.Fori(0, STEPS) as it:
                sp.wait_ge(o_done, it * SUB + SUB)
                sp.dma_start(ov[:, bass.ds(it * SUB, SUB), :], X[:, bass.ds(it * SUB, SUB), :]).then_inc(stored, 16)
            sp.wait_ge(stored, 16 * STEPS)

        @block.gpsimd
        def _(pool):
            pool.memset(ones[:, :], 1.0).then_inc(consts, 1)
            pool.memset(magic[:, :], MAGIC).then_inc(consts, 1)
            pool.memset(neg_half[:, :], -0.5).then_inc(consts, 1)
            pool.tensor_copy(ident_b[:, :], ident[:, :]).then_inc(consts, 1)
            pool.wait_ge(consts, 3)
            pool.wait_ge(aggr_done, 1)
            pool.tensor_scalar(vareps[:, :], meanvar[:, :, 1], LN_EPS, None, ALU.add).then_inc(rstd_done, 1)
            pool.wait_ge(rstd_done, 1)
            pool.tensor_tensor(rstd[:, :], vareps[:, :], neg_half[:, :], ALU.pow).then_inc(rstd_done, 1)
            pool.wait_ge(rows_done, 2)
            with pool.Fori(0, TILES) as n:
                pool.tensor_tensor(tile_of(n), tile_of(n), b2_r[:, :], ALU.add).then_inc(pre_added, 1)

        @block.scalar
        def _(act):
            act.sem_inc(h_relued, CREDIT)
            act.wait_ge(small_in, 48)
            act.activation(gate[:, :], gate_raw[:, :], ACT.Tanh).then_inc(gate_done, 1)
            act.wait_ge(consts, 4)

            def copy_piece(p):
                act.wait_ge(w_turned, p + 1)
                src = psum_bf16(p % 2).rearrange("p (i q) -> p i q", i=4)
                if p < FC:
                    dst = w1_t[:, :, p * P:(p + 1) * P]
                else:
                    c, r = (p - FC) // 4, (p - FC) % 4
                    dst = w2_t[:, 4 * r:4 * r + 4, c * P:(c + 1) * P]
                act.activation(dst, src, ACT.Copy).then_inc(w_out, 1)

            for p in range(PIECES):
                if p % FC == 0:
                    act.wait_ge(w_scaled, p // FC + 1)
                c = p if p < FC else (p - FC) // 4
                if p >= 2:
                    act.wait_ge(w_rounded, p - 1)
                act.activation(h_relu[:, p % 2, :], raw[:, p % FC, :], ACT.Identity, scale=r_w[:, p // FC, c:c + 1],
                               bias=magic[:, :]).then_inc(w_magic, 1)
                if p >= 2:
                    copy_piece(p - 2)
            copy_piece(PIECES - 2)
            copy_piece(PIECES - 1)
            act.wait_ge(x_scaled, 1)
            act.wait_ge(w_rounded, PIECES)
            for n in range(TILES):
                if n >= 2:
                    act.wait_ge(x_rounded, n - 1)
                act.activation(h_relu[:, n % 2, :], X[:, n, :], ACT.Relu, scale=x_scale[:, n:n + 1],
                               bias=x_bias[:, n:n + 1]).then_inc(x_relu, 1)
            act.wait_ge(h_scaled, 1)
            with act.Fori(0, STEPS) as it:
                for f in range(FC):
                    act.wait_ge(h_full, it * FC + (f + 1))
                    act.wait_ge(h_rounded, it * FC + (max(f + 1 - HB, 0) + CREDIT))
                    act.activation(h_relu[:, f % HB, :], ps[:, f % HB, :], ACT.Relu, scale=col[:, 8, f:f + 1],
                                   bias=col[:, 9, f:f + 1]).then_inc(h_relued, 1)

        @block.vector
        def _(dve):
            steps = [0]

            def step(i):
                steps[0] += 1
                i.then_inc(vec, 1)
                dve.wait_ge(vec, steps[0])

            def magic_round(dst, v, tmp, keep):
                step(dve.tensor_scalar(tmp, v, MAGIC, -MAGIC, ALU.add, ALU.add))
                step(dve.tensor_tensor(keep, v, v, ALU.mult))
                step(dve.tensor_scalar(keep, keep, 2.0**44, None, ALU.is_lt))
                step(dve.tensor_tensor(tmp, tmp, v, ALU.subtract))
                step(dve.tensor_tensor(tmp, tmp, keep, ALU.mult))
                step(dve.tensor_tensor(dst, v, tmp, ALU.add))

            for buffers_free in (h_rounded, m_free, o_scaled):
                dve.sem_inc(buffers_free, CREDIT)
            for n in range(TILES):
                dve.bn_stats(stats[:, n, :], X[:, n, :])
            step(dve.tensor_reduce(row_max[:, :], X[:, :, :], axis=AX.X, op=ALU.max))
            for n in range(TILES):
                i = dve.bn_aggr(meanvar[:, n, :], stats[:, n, :])
            i.then_inc(aggr_done, 1)
            for j, arrived in enumerate((w1_in, w2_in)):
                n = FC if j == 0 else CH
                dve.wait_ge(arrived, 16)
                src = raw[:, :, :] if j == 0 else raw[:, :, :].rearrange("p (c r) d -> p c (r d)", c=CH)
                step(dve.tensor_reduce(s_w[:, j, 0:n], src, axis=AX.X, op=ALU.max, apply_absolute_value=True))
                step(dve.tensor_scalar(s_w[:, j, 0:n], s_w[:, j, 0:n], Q_EPS, 1.0 / 127.0, ALU.max, ALU.mult))
                dve.reciprocal(r_w[:, j, 0:n], s_w[:, j, 0:n]).then_inc(w_scaled, 1)
                for p in range(j * FC, (j + 1) * FC):
                    dve.wait_ge(w_magic, p + 1)
                    if p >= 2:
                        dve.wait_ge(w_turned, p - 1)
                    dve.tensor_scalar(rounded[:, p % 2, :], h_relu[:, p % 2, :], -MAGIC, None, ALU.add).then_inc(w_rounded, 1)

            def maximum_of_partitions(j):
                dve.tensor_scalar(diag[:, :], ident[:, :], one[:, 2 * j:2 * j + 1], None, ALU.mult).then_inc(part_max, 1)
                dve.wait_ge(global_max, j + 1)
                step(dve.tensor_reduce(one[:, 2 * j + 1:2 * j + 2], ps[:, 6, 0:P], axis=AX.X, op=ALU.max))

            dve.wait_ge(rstd_done, 2)
            step(dve.tensor_tensor(row_max[:, :], row_max[:, :], meanvar[:, :, 0], ALU.subtract))
            step(dve.tensor_tensor(row_max[:, :], row_max[:, :], rstd[:, :], ALU.mult))
            step(dve.tensor_reduce(one[:, 0:1], row_max[:, :], axis=AX.X, op=ALU.max))
            maximum_of_partitions(0)
            step(dve.tensor_scalar(one[:, 4:5], one[:, 1:2], Q_EPS, 1.0 / 255.0, ALU.max, ALU.mult))
            step(dve.reciprocal(one[:, 5:6], one[:, 4:5]))
            step(dve.tensor_scalar(x_scale[:, :], rstd[:, :], one[:, 5:6], None, ALU.mult))
            step(dve.tensor_scalar(x_bias[:, :], meanvar[:, :, 0], -1.0, None, ALU.mult))
            dve.tensor_tensor(x_bias[:, :], x_bias[:, :], x_scale[:, :], ALU.mult).then_inc(x_scaled, 1)
            for c in range(CH):
                if c:
                    dve.wait_ge(srow_full, c)
                dve.tensor_scalar(diag[:, :], ident[:, :], s_w[:, 1, c:c + 1], None, ALU.mult).then_inc(diag_done, 1)
            dve.wait_ge(srow_full, CH)
            dve.tensor_copy(s2_r[:, :], ps[:, 7, :]).then_inc(vec, 1)
            steps[0] += 1

            def copy_x(n):
                dve.wait_ge(x_turned, n + 1)
                dve.tensor_copy(xq_t[:, :, n * P:(n + 1) * P],
                                psum_bf16(2 + n % 2).rearrange("p (i q) -> p i q", i=4)).then_inc(x_out, 1)

            for n in range(TILES):
                dve.wait_ge(x_relu, n + 1)
                if n >= 2:
                    dve.wait_ge(x_turned, n - 1)
                dve.tensor_scalar(rounded[:, n % 2, :], h_relu[:, n % 2, :], MAGIC, -MAGIC, ALU.add, ALU.add).then_inc(x_rounded, 1)
                if n >= 1:
                    copy_x(n - 1)
            copy_x(TILES - 1)
            sc1, bq1, v1, t1, k1 = (col[:, j, :] for j in range(5))
            dve.wait_ge(small_in, 48)
            step(dve.tensor_scalar(sc1, s_w[:, 0, :], one[:, 4:5], None, ALU.mult))
            step(dve.reciprocal(v1, sc1))
            step(dve.tensor_tensor(v1, v1, b1_c[:, :], ALU.mult))
            magic_round(bq1, v1, t1, k1)
            step(dve.tensor_tensor(bq1, bq1, sc1, ALU.mult))
            with dve.Fori(0, STEPS) as it:
                for f in range(0, FC, 2):
                    dve.wait_ge(m_full, it * (FC // 2) + (f // 2 + 1))
                    dve.tensor_reduce(flat(h_max[:, bass.ds(it, 1), f:f + 2]), ps[:, f % 8:f % 8 + 2, :], axis=AX.X,
                                      op=ALU.max).then_inc(m_free, 1)
            dve.wait_ge(m_free, STEPS * FC // 2 + CREDIT)
            step(dve.tensor_reduce(col[:, 5, :], h_max[:, :, :].rearrange("p s f -> p f s"), axis=AX.X, op=ALU.max))
            step(dve.tensor_tensor(col[:, 5, :], col[:, 5, :], sc1, ALU.mult))
            step(dve.tensor_tensor(col[:, 5, :], col[:, 5, :], bq1, ALU.add))
            step(dve.tensor_scalar(col[:, 5, :], col[:, 5, :], 0.0, None, ALU.max))
            step(dve.tensor_reduce(one[:, 2:3], col[:, 5, :], axis=AX.X, op=ALU.max))
            maximum_of_partitions(1)
            step(dve.tensor_scalar(one[:, 6:7], one[:, 3:4], Q_EPS, 1.0 / 255.0, ALU.max, ALU.mult))
            step(dve.reciprocal(one[:, 7:8], one[:, 6:7]))
            step(dve.tensor_scalar(col[:, 8, :], sc1, one[:, 7:8], None, ALU.mult))
            dve.tensor_scalar(col[:, 9, :], bq1, one[:, 7:8], None, ALU.mult).then_inc(h_scaled, 1)
            dve.wait_ge(gate_done, 1)
            v2, t2, k2 = (row_tmp[:, j, :] for j in range(3))
            step(dve.tensor_scalar(s2_r[:, :], s2_r[:, :], one[:, 6:7], None, ALU.mult))
            step(dve.reciprocal(v2, s2_r[:, :]))
            step(dve.tensor_tensor(v2, v2, b2_r[:, :], ALU.mult))
            magic_round(v2, v2, t2, k2)
            step(dve.tensor_tensor(v2, v2, s2_r[:, :], ALU.mult))
            dve.tensor_scalar(b2_r[:, :], v2, gate[:, 3:4], None, ALU.mult).then_inc(rows_done, 1)
            dve.tensor_scalar(s2_r[:, :], s2_r[:, :], gate[:, 3:4], None, ALU.mult).then_inc(rows_done, 1)
            dve.wait_ge(rows_done, 2)
            with dve.Fori(0, STEPS) as it:
                for f in range(FC):
                    dve.wait_ge(h_relued, it * FC + (f + 1 + CREDIT))
                    if f == 0:
                        dve.wait_ge(o_full, it * SUB + CREDIT)
                    dve.tensor_scalar(h_q[:, f, :], h_relu[:, f % HB, :], MAGIC, -MAGIC, ALU.add, ALU.add).then_inc(h_rounded, 1)
                for s in range(SUB):
                    dve.wait_ge(o_full, it * SUB + (s + 1 + CREDIT))
                    dve.wait_ge(pre_added, it * SUB + (s + 1))
                    if s >= 2:
                        dve.wait_ge(o_done, it * SUB + (s - 1))
                    dve.tensor_tensor(row_tmp[:, s % 2, :], ps[:, 4 + s % 2, :], s2_r[:, :], ALU.mult).then_inc(o_scaled, 1)
                    dve.wait_ge(o_scaled, it * SUB + (s + 1 + CREDIT))
                    n = it * SUB + s
                    dve.tensor_tensor(tile_of(n), tile_of(n), row_tmp[:, s % 2, :], ALU.add).then_inc(o_done, 1)

        @block.tensor
        def _(pe):
            pe.sem_inc(o_full, CREDIT)
            pe.wait_ge(consts, 4)
            for p in range(PIECES):
                pe.wait_ge(w_rounded, p + 1)
                if p >= 2:
                    pe.wait_ge(w_out, p - 1)
                for i in range(4):
                    last = nc.tensor.transpose(psum_bf16(p % 2)[:, i * P:(i + 1) * P], rounded[:, p % 2, i * P:(i + 1) * P],
                                               ident_b[:, :])
                last.then_inc(w_turned, 1)

            def spread_maxima(j):
                pe.wait_ge(part_max, j + 1)
                nc.tensor.matmul(ps[:, 6, 0:P], ones[:, :], diag[:, :], start=True, stop=True).then_inc(global_max, 1)

            spread_maxima(0)
            for c in range(CH):
                pe.wait_ge(diag_done, c + 1)
                nc.tensor.matmul(ps[:, 7, c * P:(c + 1) * P], ones[:, :], diag[:, :], start=True, stop=True)\
                    .then_inc(srow_full, 1)
            for n in range(TILES):
                pe.wait_ge(x_rounded, n + 1)
                if n >= 2:
                    pe.wait_ge(x_out, n - 1)
                for i in range(4):
                    last = nc.tensor.transpose(psum_bf16(2 + n % 2)[:, i * P:(i + 1) * P],
                                               rounded[:, n % 2, i * P:(i + 1) * P], ident_b[:, :])
                last.then_inc(x_turned, 1)

            def h_chunk(bank, it, f):
                for c in range(CH):
                    last = nc.tensor.matmul(ps[:, bank, :], w1_t[:, c, f * P:(f + 1) * P],
                                            xq_t[:, c, bass.ds(it * TOK, TOK)], start=(c == 0), stop=(c == CH - 1))
                return last

            pe.wait_ge(x_out, TILES)
            pe.wait_ge(w_out, PIECES)
            with pe.Fori(0, STEPS) as it:
                for f in range(FC):
                    if f % 2 == 0:
                        pe.wait_ge(m_free, it * (FC // 2) + (max(f // 2 - 3, 0) + CREDIT))
                    last = h_chunk(f % 8, it, f)
                    if f % 2:
                        last.then_inc(m_full, 1)
            pe.wait_ge(m_free, STEPS * FC // 2 + CREDIT)
            spread_maxima(1)
            with pe.Fori(0, STEPS) as it:
                for f in range(FC):
                    pe.wait_ge(h_relued, it * FC + (max(f + 1 - HB, 0) + CREDIT))
                    h_chunk(f % HB, it, f).then_inc(h_full, 1)
                for s in range(SUB):
                    pe.wait_ge(o_scaled, it * SUB + (max(s - 1, 0) + CREDIT))
                    for f in range(FC):
                        if s == 0:
                            pe.wait_ge(h_rounded, it * FC + (f + 1 + CREDIT))
                        last = nc.tensor.matmul(ps[:, 4 + s % 2, :], h_q[:, f, s * P:(s + 1) * P], w2_t[:, f, :],
                                                start=(f == 0), stop=(f == FC - 1))
                    last.then_inc(o_full, 1)


def flamingo(nc, x, ctxT, mask, gates, cols, rows, weights, W0, logits, u, w1, b1_cols, w2, b2_row, out):
    ctx = ExitStack()
    with ctx:
        def sb(name, shape, dt):
            return ctx.enter_context(nc.sbuf_tensor(name, shape, dt))

        def sem(name):
            return ctx.enter_context(nc.semaphore(name))

        X = sb("X", [P, TILES, D], FP32)
        ident = sb("ident", [P, P], FP32)
        attention_layers(nc, x, ctxT, mask, gates, cols, rows, weights, W0, logits, u, X, ident)
        quantised_ffn(nc, w1, b1_cols, w2, b2_row, gates, out, X, ident)


def kernel(**inputs):
    import concourse.bacc as bacc
    from concourse.bass_utils import run_bass_kernel_spmd

    nc = bacc.Bacc("TRN2", target_bir_lowering=False, num_devices=1)
    arrays = {}

    def give(name, a):
        a = np.ascontiguousarray(a)
        arrays[name] = a
        return nc.dram_tensor(name, a.shape, mybir.dt.from_np(a.dtype), kind="ExternalInput").ap()

    i = {k: np.asarray(v) for k, v in inputs.items()}

    def columns(name, a):
        return give(name, a.reshape(-1, P).T)

    x = give("x_in", i["x"].reshape(B * S, D))
    ctxT = give("ctx_T", i["ctx_1024"].reshape(B * KEYS, D).T)
    mask = give("mask_in", i["mask_BxS2_ik0"].reshape(B * KEYS))
    gates = give("gates", np.stack([i["g_xattn"], i["g_ffn"]], axis=1).reshape(4))
    cols, rows, weights = [], [], []
    for l in range(LAYERS):
        pre = f"L{l}_xattn_"
        cols.append([columns(f"b{n}{l}", i[pre + "b" + n]) for n in "qkv"])
        rows.append(give(f"bo{l}", i[pre + "bo"]))
        weights.append([give(f"W{n}T{l}", i[pre + "W" + n].T) for n in "qkvo"])
    rows.append(give("b0_in", i["L0_ffn_b"]))
    W0 = give("W0", i["L0_ffn_W"])
    logits = give("logits", i["L0_ffn_logits"].reshape(1, OPS))
    u = give("u", i["L0_ffn_u"].reshape(1, OPS))
    w1, w2 = give("w1", i["L1_ffn_w1"]), give("w2", i["L1_ffn_w2"])
    b1_cols, b2_row = columns("b1_in", i["L1_ffn_b1"]), give("b2_in", i["L1_ffn_b2"])
    out = nc.dram_tensor("out", (B * S, D), FP32, kind="ExternalOutput").ap()
    flamingo(nc, x, ctxT, mask, gates, cols, rows, weights, W0, logits, u, w1, b1_cols, w2, b2_row, out)
    r = run_bass_kernel_spmd(nc, [arrays], core_ids=[0])
    return r.results[0]["out"].reshape(B, S, D)
```

```python
from contextlib import ExitStack

import numpy as np
import concourse.bass as bass
from concourse import mybir

FP32 = mybir.dt.float32
FP32R = mybir.dt.float32r
BF16 = mybir.dt.bfloat16
I32 = mybir.dt.int32
U32 = mybir.dt.uint32
ALU = mybir.AluOpType
ACT = mybir.ActivationFunctionType
AX = mybir.AxisListType

P = 128
B, S, D = 2, 2048, 512
KEYS = 154
HEADS = 16
HD = D // HEADS
F = 2048
OPS = 8
LAYERS = 2
CH = D // P
HPG = P // HD
TOK = 512
SUB = TOK // P
TILES = B * S // P
STEPS_B = S // TOK
STEPS = B * STEPS_B
UNITS = CH * SUB
REM = KEYS - P
HALF = 2 * KEYS
FC = F // P
SCALE = float(HD) ** -0.5
CLAMP = 50000.0
NEG_FILL = -9.0e15
LN_EPS = 1e-5
Q_EPS = 1e-8
MAGIC = 12582912.0

CREDIT = 1
LAG_T = 3
PR_BUFS = 4

WINDOW = {1: [("Q", 2)], 2: [("Q", 3)], 3: [("PV", 3)], 4: [("WO", 0)], 5: [("WO", 1)], 6: [("WO", 2)],
          7: [("WO", 3), ("PV", 0)], 8: [("XT", 0)], 9: [("XT", 1)], 10: [("XT", 2)], 11: [("XT", 3), ("PV", 1)],
          13: [("Q", 0)], 14: [("Q", 1)], 15: [("PV", 2)]}
DRAIN = {16: [("Q", 2)], 17: [("Q", 3)], 19: [("PV", 3)], 20: [("WO", 0)], 21: [("WO", 1)], 22: [("WO", 2)],
         23: [("WO", 3)]}
OF_BEFORE = (("Q", 2), ("Q", 3), ("PV", 3), ("WO", 0), ("WO", 1), ("WO", 2), ("WO", 3))
OF_NEXT = (("XT", 0), ("XT", 1), ("XT", 2), ("XT", 3), ("Q", 0), ("Q", 1))


def select(table, leave_out):
    events, uses, his = {}, 0, 0
    for k in sorted(table):
        events[k] = []
        for kind, i in table[k]:
            if (kind, i) not in leave_out:
                events[k].append((kind, i, uses, his))
                uses, his = uses + 1, his + (kind != "WO")
    return events, uses, his


EVENTS = {"first": select(WINDOW, OF_BEFORE),
          "full": select(WINDOW, ()),
          "turn": select(WINDOW, (("Q", 0), ("Q", 1))),
          "last": select(WINDOW, OF_NEXT),
          "drain": select(DRAIN, ()),
          "end": select(DRAIN, (("Q", 2), ("Q", 3)))}


def carried_from(kind):
    events, uses, his = EVENTS[kind]
    return [(name, i, use - uses, hi - his) for name, i, use, hi in events.get(UNITS - 1, [])]


CARRIED = {"first": [], "full": carried_from("full"), "turn": carried_from("full"), "last": carried_from("full"),
           "drain": carried_from("full"), "end": carried_from("last")}
assert carried_from("first") == carried_from("full") and carried_from("turn") == carried_from("last")
AFTER_Q0 = EVENTS["full"][1] - 1 - next(u for events in EVENTS["full"][0].values() for n, i, u, _ in events
                                        if (n, i) == ("Q", 0))

KV_USES, KV_HIS = CH + 2, CH
PROLOGUE = 2 * CH
FULL_USES, FULL_HIS = EVENTS["full"][1:]
DENSE = [("OUT", 0), ("XT", 0), ("XT", 1), ("OUT", 1), ("XT", 2), ("XT", 3), ("OUT", 2), ("OUT", 3)]
DENSE_USES = len(DENSE)


def flat(ap):
    return ap.rearrange("p a n -> p (a n)")


def attention_layers(nc, x, ctxT, mask, gates, cols, rows, weights, W0, logits, u, X, ident, final):
    ctx = ExitStack()
    with ctx:
        def sb(name, shape, dt):
            return ctx.enter_context(nc.sbuf_tensor(name, shape, dt))

        def sem(name):
            return ctx.enter_context(nc.semaphore(name))

        wa_hi = sb("wa_hi", [P, CH, D], FP32R)
        wa_lo = sb("wa_lo", [P, CH, D], FP32R)
        wo_hi = sb("wo_hi", [P, CH, D], FP32R)
        wo_lo = sb("wo_lo", [P, CH, D], FP32R)
        k_hi = sb("k_hi", [P, CH, HPG * KEYS], FP32R)
        k_lo = sb("k_lo", [P, CH, HPG * KEYS], FP32R)
        v_main = sb("v_main", [P, D], FP32)
        v_rem = sb("v_rem", [P, CH, P], FP32)
        xt_hi = sb("xt_hi", [P, CH, TOK], FP32R)
        xt_lo = sb("xt_lo", [P, CH, TOK], FP32R)
        ot_hi = sb("ot_hi", [P, CH, TOK], FP32R)
        ot_lo = sb("ot_lo", [P, CH, TOK], FP32R)
        q_hi = sb("q_hi", [P, CH, TOK], FP32R)
        q_lo = sb("q_lo", [P, CH, TOK], FP32R)
        xn = sb("xn", [P, SUB, D], FP32)
        sc = sb("sc", [P, 2, HPG, KEYS], FP32)
        soft = sb("soft", [P, PR_BUFS * HPG * KEYS], FP32)
        pn_rem = sb("pn_rem", [P, PR_BUFS, P], FP32)
        pT = sb("pT", [P, HPG + 1, TOK], FP32)
        bias_cols = sb("bias_cols", [P, 3 * LAYERS, CH], FP32)
        bk_scaled = sb("bk_scaled", [P, LAYERS, CH], FP32)
        bo_row = sb("bo_row", [P, D], FP32)
        mask_add = sb("mask_add", [P, B, KEYS], FP32)
        gate_raw = sb("gate_raw", [P, 4], FP32)
        gate = sb("gate", [P, 4], FP32)
        stats = sb("stats", [P, SUB, 6], FP32)
        f_stats = sb("f_stats", [P, SUB, 6], FP32)
        f_meanvar = sb("f_meanvar", [P, SUB, 2], FP32)
        f_vareps = sb("f_vareps", [P, SUB], FP32)
        meanvar = sb("meanvar", [P, SUB, 2], FP32)
        vareps = sb("vareps", [P, SUB], FP32)
        rstd = sb("rstd", [P, SUB], FP32)
        neg_half = sb("neg_half", [P, SUB], FP32)
        eps_row = sb("eps_row", [P, SUB], FP32)
        smax = sb("smax", [P, 2, HPG], FP32)
        nmax = sb("nmax", [P, 2, HPG], FP32)
        rsum = sb("rsum", [P, PR_BUFS, HPG], FP32)
        wait_pad = sb("wait_pad", [P, 1], FP32)
        rec = sb("rec", [P, PR_BUFS, HPG], FP32)
        gum = sb("gum", [1, 8, OPS], FP32)
        gmax = sb("gmax", [1, OPS], FP32)
        gidx = sb("gidx", [1, OPS], U32)
        ps = ctx.enter_context(nc.psum_tensor("ps", [P, 8, 512], FP32))
        consts = sem("consts")
        zeroed = sem("zeroed")
        k_lo_zero = sem("k_lo_zero")
        small_in = sem("small_in")
        x_in0 = sem("x_in0")
        x_in1 = sem("x_in1")
        x_in2 = sem("x_in2")
        first_qo_in = sem("first_qo_in")
        raw_in = sem("raw_in")
        dense_in = sem("dense_in")
        brow_in = sem("brow_in")
        prep = sem("prep")
        act_prep = sem("act_prep")
        bo_scaled = sem("bo_scaled")
        choice_max = sem("choice_max")
        pick = sem("pick")
        split_hi = sem("split_hi")
        split_lo = sem("split_lo")
        stats_done = sem("stats_done")
        aggr_done = sem("aggr_done")
        f_stats_done = sem("f_stats_done")
        f_aggr_done = sem("f_aggr_done")
        f_eps_done = sem("f_eps_done")
        eps_done = sem("eps_done")
        rstd_done = sem("rstd_done")
        xn_ready = sem("xn_ready")
        pre_added = sem("pre_added")
        a_full = sem("a_full")
        a_free = sem("a_free")
        hi_done = sem("hi_done")
        k_tmp_done = sem("k_tmp_done")
        s_full = sem("s_full")
        s_free = sem("s_free")
        masked = sem("masked")
        max_done = sem("max_done")
        exp_done = sem("exp_done")
        rec_done = sem("rec_done")
        pn_done = sem("pn_done")
        t_full = sem("t_full")
        ptm_out = sem("ptm_out")
        ptr_out = sem("ptr_out")
        block = ctx.enter_context(nc.Block())

        pr = soft[:, :].rearrange("p (b h k) -> p b h k", b=PR_BUFS, h=HPG)
        raw_a = pT[:, 0:CH, :]
        raw_b = soft[:, 0:CH * D].rearrange("p (c n) -> p c n", c=CH)
        TAIL = TILES - 2 * CH
        first_qo = X[:, TAIL:TAIL + CH, :], X[:, TAIL + CH:TILES, :]
        scf = sc[:, :, :, :].rearrange("p b h k -> p (b h k)")
        ctx_t = scf[:, 0:CH * KEYS].rearrange("p (c k) -> p c k", c=CH)
        k_tmp = scf[:, CH * KEYS:2 * CH * KEYS].rearrange("p (c k) -> p c k", c=CH)
        mask_i = scf[:, CH * KEYS:(CH + B) * KEYS].bitcast(I32).rearrange("p (b k) -> p b k", b=B)
        mask_f = scf[:, (CH + B) * KEYS:(CH + 2 * B) * KEYS].rearrange("p (b k) -> p b k", b=B)

        def work(a):
            return ps[:, a % 2, :]

        def dense_bank(n):
            return ps[:, n % 4, :]

        def score_bank(v):
            return ps[:, 2 + v % 4, 0:HALF]

        PTM, PTR = ps[:, 6, :], ps[:, 7, :]

        def tile_of(n):
            return flat(X[:, bass.ds(n, 1), :])

        LAST_WINDOW = ("turn", "last")
        at = {}
        uses = his = 0

        def part(name, part_uses, part_his):
            nonlocal uses, his
            at[name] = (uses, his)
            uses, his = uses + part_uses, his + part_his

        for l in range(LAYERS):
            part(("kv", l, 0), KV_USES, KV_HIS)
            if l:
                part("dense end", 2 * DENSE_USES - CH, CH)
            part(("prologue", l), PROLOGUE, PROLOGUE)
            part(("first", l, 0), *EVENTS["first"][1:])
            part(("full", l, 0), (STEPS_B - 1) * FULL_USES, (STEPS_B - 1) * FULL_HIS)
            part(("drain", l, 0), *EVENTS["drain"][1:])
            part(("kv", l, 1), KV_USES, KV_HIS)
            part(("first", l, 1), *EVENTS["first"][1:])
            part(("full", l, 1), (STEPS_B - 2) * FULL_USES, (STEPS_B - 2) * FULL_HIS)
            kind = LAST_WINDOW[l]
            part((kind, l, 1), *EVENTS[kind][1:])
            part(("end", l, 1), *EVENTS["end"][1:])
            if l == 0:
                part("dense", (STEPS - 2) * DENSE_USES, (STEPS - 2) * CH)
        part("end", 0, 0)
        LN = (0, 2 * STEPS)
        LN_DENSE = STEPS

        def layer_program(eng, l, kv, prologue, units):
            def one(kind, b, step):
                a, h = at[kind, l, b]
                units(l, b, step, a, h, kind, a)

            def full(b, step, count):
                a, h = at["full", l, b]
                with eng.Fori(0, count) as it:
                    units(l, b, it + step, it * FULL_USES + a, it * FULL_HIS + h, "full", a)

            if l == 0:
                kv(l, 0)
            prologue(l)
            one("first", 0, 0)
            full(0, 1, STEPS_B - 1)
            one("drain", 0, STEPS_B - 1)
            kv(l, 1)
            one("first", 1, STEPS_B)
            full(1, STEPS_B + 1, STEPS_B - 2)
            one(LAST_WINDOW[l], 1, STEPS - 1)
            one("end", 1, STEPS - 1)

        def schedule(kind):
            events = EVENTS[kind][0]
            draining = kind in ("drain", "end")
            ks = range(UNITS, max(DRAIN) + 2) if draining else range(UNITS)
            carried = kind != "first"

            def events_of(k):
                if k == ks[0] - 1:
                    return CARRIED[kind]
                return events.get(k, [])

            return ks, draining, carried, events_of

        def load_biases(queue, l):
            for k in range(3):
                queue.dma_start(bias_cols[:, 3 * l + k, :], cols[l][k]).then_inc(small_in, 16)

        @block.sync
        def _(sp):
            def load_raw(dst, src):
                sp.dma_start(dst, src.rearrange("(c p) n -> p c n", p=P)).then_inc(raw_in, 16)

            def load_kv(l, b):
                load_raw(ctx_t, ctxT[:, b * KEYS:(b + 1) * KEYS])
                load_raw(raw_a, weights[l][1])
                load_raw(raw_b, weights[l][2])

            def load_qo(l):
                sp.wait_ge(a_free, at["kv", l, 0][0] + KV_USES)
                load_raw(raw_a, weights[l][0])
                load_raw(raw_b, weights[l][3])

            def after_values(l, b):
                kind = "end" if b else "drain"
                return at[kind, l, b][0] + EVENTS[kind][0][max(DRAIN) - SUB][0][2] + 1

            xv = x.rearrange("(t p) n -> p t n", p=P)

            def load_x(a, b, arrived):
                sp.dma_start(X[:, a:b, :], xv[:, a:b, :]).then_inc(arrived, 16)

            load_raw(ctx_t, ctxT[:, 0:KEYS])
            load_biases(sp, 0)
            load_raw(raw_a, weights[0][1])
            load_x(0, SUB, x_in0)
            load_raw(raw_b, weights[0][2])
            for k in range(2):
                sp.dma_start(first_qo[k], weights[0][3 * k].rearrange("(c p) n -> p c n", p=P)).then_inc(first_qo_in, 16)
            load_x(SUB, TAIL, x_in1)
            sp.dma_start(bo_row[:, :], rows[0].partition_broadcast(P)).then_inc(brow_in, 16)
            sp.wait_ge(split_lo, 2)
            load_x(TAIL, TILES, x_in2)
            sp.wait_ge(a_free, after_values(0, 0))
            load_kv(0, 1)
            sp.wait_ge(pick, 10)
            sp.wait_ge(a_free, at["turn", 0, 1][0] + next(use for events in EVENTS["turn"][0].values()
                                                          for name, i, use, _ in events if (name, i) == ("XT", 3)) + 1)
            idx = sp.value_load(gidx[0:1, 0:1], min_val=0, max_val=OPS - 1)
            sp.dma_start(xn[:, :, :], W0[bass.ds(idx, 1), :, :].rearrange("a (c p) n -> p (a c) n", p=P)).then_inc(dense_in, 16)
            sp.wait_ge(pre_added, STEPS * SUB)
            sp.dma_start(bo_row[:, :], rows[LAYERS][bass.ds(idx, 1), :].partition_broadcast(P)).then_inc(brow_in, 16)
            sp.wait_ge(a_free, after_values(0, 1))
            load_kv(1, 0)
            load_qo(1)
            sp.wait_ge(pre_added, 2 * STEPS * SUB)
            sp.dma_start(bo_row[:, :], rows[1].partition_broadcast(P)).then_inc(brow_in, 16)
            sp.wait_ge(a_free, after_values(1, 0))
            load_kv(1, 1)

        @block.gpsimd
        def _(pool):
            pool.sem_inc(pn_done, CREDIT)
            pool.memset(k_lo[:, :, :].bitcast(FP32), 0.0).then_inc(k_lo_zero, 1)
            pool.memset(ident[:, :], 0.0).then_inc(consts, 1)
            pool.memset(neg_half[:, :], -0.5).then_inc(consts, 1)
            pool.memset(eps_row[:, :], LN_EPS).then_inc(consts, 1)
            pool.wait_ge(consts, 1)
            pool.affine_select(out=ident[:, :], in_=ident[:, :], compare_op=ALU.not_equal, fill=1.0, base=0,
                               pattern=[[-1, P]], channel_multiplier=1).then_inc(consts, 1)
            pool.memset(pn_rem[:, :, :], 0.0).then_inc(consts, 1)
            pool.wait_ge(consts, 5)

            def rstd_of(ln):
                pool.wait_ge(aggr_done, (ln + 1) * SUB)
                pool.tensor_tensor(vareps[:, :], vareps[:, :], meanvar[:, :, 1], ALU.add).then_inc(eps_done, 1)
                pool.wait_ge(eps_done, ln + 1)
                pool.tensor_tensor(rstd[:, :], vareps[:, :], neg_half[:, :], ALU.pow).then_inc(rstd_done, 1)

            def pre_add(ln, n, s):
                if s == 0:
                    pool.wait_ge(xn_ready, (ln + 1) * SUB)
                pool.tensor_tensor(tile_of(n + s), tile_of(n + s), bo_row[:, :], ALU.add).then_inc(pre_added, 1)

            def normalise(unit, slot):
                pool.wait_ge(rec_done, unit + 1)
                r = rec[:, slot, :, None]
                pool.tensor_tensor(pn_rem[:, slot, :].rearrange("p (h k) -> p h k", h=HPG)[:, :, 0:REM],
                                   pr[:, slot, :, P:KEYS], r.broadcast_to([P, HPG, REM]), ALU.mult)
                pool.tensor_tensor(pr[:, slot, :, 0:P], pr[:, slot, :, 0:P], r.broadcast_to([P, HPG, P]),
                                   ALU.mult).then_inc(pn_done, 1)

            def prologue(l):
                rstd_of(LN[l])
                pool.wait_ge(bo_scaled, 2 * l + 1)
                for s in range(SUB):
                    pre_add(LN[l], 0, s)

            def final_rstd(of):
                pool.wait_ge(f_aggr_done, of)
                pool.tensor_tensor(f_vareps[:, :], final["meanvar"][:, bass.ds(of * SUB - SUB, SUB), 1], eps_row[:, :],
                                   ALU.add).then_inc(f_eps_done, 1)
                pool.wait_ge(f_eps_done, of)
                pool.tensor_tensor(final["rstd"][:, bass.ds(of * SUB - SUB, SUB)], f_vareps[:, :], neg_half[:, :], ALU.pow)

            def units(l, b, step, a, h, kind, a_static):
                ks, draining, carried, _ = schedule(kind)
                if draining:
                    if (l, kind) == (1, "end"):
                        final_rstd(STEPS)
                    return
                unit0 = (step + l * STEPS) * UNITS
                for k in ks:
                    if k == SUB and kind != "last":
                        rstd_of(step + (LN[l] + 1))
                    normalise(unit0 + k, k % PR_BUFS)
                    if k == 13 and l == 1 and not (kind == "first" and b == 0):
                        final_rstd(step)
                    if k in (8, 10, 12, 14) and kind in ("first", "full"):
                        pre_add(step + (LN[l] + 1), (step + 1) * SUB, (k - 8) // 2)

            layer_program(pool, 0, lambda l, b: None, prologue, units)
            rstd_of(LN_DENSE + 1)
            pool.wait_ge(bo_scaled, 2)
            for s in range(SUB):
                pre_add(LN_DENSE, 0, s)
            for s in range(SUB):
                pre_add(LN_DENSE + 1, SUB, s)
            with pool.Fori(0, STEPS - 2) as it:
                rstd_of(it + (LN_DENSE + 2))
                for s in range(SUB):
                    pre_add(it + (LN_DENSE + 2), (it + 2) * SUB, s)
            layer_program(pool, 1, lambda l, b: None, prologue, units)

        @block.scalar
        def _(act):
            act.dma_start(gum[0:1, 0, :], u).then_inc(small_in, 16)
            act.dma_start(gum[0:1, 1, :], logits).then_inc(small_in, 16)
            act.dma_start(gate_raw[:, :], gates.partition_broadcast(P)).then_inc(small_in, 16)
            load_biases(act, 1)
            act.dma_start(flat(mask_i), mask.partition_broadcast(P)).then_inc(small_in, 16)
            act.sem_inc(ptm_out, CREDIT)
            act.sem_inc(ptr_out, CREDIT)
            act.wait_ge(small_in, 160)
            for l in range(LAYERS):
                act.activation(bk_scaled[:, l, :], bias_cols[:, 3 * l + 1, :], ACT.Copy, scale=SCALE).then_inc(act_prep, 1)
            act.activation(gate[:, :], gate_raw[:, :], ACT.Tanh).then_inc(act_prep, 1)
            act.wait_ge(zeroed, 1)
            act.wait_ge(act_prep, 3)
            act.wait_ge(prep, 4)

            def choice():
                act.activation(gum[0:1, 2, :], gum[0:1, 0, :], ACT.Ln).then_inc(pick, 1)
                act.wait_ge(pick, 1)
                act.activation(gum[0:1, 3, :], gum[0:1, 2, :], ACT.Ln, scale=-1.0).then_inc(pick, 1)
                act.wait_ge(pick, 4)
                act.activation(gum[0:1, 5, :], gum[0:1, 4, :], ACT.Exp, accum_out=gum[0:1, 6, 0:1]).then_inc(pick, 1)
                act.wait_ge(pick, 5)
                act.activation(gum[0:1, 6, 1:2], gum[0:1, 6, 0:1], ACT.Ln).then_inc(pick, 1)

            def upper_of_weights(arrived, n, pairs):
                act.wait_ge(arrived, n)
                for dst, src in pairs:
                    act.activation(dst, src, ACT.Copy).then_inc(split_hi, 1)

            def upper(use, bank, dst, bias=None):
                act.wait_ge(a_full, use + 1)
                if bias is None:
                    act.activation(dst, bank, ACT.Copy).then_inc(hi_done, 1)
                else:
                    act.activation(dst, bank, ACT.Identity, bias=bias).then_inc(hi_done, 1)

            def exps(l, unit0, k, carried):
                free = k + 1 - PR_BUFS
                act.wait_ge(t_full, unit0 + ((free if carried else max(free, 0)) + CREDIT))
                for h in range(HPG):
                    if l == 0:
                        if h == 0:
                            act.wait_ge(max_done, unit0 + (k + 1))
                        src = sc[:, k % 2, h, :]
                    else:
                        if h % 2 == 0:
                            act.wait_ge(max_done, unit0 * 2 + (2 * k + h // 2 + 1 - STEPS * UNITS))
                        src = score_bank(2 * k + h // 2)[:, (h % 2) * KEYS:(h % 2 + 1) * KEYS]
                    i = act.activation(pr[:, k % PR_BUFS, h, :], src, ACT.Exp, bias=nmax[:, k % 2, h:h + 1],
                                       accum_out=rsum[:, k % PR_BUFS, h:h + 1])
                    if l == 1 and h % 2:
                        i.then_inc(s_free, 1)
                    if l == 0 and h == HPG - 1:
                        i.then_inc(exp_done, 1)

            def copy_pT(unit0, k):
                g, s = k // SUB, k % SUB
                act.wait_ge(t_full, unit0 + (k + 1 + CREDIT))
                act.activation(pT[:, 0:HPG, s * P:(s + 1) * P], PTM.rearrange("p (h q) -> p h q", h=HPG),
                               ACT.Copy).then_inc(ptm_out, 1)
                if s == SUB - 1:
                    act.activation(pT[:, HPG, :], PTR, ACT.Copy).then_inc(ptr_out, 1)

            def event(l, kind, i, bank, use):
                if kind == "XT":
                    upper(use, bank, xt_hi[:, i, :])
                elif kind == "Q":
                    upper(use, bank, q_hi[:, i, :], bias_cols[:, 3 * l, i:i + 1])
                elif kind == "PV":
                    upper(use, bank, ot_hi[:, i, :], bias_cols[:, 3 * l + 2, i:i + 1])

            def kv(l, b):
                if (l, b) == (0, 1):
                    choice()
                a0, _ = at["kv", l, b]
                for g in range(CH):
                    act.wait_ge(a_full, a0 + g + 1)
                    act.activation(k_tmp[:, g, :], work(a0 + g)[:, 0:KEYS], ACT.Identity, scale=SCALE,
                                   bias=bk_scaled[:, l, g:g + 1]).then_inc(k_tmp_done, 1)
                    act.wait_ge(k_tmp_done, (l * B + b) * CH + g + 1)
                    for h in range(HPG):
                        q = slice(h * HD, (h + 1) * HD)
                        i = act.activation(k_hi[q, g, h * KEYS:(h + 1) * KEYS], k_tmp[q, g, :], ACT.Copy)
                    i.then_inc(hi_done, 1)

            def prologue(l):
                if l:
                    act.wait_ge(a_full, at["prologue", l][0])
                raw_q, raw_o = (raw_a, raw_b) if l else first_qo
                arrived = (raw_in, 176) if l else (first_qo_in, 32)
                upper_of_weights(*arrived, ((wa_hi[:, :, :], raw_q),))
                a0, _ = at["prologue", l]
                for i in range(PROLOGUE):
                    event(l, "XT" if i < CH else "Q", i % CH, work(a0 + i), a0 + i)
                    if i == CH:
                        upper_of_weights(*arrived, ((wo_hi[:, :, :], raw_o),))

            def units(l, b, step, a, h, kind, a_static):
                unit0 = (step + l * STEPS) * UNITS
                ks, draining, carried, events_of = schedule(kind)
                for k in ks:
                    for name, i, use, _ in events_of(k - 1):
                        event(l, name, i, work(a_static + use), a + use)
                    if not draining:
                        exps(l, unit0, k, carried)
                    if l == 0 and (carried or k >= LAG_T) and k - LAG_T < UNITS:
                        copy_pT(unit0, k - LAG_T)
                    if (l, kind, k) == (0, "end", max(DRAIN) - 2):
                        upper_of_weights(dense_in, 16, ((wa_hi[:, :, :], xn[:, :, :]),))

            layer_program(act, 0, kv, prologue, units)
            bufs = (xt_hi, ot_hi)

            def dense_step(a, j, turned):
                for n, (kind, i) in enumerate(DENSE):
                    if kind == "XT" and turned:
                        upper(a + n, dense_bank(n), bufs[1 - j][:, i, :])

            a0, _ = at["dense"]
            with act.Fori(0, (STEPS - 2) // 2) as it:
                for j in range(2):
                    dense_step(it * (2 * DENSE_USES) + (a0 + j * DENSE_USES), j, True)
            kv(1, 0)
            dense_step(at["dense end"][0], 0, True)
            layer_program(act, 1, kv, prologue, units)

        @block.vector
        def _(dve):
            dve.sem_inc(s_free, CREDIT)
            dve.memset(k_hi[:, :, :].bitcast(FP32), 0.0).then_inc(zeroed, 1)
            dve.memset(v_rem[:, :, :], 0.0).then_inc(prep, 1)
            dve.wait_ge(small_in, 160)
            dve.tensor_copy(mask_f, mask_i).then_inc(prep, 1)
            dve.wait_ge(prep, 2)
            dve.tensor_scalar(mask_add[:, :, :], mask_f, 0.0, NEG_FILL, ALU.is_equal, ALU.mult).then_inc(prep, 1)
            dve.wait_ge(prep, 3)
            dve.tensor_tensor(mask_add[:, :, :], mask_add[:, :, :], mask_f, ALU.add).then_inc(prep, 1)
            dve.wait_ge(prep, 4)
            dve.wait_ge(act_prep, 3)
            dve.wait_ge(k_lo_zero, 1)

            def choice():
                dve.tensor_reduce(gum[0:1, 7, 0:1], gum[0:1, 1, :], axis=AX.X, op=ALU.max).then_inc(choice_max, 1)
                dve.wait_ge(choice_max, 1)
                dve.wait_ge(pick, 2)
                dve.tensor_scalar(gum[0:1, 4, :], gum[0:1, 1, :], gum[0:1, 7, 0:1], None, ALU.subtract).then_inc(pick, 2)
                dve.wait_ge(pick, 6)
                dve.tensor_scalar(gum[0:1, 7, :], gum[0:1, 4, :], gum[0:1, 6, 1:2], None, ALU.subtract).then_inc(pick, 1)
                dve.wait_ge(pick, 7)
                dve.tensor_tensor(gum[0:1, 7, :], gum[0:1, 7, :], gum[0:1, 3, :], ALU.subtract).then_inc(pick, 1)
                dve.wait_ge(pick, 8)
                dve.max(gmax[0:1, :], gum[0:1, 7, :]).then_inc(pick, 1)
                dve.wait_ge(pick, 9)
                dve.max_index(gidx[0:1, :], gmax[0:1, :], gum[0:1, 7, :]).then_inc(pick, 1)

            def scale_row(n, gate_col):
                dve.wait_ge(brow_in, 16 * n)
                dve.tensor_scalar(bo_row[:, :], bo_row[:, :], gate[:, gate_col:gate_col + 1], None, ALU.mult)\
                    .then_inc(bo_scaled, 1)

            def lower_of_weights(arrived, n, done, pairs):
                dve.wait_ge(arrived, n)
                for j, (dst, src, hi) in enumerate(pairs):
                    dve.wait_ge(split_hi, done + j + 1)
                    dve.tensor_tensor(dst, src, hi.bitcast(FP32), ALU.subtract).then_inc(split_lo, 1)

            def statistics(n, which):
                for s in which:
                    dve.bn_stats(stats[:, s, :], tile_of(n + s)).then_inc(stats_done, 1)

            def aggregates(ln):
                dve.wait_ge(stats_done, (ln + 1) * SUB)
                dve.memset(vareps[:, :], LN_EPS)
                for s in range(SUB):
                    dve.bn_aggr(meanvar[:, s, :], stats[:, s, :]).then_inc(aggr_done, 1)

            def normalised(ln, n, which):
                for s in which:
                    if s == 0:
                        dve.wait_ge(rstd_done, ln + 1)
                    dve.tensor_scalar(xn[:, s, :], tile_of(n + s), meanvar[:, s, 0:1], rstd[:, s:s + 1],
                                      ALU.subtract, ALU.mult).then_inc(xn_ready, 1)

            def layer_norm(ln, n):
                statistics(n, range(SUB))
                aggregates(ln)
                normalised(ln, n, range(SUB))

            def lower(hi_count, bank, dst, hi, bias=None):
                dve.wait_ge(hi_done, hi_count)
                if bias is None:
                    dve.tensor_tensor(dst, bank, hi.bitcast(FP32), ALU.subtract).then_inc(a_free, 1)
                else:
                    dve.scalar_tensor_tensor(out=dst, in0=bank, scalar=bias, in1=hi.bitcast(FP32),
                                             op0=ALU.add, op1=ALU.subtract).then_inc(a_free, 1)

            def residual(use, bank, n, gate_col, pre):
                dve.wait_ge(a_full, use + 1)
                dve.wait_ge(pre_added, pre)
                dve.scalar_tensor_tensor(out=tile_of(n), in0=bank, scalar=gate[:, gate_col:gate_col + 1],
                                         in1=tile_of(n), op0=ALU.mult, op1=ALU.add).then_inc(a_free, 1)

            def maxima(l, b, unit0, k):
                for half in range(2):
                    v = 2 * k + half
                    dve.wait_ge(s_full, unit0 * 2 + (v + 1))
                    bank = score_bank(v).rearrange("p (h k) -> p h k", h=2)
                    if l == 0:
                        dve.tensor_scalar(sc[:, k % 2, 2 * half:2 * half + 2, :], bank, CLAMP, -CLAMP,
                                          ALU.min, ALU.max).then_inc(s_free, 1)
                    else:
                        dve.tensor_reduce(nmax[:, k % 2, 2 * half:2 * half + 2], bank, axis=AX.X,
                                          op=ALU.max, negate=True).then_inc(max_done, 1)
                if l == 0:
                    dve.wait_ge(s_free, unit0 * 2 + (2 * k + 2 + CREDIT))
                    dve.memset(wait_pad[:, :], 0.0)
                    for h in range(HPG):
                        i = dve.tensor_tensor_reduce(out=sc[:, k % 2, h, :], in0=sc[:, k % 2, h, :],
                                                     in1=mask_add[:, b, :], scale=1.0, scalar=-3.0e38,
                                                     op0=ALU.add, op1=ALU.max, accum_out=smax[:, k % 2, h:h + 1])
                    i.then_inc(masked, 1)
                    dve.wait_ge(masked, unit0 + (k + 1))
                    dve.tensor_scalar(nmax[:, k % 2, :], smax[:, k % 2, :], -1.0, None, ALU.mult).then_inc(max_done, 1)

            def reciprocals(l, unit0, k):
                if l == 0:
                    dve.wait_ge(exp_done, unit0 + (k + 1))
                else:
                    dve.wait_ge(s_free, unit0 * 2 + (2 * k + 2 + CREDIT))
                dve.reciprocal(rec[:, k % PR_BUFS, :], rsum[:, k % PR_BUFS, :]).then_inc(rec_done, 1)

            def copy_pT(unit0, k):
                g, s = k // SUB, k % SUB
                dve.wait_ge(t_full, unit0 + (k + 1 + CREDIT))
                dve.tensor_copy(pT[:, 0:HPG, s * P:(s + 1) * P],
                                PTM.rearrange("p (h q) -> p h q", h=HPG)).then_inc(ptm_out, 1)
                if s == SUB - 1:
                    dve.tensor_copy(pT[:, HPG, :], PTR).then_inc(ptr_out, 1)

            def event(l, kind, i, bank, use, hi_count, step):
                if kind == "XT":
                    lower(hi_count, work(bank), xt_lo[:, i, :], xt_hi[:, i, :])
                elif kind == "Q":
                    lower(hi_count, work(bank), q_lo[:, i, :], q_hi[:, i, :], bias_cols[:, 3 * l, i:i + 1])
                elif kind == "PV":
                    lower(hi_count, work(bank), ot_lo[:, i, :], ot_hi[:, i, :], bias_cols[:, 3 * l + 2, i:i + 1])
                else:
                    residual(use, work(bank), step * SUB + (i - SUB), 2 * l, step * SUB + ((LN[l] - 1) * SUB + i + 1))

            def kv(l, b):
                if (l, b) == (0, 1):
                    choice()
                a0, h0 = at["kv", l, b]
                for g in range(CH):
                    dve.wait_ge(hi_done, h0 + g + 1)
                    for h in range(HPG):
                        q = slice(h * HD, (h + 1) * HD)
                        blk = slice(h * KEYS, (h + 1) * KEYS)
                        i = dve.tensor_tensor(k_lo[q, g, blk], k_tmp[q, g, :], k_hi[q, g, blk].bitcast(FP32), ALU.subtract)
                    i.then_inc(a_free, 1)
                dve.wait_ge(a_full, a0 + CH + 1)
                dve.tensor_copy(v_main[:, :], work(a0 + CH)).then_inc(a_free, 1)
                dve.wait_ge(a_full, a0 + CH + 2)
                for h in range(HPG):
                    q = slice(h * HD, h * HD + REM)
                    i = dve.tensor_copy(v_rem[q, :, h * HD:(h + 1) * HD],
                                        work(a0 + CH + 1)[q, 0:P].rearrange("p (g d) -> p g d", g=CH))
                i.then_inc(a_free, 1)

            def prologue(l):
                raw_q, raw_o = (raw_a, raw_b) if l else first_qo
                arrived = (raw_in, 176) if l else (first_qo_in, 32)
                lower_of_weights(*arrived, 3 * l, ((wa_lo[:, :, :], raw_q, wa_hi[:, :, :]),))
                a0, h0 = at["prologue", l]
                for i in range(PROLOGUE):
                    event(l, "XT" if i < CH else "Q", i % CH, a0 + i, a0 + i, h0 + i + 1, 0)
                    if i == CH:
                        lower_of_weights(*arrived, 3 * l + 1, ((wo_lo[:, :, :], raw_o, wo_hi[:, :, :]),))
                scale_row(2 * l + 1, 2 * l)

            def units(l, b, step, a, h, kind, a_static):
                unit0 = (step + l * STEPS) * UNITS
                ks, draining, carried, events_of = schedule(kind)
                ln, n_next = step + (LN[l] + 1), 0 if kind == "turn" else (step + 1) * SUB
                if kind == "turn":
                    dve.wait_ge(a_free, at["full", l, 1][0])
                if (l, kind, b) == (0, "first", 0):
                    dve.wait_ge(x_in1, 16)
                for k in ks:
                    early = k == 4 and not draining
                    if early:
                        for name, i, use, hi in events_of(k - 1):
                            event(l, name, i, a_static + use, a + use, h + (hi + 1), step)
                    if not draining:
                        maxima(l, b, unit0, k)
                    if (carried or k >= 1) and k - 1 < UNITS:
                        reciprocals(l, unit0, k - 1)
                    for name, i, use, hi in () if early else events_of(k - 1):
                        of = step + 1 if draining else step
                        event(l, name, i, a_static + use, a + use, h + (hi + 1), of)
                        if (l, name) == (1, "WO"):
                            n = of * SUB + (i - SUB)
                            dve.wait_ge(a_free, a + (use + 1))
                            dve.tensor_reduce(final["max"][:, bass.ds(n, 1)], tile_of(n), axis=AX.X, op=ALU.max)
                            dve.bn_stats(f_stats[:, i, :], tile_of(n)).then_inc(f_stats_done, 1)
                            if i == SUB - 1:
                                dve.wait_ge(f_stats_done, of * (SUB + 1) - 1)
                                dve.memset(wait_pad[:, :], 0.0)
                                for s in range(SUB):
                                    last = dve.bn_aggr(f_meanvar[:, s, :], f_stats[:, s, :])
                                last.then_inc(f_stats_done, 1)
                                dve.wait_ge(f_stats_done, of * (SUB + 1))
                                dve.tensor_copy(final["meanvar"][:, bass.ds(of * SUB - SUB, SUB), :],
                                                f_meanvar[:, :, :]).then_inc(f_aggr_done, 1)
                    if l == 1 and (carried or k >= LAG_T) and k - LAG_T < UNITS:
                        copy_pT(unit0, k - LAG_T)
                    if (l, kind, k) == (0, "end", max(DRAIN) - 1):
                        lower_of_weights(dense_in, 16, 2, ((wa_lo[:, :, :], xn[:, :, :], wa_hi[:, :, :]),))
                    if kind in ("first", "full", "turn"):
                        if k < SUB:
                            statistics(n_next, (k,))
                        if k == SUB - 1:
                            aggregates(ln)
                        if SUB <= k < 2 * SUB:
                            normalised(ln, n_next, (k - SUB,))
                if (l, kind, b) == (0, "first", 0):
                    dve.wait_ge(x_in2, 16)

            dve.wait_ge(x_in0, 16)
            layer_norm(LN[0], 0)
            layer_program(dve, 0, kv, prologue, units)
            dve.wait_ge(a_free, at["dense"][0])
            hi_bufs, lo_bufs = (xt_hi, ot_hi), (xt_lo, ot_lo)
            layer_norm(LN_DENSE + 1, SUB)
            scale_row(2, 1)

            def dense_step(step, a, h, j, turned, norm):
                hi = 0
                for n, (kind, i) in enumerate(DENSE if turned else [e for e in DENSE if e[0] == "OUT"]):
                    if kind == "XT":
                        hi += 1
                        lower(h + hi, dense_bank(n), lo_bufs[1 - j][:, i, :], hi_bufs[1 - j][:, i, :])
                    else:
                        residual(a + n, dense_bank(n), step * SUB + i, 1, step * SUB + (LN_DENSE * SUB + i + 1))
                    if norm:
                        ln, tile = norm
                        if (kind, i) == ("XT", 3):
                            statistics(tile, range(SUB))
                        elif (kind, i) == ("OUT", 2):
                            aggregates(ln)
                        elif (kind, i) == ("OUT", 3):
                            normalised(ln, tile, range(SUB))

            a0, h0 = at["dense"]
            with dve.Fori(0, (STEPS - 2) // 2) as it:
                for j in range(2):
                    step = it * 2 + j
                    dense_step(step, it * (2 * DENSE_USES) + (a0 + j * DENSE_USES), it * (2 * CH) + (h0 + j * CH), j, True,
                               (step + (LN_DENSE + 2), (step + 2) * SUB))
            kv(1, 0)
            a0, h0 = at["dense end"]
            dense_step(STEPS - 2, a0, h0, 0, True, (LN[1], 0))
            dense_step(STEPS - 1, a0 + DENSE_USES, h0 + CH, 1, False, None)
            layer_program(dve, 1, kv, prologue, units)

        @block.tensor
        def _(pe):
            pe.sem_inc(t_full, CREDIT)
            pe.wait_ge(consts, 5)

            def three_passes(out, pairs):
                n = 3 * len(pairs)
                j = 0
                for (w_hi, w_lo), (m_hi, m_lo) in pairs:
                    for w, m in ((w_hi, m_hi), (w_hi, m_lo), (w_lo, m_hi)):
                        last = nc.tensor.matmul(out, w, m, start=(j == 0), stop=(j == n - 1))
                        j += 1
                return last

            def transposes(bank, c, ln):
                for s in range(SUB):
                    if c == 0 and s == 0:
                        pe.wait_ge(xn_ready, (ln + 1) * SUB)
                    last = nc.tensor.transpose(bank[:, s * P:(s + 1) * P], xn[:, s, c * P:(c + 1) * P], ident[:, :])
                last.then_inc(a_full, 1)

            def queries(bank, m):
                ms = slice(m * P, (m + 1) * P)
                three_passes(work(bank), [((wa_hi[:, c, ms], wa_lo[:, c, ms]), (xt_hi[:, c, :], xt_lo[:, c, :]))
                                          for c in range(CH)]).then_inc(a_full, 1)

            def out_rows(bank, s, i_hi, i_lo, w_hi, w_lo):
                q = slice(s * P, (s + 1) * P)
                three_passes(bank, [((i_hi[:, c, q], i_lo[:, c, q]), (w_hi[:, c, :], w_lo[:, c, :]))
                                    for c in range(CH)]).then_inc(a_full, 1)

            def values(bank, g):
                nc.tensor.matmul(work(bank), v_rem[:, g, :], pT[:, HPG, :], start=True, stop=False, skip_group_check=True)
                for h in range(HPG):
                    last = nc.tensor.matmul(work(bank)[h * HD:(h + 1) * HD, :],
                                            v_main[:, (g * HPG + h) * HD:(g * HPG + h + 1) * HD], pT[:, h, :],
                                            start=False, stop=(h == HPG - 1), skip_group_check=True)
                last.then_inc(a_full, 1)

            def kv(l, b):
                a0, _ = at["kv", l, b]
                pe.wait_ge(raw_in, (48, 96, 144, 224)[l * B + b])
                for g in range(CH):
                    if a0 + g >= 2:
                        pe.wait_ge(a_free, a0 + g - 1)
                    for c in range(CH):
                        last = nc.tensor.matmul(work(a0 + g)[:, 0:KEYS], raw_a[:, c, g * P:(g + 1) * P],
                                                ctx_t[:, c, :], start=(c == 0), stop=(c == CH - 1))
                    last.then_inc(a_full, 1)
                pe.wait_ge(a_free, a0 + CH - 1)
                for c in range(CH):
                    last = nc.tensor.matmul(work(a0 + CH), ctx_t[:, c, 0:P], raw_b[:, c, :],
                                            start=(c == 0), stop=(c == CH - 1))
                last.then_inc(a_full, 1)
                pe.wait_ge(a_free, a0 + CH)
                for h in range(HPG):
                    for c in range(CH):
                        last = nc.tensor.matmul(
                            work(a0 + CH + 1)[h * HD:h * HD + REM, 0:P], ctx_t[:, c, P:KEYS],
                            raw_b[:, c, :].rearrange("p (g h d) -> p g h d", g=CH, h=HPG)[:, :, h, :],
                            start=(c == 0), stop=(c == CH - 1))
                last.then_inc(a_full, 1)

            def prologue(l):
                a0, _ = at["prologue", l]
                for c in range(CH):
                    pe.wait_ge(a_free, a0 + c - 1)
                    transposes(work(c), c, LN[l])
                pe.wait_ge(a_free, a0 + CH)
                pe.wait_ge(split_lo, 3 * l + 1)
                for m in range(CH):
                    pe.wait_ge(a_free, a0 + CH + max(m - 1, 0))
                    queries(m, m)

            def units(l, b, step, a, h, kind, a_static):
                unit0 = (step + l * STEPS) * UNITS
                group0 = (step + l * STEPS) * CH
                ks, draining, carried, events_of = schedule(kind)
                if (kind, b) == ("full", 0):
                    pe.wait_ge(split_lo, 3 * l + 2)
                for k in ks:
                    if not draining:
                        g, s = k // SUB, k % SUB
                        q = slice(s * P, (s + 1) * P)
                        if k == 0:
                            pe.wait_ge(a_free, a - AFTER_Q0 if carried else a)
                        for half in range(2):
                            v = 2 * k + half
                            pe.wait_ge(s_free, unit0 * 2 + ((v - 3 if carried else max(v - 3, 0)) + CREDIT))
                            cs = slice(half * HALF, (half + 1) * HALF)
                            three_passes(score_bank(v), [((q_hi[:, g, q], q_lo[:, g, q]),
                                                          (k_hi[:, g, cs], k_lo[:, g, cs]))]).then_inc(s_full, 1)
                    for name, i, use, _ in events_of(k):
                        pe.wait_ge(a_free, a + (use if (name, i) in (("WO", 0), ("Q", 0)) else use - 1))
                        bank = a_static + use
                        if name == "WO":
                            out_rows(work(bank), i, ot_hi, ot_lo, wo_hi, wo_lo)
                        elif name == "XT":
                            transposes(work(bank), i, step + (LN[l] + 1))
                        elif name == "Q":
                            queries(bank, i)
                        else:
                            back = 1 if k < (i + 1) * SUB else 0
                            pe.wait_ge(ptm_out, unit0 + ((i + 1) * SUB - back * UNITS + CREDIT))
                            pe.wait_ge(ptr_out, group0 + (i + 1 - back * CH + CREDIT))
                            values(bank, i)
                    t = k - LAG_T
                    if (carried or t >= 0) and t < UNITS:
                        pe.wait_ge(pn_done, unit0 + (t + 1 + CREDIT))
                        pe.wait_ge(ptm_out, unit0 + (t + CREDIT))
                        s = t % SUB
                        if s == 0:
                            pe.wait_ge(ptr_out, group0 + (t // SUB + CREDIT))
                        nc.tensor.transpose(PTR[:, s * P:(s + 1) * P], pn_rem[:, t % PR_BUFS, :], ident[:, :])
                        for h in range(HPG):
                            i = nc.tensor.transpose(PTM[:, h * P:(h + 1) * P], pr[:, t % PR_BUFS, h, 0:P], ident[:, :])
                        i.then_inc(t_full, 1)

            layer_program(pe, 0, kv, prologue, units)
            pe.wait_ge(split_lo, 3)
            hi_bufs, lo_bufs = (xt_hi, ot_hi), (xt_lo, ot_lo)

            def dense_step(step, a, j, turned):
                for n, (kind, i) in enumerate(DENSE if turned else [e for e in DENSE if e[0] == "OUT"]):
                    pe.wait_ge(a_free, a + max(n - 3, 0))
                    if kind == "XT":
                        transposes(dense_bank(n), i, step + (LN_DENSE + 1))
                    else:
                        out_rows(dense_bank(n), i, hi_bufs[j], lo_bufs[j], wa_hi, wa_lo)

            a0, _ = at["dense"]
            with pe.Fori(0, (STEPS - 2) // 2) as it:
                for j in range(2):
                    dense_step(it * 2 + j, it * (2 * DENSE_USES) + (a0 + j * DENSE_USES), j, True)
            kv(1, 0)
            a0, _ = at["dense end"]
            dense_step(STEPS - 2, a0, 0, True)
            dense_step(STEPS - 1, a0 + DENSE_USES, 1, False)
            layer_program(pe, 1, kv, prologue, units)


def quantised_ffn(nc, w1, b1_cols, w2, b2_row, gates, out, X, ident, final):
    HB = 4
    PAIRS = FC // 2
    PAIR_BANKS = (0, 1, 2, 0, 1, 2, 0, 1)
    PAIR_CREDIT = 3
    FIRST_JOBS = [("x", i) for i in range(SUB)] + [("w1", i) for i in range(SUB)]
    rest = [("w1", i) for i in range(SUB, FC)] + [("x", i) for i in range(SUB)]
    STEP0 = [rest[2 * i:2 * i + 2] for i in range(PAIRS)]
    LOOP = [[[("x", 0)], [("x", 1)], [("x", 2)], [], [("x", 3)], [("w2", 2 * j)], [("w2", 2 * j + 1)], []]
            for j in range(2)]
    LAST = [[], [], [], [], [("w2", 0)], [("w2", 1)], [("w2", 2)], [("w2", 3)]]
    SCALES_AT = 3
    JOBS0 = len(FIRST_JOBS) + len(rest)
    LOOP_JOBS = sum(len(jobs) for steps in LOOP for jobs in steps)
    LOOPS = (STEPS - 2) // 2
    JOBS = JOBS0 + LOOPS * LOOP_JOBS + CH
    ctx = ExitStack()
    with ctx:
        def sb(name, shape, dt):
            return ctx.enter_context(nc.sbuf_tensor(name, shape, dt))

        def sem(name):
            return ctx.enter_context(nc.semaphore(name))

        xq_t = sb("xq_t", [P, CH, B * S], BF16)
        w1_t = sb("w1_t", [P, CH, F], BF16)
        w2_t = sb("w2_t", [P, FC, D], BF16)
        raw = sb("raw", [P, FC, D], FP32)
        h_relu = sb("h_relu", [P, HB, TOK], FP32)
        rounded = sb("rounded", [P, 2, D], BF16)
        diag = sb("diag", [P, P], FP32)
        ones = sb("ones", [P, P], FP32)
        ident_b = sb("ident_b", [P, P], BF16)
        magic = sb("magic", [P, 1], FP32)
        s_w1 = sb("s_w1", [P, FC], FP32)
        r_w1 = sb("r_w1", [P, FC], FP32)
        s_w2 = sb("s_w2", [P, 1], FP32)
        r_w2 = sb("r_w2", [P, 1], FP32)
        norm_max = sb("norm_max", [P, TILES], FP32)
        x_bias = sb("x_bias", [P, TILES], FP32)
        x_scale = sb("x_scale", [P, TILES], FP32)
        h_max = sb("h_max", [P, STEPS, FC], FP32)
        col = sb("col", [P, 12, FC], FP32)
        one = sb("one", [P, 16], FP32)
        b1_c = sb("b1_c", [P, FC], FP32)
        b2_r = sb("b2_r", [P, D], FP32)
        s2_r = sb("s2_r", [P, D], FP32)
        row_tmp = sb("row_tmp", [P, 3, D], FP32)
        gate_raw = sb("gate_raw2", [P, 4], FP32)
        gate = sb("gate2", [P, 4], FP32)
        ps = ctx.enter_context(nc.psum_tensor("ps2", [P, 8, 512], FP32))
        consts = sem("q_consts")
        w1_in = [sem(f"q_w1_in{c}") for c in range(CH)]
        w2_in = sem("q_w2_in")
        small_in = sem("q_small")
        vec = sem("q_vec")
        w_scaled = sem("q_ws")
        scaled = sem("q_js")
        rounded_done = sem("q_jr")
        turned = sem("q_jt")
        turned_out = sem("q_jo")
        gate_done = sem("q_gate")
        diag_done = sem("q_diag")
        srow_full = sem("q_srow")
        part_max = sem("q_pmax")
        global_max = sem("q_gmax")
        x_scaled = sem("q_xs")
        w2_vec = sem("q_w2v")
        s2_done = sem("q_s2")
        m_full = sem("q_mf")
        m_free = sem("q_mr")
        h_scaled = sem("q_hs")
        rows_done = sem("q_rows")
        h_full = sem("q_hf")
        h_relued = sem("q_hr")
        h_rounded = sem("q_hi")
        o_full = sem("q_of")
        o_scaled = sem("q_os")
        o_done = sem("q_od")
        pre_added = sem("q_pre")
        stored = sem("q_st")
        block = ctx.enter_context(nc.Block())
        row_max, meanvar, rstd = final["max"], final["meanvar"], final["rstd"]
        h_q = raw[:, 0:FC // 2, :].rearrange("p f d -> p (f d)").bitcast(BF16).rearrange("p (f n) -> p f n", f=FC)

        def turned_bank(j):
            return ps[:, 6 + j % 2, 0:TOK // 2].bitcast(BF16)

        def pair_banks(i):
            return 2 * PAIR_BANKS[i]

        def pairs_before(i):
            return max(k for k in range(-PAIRS, i) if PAIR_BANKS[k % PAIRS] == PAIR_BANKS[i]) + 1

        def nothing(*_):
            pass

        def first_pass(eng, job, before_jobs=nothing, after_jobs=nothing, finish=nothing, before_first=nothing,
                       after_step0=nothing):
            def step_of(step, c, j, j_static, pairs, starts, former=None):
                for i in range(PAIRS):
                    before_jobs(step, i, c if starts else None)
                    for kind, idx in pairs[i]:
                        this = (j, j_static, kind, step + 1, idx, c)
                        job(*this, former)
                        former, j, j_static = this, j + 1, j_static + 1
                    after_jobs(step, i, c if starts else None)
                finish(*former)

            former = None
            for j, (kind, idx) in enumerate(FIRST_JOBS):
                before_first(j)
                this = (j, j, kind, 0, idx, None)
                job(*this, former)
                former = this
            before_first(len(FIRST_JOBS))
            step_of(0, None, len(FIRST_JOBS), len(FIRST_JOBS), STEP0, False, former)
            after_step0()
            per_step = LOOP_JOBS // 2
            with eng.Fori(0, LOOPS) as it:
                for half in range(2):
                    j = JOBS0 + half * per_step
                    step_of(it * 2 + (half + 1), it, it * LOOP_JOBS + j, j, LOOP[half], half == 0)
            last = JOBS0 + LOOPS * LOOP_JOBS
            step_of(STEPS - 1, LOOPS, last, last, LAST, True)

        def tile_of(n):
            return flat(X[:, bass.ds(n, 1), :])

        @block.sync
        def _(sp):
            w1_v, w2_v = w1.rearrange("(f p) d -> p f d", p=P), w2.rearrange("(c p) (r d) -> c p r d", p=P, d=D)
            for c in range(CH):
                sp.dma_start(raw[:, 4 * c:4 * c + 4, :], w1_v[:, 4 * c:4 * c + 4, :]).then_inc(w1_in[c], 16)
            sp.dma_start(b1_c[:, :], b1_cols).then_inc(small_in, 16)
            sp.dma_start(b2_r[:, :], b2_row.partition_broadcast(P)).then_inc(small_in, 16)
            sp.dma_start(gate_raw[:, :], gates.partition_broadcast(P)).then_inc(small_in, 16)
            for c in range(CH):
                sp.wait_ge(scaled, SUB + 4 * c + 4)
                if c:
                    sp.wait_ge(w2_in, 16 * c)
                sp.dma_start(raw[:, 4 * c:4 * c + 4, :], w2_v[c]).then_inc(w2_in, 16)
            ov = out.rearrange("(t p) n -> p t n", p=P)
            with sp.Fori(0, STEPS) as it:
                sp.wait_ge(o_done, it * SUB + SUB)
                sp.dma_start(ov[:, bass.ds(it * SUB, SUB), :], X[:, bass.ds(it * SUB, SUB), :]).then_inc(stored, 16)
            sp.wait_ge(stored, 16 * STEPS)

        @block.gpsimd
        def _(pool):
            pool.memset(ones[:, :], 1.0).then_inc(consts, 1)
            pool.memset(magic[:, :], MAGIC).then_inc(consts, 1)
            pool.tensor_copy(ident_b[:, :], ident[:, :]).then_inc(consts, 1)
            pool.wait_ge(rows_done, 2)
            with pool.Fori(0, TILES) as n:
                pool.tensor_tensor(tile_of(n), tile_of(n), b2_r[:, :], ALU.add).then_inc(pre_added, 1)

        @block.scalar
        def _(act):
            act.sem_inc(h_relued, CREDIT)
            act.wait_ge(consts, 3)

            def copy_out(j, j_static, kind, step, i, c):
                act.wait_ge(turned, j + 1)
                src = turned_bank(j_static).rearrange("p (i q) -> p i q", i=4)
                if kind == "x":
                    dst = xq_t[:, :, bass.ds((step * SUB + i) * P, P)]
                elif kind == "w1":
                    dst = w1_t[:, :, i * P:(i + 1) * P]
                else:
                    dst = w2_t[:, 4 * i:4 * i + 4, bass.ds(c * P, P)]
                act.activation(dst, src, ACT.Copy).then_inc(turned_out, 1)

            def scale_job(j, j_static, kind, step, i, c):
                if j_static >= 2:
                    act.wait_ge(rounded_done, j - 1)
                dst = h_relu[:, j_static % 2, :]
                if kind == "x":
                    if j_static == 0:
                        act.wait_ge(x_scaled, 1)
                    n = step * SUB + i
                    a = act.activation(dst, tile_of(n), ACT.Relu, scale=x_scale[:, bass.ds(n, 1)],
                                       bias=x_bias[:, bass.ds(n, 1)])
                elif kind == "w1":
                    act.wait_ge(w_scaled, i // 4 + 1)
                    a = act.activation(dst, raw[:, i, :], ACT.Identity, scale=r_w1[:, i:i + 1], bias=magic[:, :])
                else:
                    act.wait_ge(w_scaled, CH + 1 + c)
                    a = act.activation(dst, flat(raw[:, bass.ds(c * 4 + i, 1), :]), ACT.Identity, scale=r_w2[:, :],
                                       bias=magic[:, :])
                a.then_inc(scaled, 1)

            def job(*this_and_former):
                scale_job(*this_and_former[:-1])
                if this_and_former[-1]:
                    copy_out(*this_and_former[-1])

            first_pass(act, job, finish=copy_out)
            act.wait_ge(small_in, 48)
            act.activation(gate[:, :], gate_raw[:, :], ACT.Tanh).then_inc(gate_done, 1)
            act.wait_ge(h_scaled, 1)
            with act.Fori(0, STEPS) as it:
                for f in range(FC):
                    act.wait_ge(h_full, it * FC + (f + 1))
                    act.wait_ge(h_rounded, it * FC + (max(f + 1 - HB, 0) + CREDIT))
                    act.activation(h_relu[:, f % HB, :], ps[:, f % HB, :], ACT.Relu, scale=col[:, 8, f:f + 1],
                                   bias=col[:, 9, f:f + 1]).then_inc(h_relued, 1)

        @block.vector
        def _(dve):
            steps = [0]

            def step(i):
                steps[0] += 1
                i.then_inc(vec, 1)
                dve.wait_ge(vec, steps[0])

            def magic_round(dst, v, tmp, keep):
                step(dve.tensor_scalar(tmp, v, MAGIC, -MAGIC, ALU.add, ALU.add))
                step(dve.tensor_tensor(keep, v, v, ALU.mult))
                step(dve.tensor_scalar(keep, keep, 2.0**44, None, ALU.is_lt))
                step(dve.tensor_tensor(tmp, tmp, v, ALU.subtract))
                step(dve.tensor_tensor(tmp, tmp, keep, ALU.mult))
                step(dve.tensor_tensor(dst, v, tmp, ALU.add))

            for buffers_free in (h_rounded, o_scaled, s2_done):
                dve.sem_inc(buffers_free, CREDIT)
            dve.sem_inc(m_free, PAIR_CREDIT)

            def scales_of_w1(c):
                dve.wait_ge(w1_in[c], 16)
                s, r = s_w1[:, 4 * c:4 * c + 4], r_w1[:, 4 * c:4 * c + 4]
                step(dve.tensor_reduce(s, raw[:, 4 * c:4 * c + 4, :], axis=AX.X, op=ALU.max, apply_absolute_value=True))
                step(dve.tensor_scalar(s, s, Q_EPS, 1.0 / 127.0, ALU.max, ALU.mult))
                dve.reciprocal(r, s).then_inc(w_scaled, 1)

            def scales_of_w2(c):
                dve.wait_ge(w2_in, c * 16 + 16)
                dve.tensor_reduce(s_w2[:, :], raw[:, bass.ds(c * 4, 4), :], axis=AX.XY, op=ALU.max,
                                  apply_absolute_value=True).then_inc(w2_vec, 1)
                dve.wait_ge(w2_vec, c * 2 + 1)
                dve.tensor_scalar(s_w2[:, :], s_w2[:, :], Q_EPS, 1.0 / 127.0, ALU.max, ALU.mult).then_inc(w2_vec, 1)
                dve.wait_ge(w2_vec, c * 2 + 2)
                dve.reciprocal(r_w2[:, :], s_w2[:, :]).then_inc(w_scaled, 1)
                dve.tensor_scalar(diag[:, :], ident[:, :], s_w2[:, :], None, ALU.mult).then_inc(diag_done, 1)

            def maximum_of_partitions(j):
                dve.tensor_scalar(diag[:, :], ident[:, :], one[:, 2 * j:2 * j + 1], None, ALU.mult).then_inc(part_max, 1)
                dve.wait_ge(global_max, j + 1)
                step(dve.tensor_reduce(one[:, 2 * j + 1:2 * j + 2], ps[:, 6, P:2 * P], axis=AX.X, op=ALU.max))

            step(dve.tensor_tensor(norm_max[:, :], row_max[:, :], meanvar[:, :, 0], ALU.subtract))
            step(dve.tensor_tensor(norm_max[:, :], norm_max[:, :], rstd[:, :], ALU.mult))
            step(dve.tensor_reduce(one[:, 0:1], norm_max[:, :], axis=AX.X, op=ALU.max))
            maximum_of_partitions(0)
            step(dve.tensor_scalar(one[:, 4:5], one[:, 1:2], Q_EPS, 1.0 / 255.0, ALU.max, ALU.mult))
            step(dve.reciprocal(one[:, 5:6], one[:, 4:5]))
            step(dve.tensor_scalar(x_scale[:, :], rstd[:, :], one[:, 5:6], None, ALU.mult))
            step(dve.tensor_scalar(x_bias[:, :], meanvar[:, :, 0], -1.0, None, ALU.mult))
            dve.tensor_tensor(x_bias[:, :], x_bias[:, :], x_scale[:, :], ALU.mult).then_inc(x_scaled, 1)

            def job(j, j_static, kind, step_of_x, i, c, former):
                dve.wait_ge(scaled, j + 1)
                if j_static >= 2:
                    dve.wait_ge(turned, j - 1)
                if kind == "x":
                    a = dve.tensor_scalar(rounded[:, j_static % 2, :], h_relu[:, j_static % 2, :], MAGIC, -MAGIC,
                                          ALU.add, ALU.add)
                else:
                    a = dve.tensor_scalar(rounded[:, j_static % 2, :], h_relu[:, j_static % 2, :], -MAGIC, None, ALU.add)
                a.then_inc(rounded_done, 1)

            scales_before_job = {SUB: 0, 2 * SUB: 1}
            scales_before_pair = {1: 2, 3: 3}

            def before_first(j):
                if j in scales_before_job:
                    scales_of_w1(scales_before_job[j])

            def before_jobs(step_now, i, c):
                if isinstance(step_now, int) and step_now == 0 and i in scales_before_pair:
                    scales_of_w1(scales_before_pair[i])

            def maxima_of_h(step_now, i, c):
                if c is not None and i == SCALES_AT:
                    scales_of_w2(c)
                if c is not None and i == SCALES_AT + 2:
                    dve.wait_ge(srow_full, c + 1)
                    dve.tensor_copy(s2_r[:, bass.ds(c * P, P)], ps[:, 6, 0:P]).then_inc(s2_done, 1)
                dve.wait_ge(m_full, step_now * PAIRS + (i + 1))
                b = pair_banks(i)
                dve.tensor_reduce(flat(h_max[:, bass.ds(step_now, 1), 2 * i:2 * i + 2]), ps[:, b:b + 2, :], axis=AX.X,
                                  op=ALU.max).then_inc(m_free, 1)

            sc1, bq1, v1, t1, k1 = (col[:, j, :] for j in range(5))

            def scale_and_bias_of_h():
                dve.wait_ge(small_in, 48)
                step(dve.tensor_scalar(sc1, s_w1[:, :], one[:, 4:5], None, ALU.mult))
                step(dve.reciprocal(v1, sc1))
                step(dve.tensor_tensor(v1, v1, b1_c[:, :], ALU.mult))
                magic_round(bq1, v1, t1, k1)
                step(dve.tensor_tensor(bq1, bq1, sc1, ALU.mult))

            first_pass(dve, job, before_jobs, maxima_of_h, before_first=before_first, after_step0=scale_and_bias_of_h)
            dve.wait_ge(s2_done, CH + CREDIT)
            dve.wait_ge(m_free, STEPS * PAIRS + PAIR_CREDIT)
            step(dve.tensor_reduce(col[:, 5, :], h_max[:, :, :].rearrange("p s f -> p f s"), axis=AX.X, op=ALU.max))
            step(dve.tensor_tensor(col[:, 5, :], col[:, 5, :], sc1, ALU.mult))
            step(dve.tensor_tensor(col[:, 5, :], col[:, 5, :], bq1, ALU.add))
            step(dve.tensor_scalar(col[:, 5, :], col[:, 5, :], 0.0, None, ALU.max))
            step(dve.tensor_reduce(one[:, 2:3], col[:, 5, :], axis=AX.X, op=ALU.max))
            maximum_of_partitions(1)
            step(dve.tensor_scalar(one[:, 6:7], one[:, 3:4], Q_EPS, 1.0 / 255.0, ALU.max, ALU.mult))
            step(dve.reciprocal(one[:, 7:8], one[:, 6:7]))
            step(dve.tensor_scalar(col[:, 8, :], sc1, one[:, 7:8], None, ALU.mult))
            dve.tensor_scalar(col[:, 9, :], bq1, one[:, 7:8], None, ALU.mult).then_inc(h_scaled, 1)
            dve.wait_ge(gate_done, 1)
            v2, t2, k2 = (row_tmp[:, j, :] for j in range(3))
            step(dve.tensor_scalar(s2_r[:, :], s2_r[:, :], one[:, 6:7], None, ALU.mult))
            step(dve.reciprocal(v2, s2_r[:, :]))
            step(dve.tensor_tensor(v2, v2, b2_r[:, :], ALU.mult))
            magic_round(v2, v2, t2, k2)
            step(dve.tensor_tensor(v2, v2, s2_r[:, :], ALU.mult))
            dve.tensor_scalar(b2_r[:, :], v2, gate[:, 3:4], None, ALU.mult).then_inc(rows_done, 1)
            dve.tensor_scalar(s2_r[:, :], s2_r[:, :], gate[:, 3:4], None, ALU.mult).then_inc(rows_done, 1)
            dve.wait_ge(rows_done, 2)
            with dve.Fori(0, STEPS) as it:
                for f in range(FC):
                    dve.wait_ge(h_relued, it * FC + (f + 1 + CREDIT))
                    if f == 0:
                        dve.wait_ge(o_full, it * SUB + CREDIT)
                    dve.tensor_scalar(h_q[:, f, :], h_relu[:, f % HB, :], MAGIC, -MAGIC, ALU.add, ALU.add).then_inc(h_rounded, 1)
                for s in range(SUB):
                    dve.wait_ge(o_full, it * SUB + (s + 1 + CREDIT))
                    dve.wait_ge(pre_added, it * SUB + (s + 1))
                    if s >= 2:
                        dve.wait_ge(o_done, it * SUB + (s - 1))
                    dve.tensor_tensor(row_tmp[:, s % 2, :], ps[:, 4 + s % 2, :], s2_r[:, :], ALU.mult).then_inc(o_scaled, 1)
                    dve.wait_ge(o_scaled, it * SUB + (s + 1 + CREDIT))
                    n = it * SUB + s
                    dve.tensor_tensor(tile_of(n), tile_of(n), row_tmp[:, s % 2, :], ALU.add).then_inc(o_done, 1)

        @block.tensor
        def _(pe):
            pe.sem_inc(o_full, CREDIT)
            pe.wait_ge(consts, 3)

            def spread_maxima(j):
                pe.wait_ge(part_max, j + 1)
                nc.tensor.matmul(ps[:, 6, P:2 * P], ones[:, :], diag[:, :], start=True, stop=True).then_inc(global_max, 1)

            spread_maxima(0)

            last_even = [None]

            def job(j, j_static, kind, step, i, c, former):
                if j_static % 2 == 0:
                    last_even[0] = j
                pe.wait_ge(rounded_done, j + 1)
                if j_static >= 2:
                    pe.wait_ge(turned_out, j - 1)
                for q in range(4):
                    last = nc.tensor.transpose(turned_bank(j_static)[:, q * P:(q + 1) * P],
                                               rounded[:, j_static % 2, q * P:(q + 1) * P], ident_b[:, :])
                last.then_inc(turned, 1)

            def h_chunk(bank, it, f):
                for c in range(CH):
                    last = nc.tensor.matmul(ps[:, bank, :], w1_t[:, c, f * P:(f + 1) * P],
                                            xq_t[:, c, bass.ds(it * TOK, TOK)], start=(c == 0), stop=(c == CH - 1))
                return last

            def products(step, i, c):
                if isinstance(step, int) and step == 0:
                    pe.wait_ge(turned_out, SUB + 2 * i + 2)
                elif i == 0:
                    pe.wait_ge(turned_out, (step - 1) * (LOOP_JOBS // 2) + JOBS0)
                pe.wait_ge(m_free, step * PAIRS + (pairs_before(i) + PAIR_CREDIT))
                b = pair_banks(i)
                h_chunk(b, step, 2 * i)
                h_chunk(b + 1, step, 2 * i + 1).then_inc(m_full, 1)
                if c is not None and i == SCALES_AT + 2:
                    pe.wait_ge(s2_done, c + (1 + CREDIT))

            def spread_scales(step, i, c):
                if c is not None and i == SCALES_AT + 1:
                    pe.wait_ge(turned_out, last_even[0] + 1)
                    pe.wait_ge(diag_done, c + 1)
                    nc.tensor.matmul(ps[:, 6, 0:P], ones[:, :], diag[:, :], start=True, stop=True).then_inc(srow_full, 1)

            first_pass(pe, job, products, spread_scales)
            pe.wait_ge(turned_out, JOBS)
            pe.wait_ge(m_free, STEPS * PAIRS + PAIR_CREDIT)
            spread_maxima(1)
            with pe.Fori(0, STEPS) as it:
                for f in range(FC):
                    pe.wait_ge(h_relued, it * FC + (max(f + 1 - HB, 0) + CREDIT))
                    h_chunk(f % HB, it, f).then_inc(h_full, 1)
                for s in range(SUB):
                    pe.wait_ge(o_scaled, it * SUB + (max(s - 1, 0) + CREDIT))
                    for f in range(FC):
                        if s == 0:
                            pe.wait_ge(h_rounded, it * FC + (f + 1 + CREDIT))
                        last = nc.tensor.matmul(ps[:, 4 + s % 2, :], h_q[:, f, s * P:(s + 1) * P], w2_t[:, f, :],
                                                start=(f == 0), stop=(f == FC - 1))
                    last.then_inc(o_full, 1)


def flamingo(nc, x, ctxT, mask, gates, cols, rows, weights, W0, logits, u, w1, b1_cols, w2, b2_row, out):
    ctx = ExitStack()
    with ctx:
        def sb(name, shape, dt):
            return ctx.enter_context(nc.sbuf_tensor(name, shape, dt))

        def sem(name):
            return ctx.enter_context(nc.semaphore(name))

        X = sb("X", [P, TILES, D], FP32)
        ident = sb("ident", [P, P], FP32)
        final = {"max": sb("row_max", [P, TILES], FP32), "meanvar": sb("final_meanvar", [P, TILES, 2], FP32),
                 "rstd": sb("final_rstd", [P, TILES], FP32)}
        attention_layers(nc, x, ctxT, mask, gates, cols, rows, weights, W0, logits, u, X, ident, final)
        quantised_ffn(nc, w1, b1_cols, w2, b2_row, gates, out, X, ident, final)


def kernel(**inputs):
    import concourse.bacc as bacc
    from concourse.bass_utils import run_bass_kernel_spmd

    nc = bacc.Bacc("TRN2", target_bir_lowering=False, num_devices=1)
    arrays = {}

    def give(name, a):
        a = np.ascontiguousarray(a)
        arrays[name] = a
        return nc.dram_tensor(name, a.shape, mybir.dt.from_np(a.dtype), kind="ExternalInput").ap()

    i = {k: np.asarray(v) for k, v in inputs.items()}

    def columns(name, a):
        return give(name, a.reshape(-1, P).T)

    x = give("x_in", i["x"].reshape(B * S, D))
    ctxT = give("ctx_T", i["ctx_1024"].reshape(B * KEYS, D).T)
    mask = give("mask_in", i["mask_BxS2_ik0"].reshape(B * KEYS))
    gates = give("gates", np.stack([i["g_xattn"], i["g_ffn"]], axis=1).reshape(4))
    cols, rows, weights = [], [], []
    for l in range(LAYERS):
        pre = f"L{l}_xattn_"
        cols.append([columns(f"b{n}{l}", i[pre + "b" + n]) for n in "qkv"])
        rows.append(give(f"bo{l}", i[pre + "bo"]))
        weights.append([give(f"W{n}T{l}", i[pre + "W" + n].T) for n in "qkvo"])
    rows.append(give("b0_in", i["L0_ffn_b"]))
    W0 = give("W0", i["L0_ffn_W"])
    logits = give("logits", i["L0_ffn_logits"].reshape(1, OPS))
    u = give("u", i["L0_ffn_u"].reshape(1, OPS))
    w1, w2 = give("w1", i["L1_ffn_w1"]), give("w2", i["L1_ffn_w2"])
    b1_cols, b2_row = columns("b1_in", i["L1_ffn_b1"]), give("b2_in", i["L1_ffn_b2"])
    out = nc.dram_tensor("out", (B * S, D), FP32, kind="ExternalOutput").ap()
    flamingo(nc, x, ctxT, mask, gates, cols, rows, weights, W0, logits, u, w1, b1_cols, w2, b2_row, out)
    r = run_bass_kernel_spmd(nc, [arrays], core_ids=[0])
    return r.results[0]["out"].reshape(B, S, D)
```
